# Optimizing a Trainium2 kernel written in Bass

```python
import numpy as np
import jax
import jax.numpy as jnp

def _softmax(x, axis=-1):
    return jax.nn.softmax(x, axis=axis)

def _gelu(x):
    return jax.nn.gelu(x, approximate=True)

def _silu(x):
    return jax.nn.silu(x)

def _sigmoid(x):
    return jax.nn.sigmoid(x)

def _layernorm(x, axis=-1, eps=1e-05):
    m = jnp.mean(x, axis=axis, keepdims=True)
    v = jnp.var(x, axis=axis, keepdims=True)
    return (x - m) / jnp.sqrt(v + eps)

def _scatter_add(tgt, idx, src, axis=0):
    return tgt.at[idx].add(src)

def _segment_sum(src, seg, n):
    return jax.ops.segment_sum(src, seg, n)
kernel_name = 'mk_pixart_seq_d4_seqx_r8_25616c'

def setup_inputs(seed: int=0):
    np.random.seed(seed)
    _w = jnp.asarray

    def _rec_inputs():
        import jax
        import jax.numpy as jnp
        _rk = jax.random.key(seed)
        x = 7.22e-05 + 1 * jax.random.normal(jax.random.fold_in(_rk, 1), (64, 128, 128), jnp.float32)
        _lenS = 128 - jax.random.randint(jax.random.fold_in(_rk, 7), (64,), 0, max(1, 128 // 4) + 1, jnp.int32)
        _lenS2 = 77 - jax.random.randint(jax.random.fold_in(_rk, 8), (64,), 0, max(1, 77 // 4) + 1, jnp.int32)
        cond_1024 = 0.000887014 + 1.03683 * jax.random.normal(jax.random.fold_in(_rk, 11), (64, 128), jnp.float32)
        _ctx_1024P = jax.random.normal(jax.random.fold_in(_rk, 12), (64, 16, 128), jnp.float32)
        _ctx_1024c = jax.random.dirichlet(jax.random.fold_in(_rk, 512), 0.3 * jnp.ones((16,), jnp.float32), (64, 77))
        _ctx_1024t = jnp.einsum('bsk,bkd->bsd', _ctx_1024c, _ctx_1024P)
        _ctx_1024t = _ctx_1024t * jax.lax.rsqrt(jnp.mean(jnp.square(_ctx_1024t)) + 1e-12) * 0.953939
        ctx_1024 = 0.00086875 + 0.999764 * (_ctx_1024t + 0.3 * jax.random.normal(jax.random.fold_in(_rk, 612), (64, 77, 128), jnp.float32))
        return (x, cond_1024, ctx_1024)
    x, cond_1024, ctx_1024 = _rec_inputs()

    def _L0_xcond_setup():
        import jax, jax.numpy as jnp
        import numpy as np
        C = 128
        H = 16
        D = C // H
        WIN = 64
        SHIFT = 32
        TOPK = 16
        HID = 512
        EPS = 1e-06

        def _ln(x):
            x32 = x.astype(jnp.float32)
            m = x32.mean(-1, keepdims=True)
            v = jnp.mean((x32 - m) ** 2, axis=-1, keepdims=True)
            return ((x32 - m) * jax.lax.rsqrt(v + EPS)).astype(x.dtype)

        def _self_attn(h, w_qkv, b_qkv, w_so, b_so):
            B, L, _ = h.shape
            qkv = h @ w_qkv + b_qkv
            qkv = jnp.roll(qkv, -SHIFT, axis=1)
            nw = L // WIN
            qkv = qkv.reshape(B, nw, WIN, 3, H, D)
            q, k, v = (qkv[:, :, :, 0], qkv[:, :, :, 1], qkv[:, :, :, 2])
            scores = jnp.einsum('bnqhd,bnkhd->bnhqk', q, k) / jnp.sqrt(jnp.float32(D)).astype(h.dtype)
            attn = jax.nn.softmax(scores, axis=-1)
            o = jnp.einsum('bnhqk,bnkhd->bnqhd', attn, v).reshape(B, L, C)
            o = jnp.roll(o, SHIFT, axis=1)
            return o @ w_so + b_so

        def _topk_cross_attn(h, ctx, w_q, b_q, w_kv, b_kv, w_co, b_co):
            B, L, _ = h.shape
            Lc = ctx.shape[1]
            q = (h @ w_q + b_q).reshape(B, L, H, D)
            kv = (ctx @ w_kv + b_kv).reshape(B, Lc, 2, H, D)
            k, v = (kv[:, :, 0], kv[:, :, 1])
            scores = jnp.einsum('bqhd,bkhd->bhqk', q, k) / jnp.sqrt(jnp.float32(D)).astype(h.dtype)
            top_s, top_i = jax.lax.top_k(scores, TOPK)
            attn = jax.nn.softmax(top_s, axis=-1)
            v_bh = jnp.transpose(v, (0, 2, 1, 3))
            vg = jnp.take_along_axis(v_bh[:, :, None, :, :], top_i[..., None], axis=3)
            o = jnp.einsum('bhqk,bhqkd->bqhd', attn, vg).reshape(B, L, C)
            return o @ w_co + b_co

        def _swiglu(h, w_m1, b_m1, w_m2, b_m2):
            u = h @ w_m1 + b_m1
            a, b = (u[..., :HID], u[..., HID:])
            return jax.nn.silu(a) * b @ w_m2 + b_m2
        key = jax.random.key(seed)
        ks = jax.random.split(key, 24)
        s = 0.02
        inp = {'x': jax.random.normal(ks[0], (2, 512, C), jnp.float32), 'mod': jax.random.normal(ks[1], (2, C), jnp.float32), 'context': jax.random.normal(ks[2], (2, 128, C), jnp.float32), 'w_ada': jax.random.normal(ks[3], (C, 9 * C), jnp.float32) * s, 'b_ada': jnp.zeros((9 * C,), jnp.float32), 'w_qkv': jax.random.normal(ks[4], (C, 3 * C), jnp.float32) * s, 'b_qkv': jnp.zeros((3 * C,), jnp.float32), 'w_so': jax.random.normal(ks[5], (C, C), jnp.float32) * s, 'b_so': jnp.zeros((C,), jnp.float32), 'w_q': jax.random.normal(ks[6], (C, C), jnp.float32) * s, 'b_q': jnp.zeros((C,), jnp.float32), 'w_kv': jax.random.normal(ks[7], (C, 2 * C), jnp.float32) * s, 'b_kv': jnp.zeros((2 * C,), jnp.float32), 'w_co': jax.random.normal(ks[8], (C, C), jnp.float32) * s, 'b_co': jnp.zeros((C,), jnp.float32), 'w_m1': jax.random.normal(ks[9], (C, 2 * HID), jnp.float32) * s, 'b_m1': jnp.zeros((2 * HID,), jnp.float32), 'w_m2': jax.random.normal(ks[10], (HID, C), jnp.float32) * s, 'b_m2': jnp.zeros((C,), jnp.float32)}
        return inp
    _L0_xcond_all = _L0_xcond_setup()
    _L0_xcond_in = {k: v for k, v in _L0_xcond_all.items() if k in ('w_ada', 'b_ada', 'w_qkv', 'b_qkv', 'w_so', 'b_so', 'w_q', 'b_q', 'w_kv', 'b_kv', 'w_co', 'b_co', 'w_m1', 'b_m1', 'w_m2', 'b_m2')}
    del _L0_xcond_all

    def _L1_xcond_setup():
        import jax, jax.numpy as jnp
        import numpy as np
        LN_EPS = 1e-06

        def _ln(x):
            mu = jnp.mean(x, axis=-1, keepdims=True)
            var = jnp.var(x, axis=-1, keepdims=True)
            return (x - mu) * jax.lax.rsqrt(var + LN_EPS)
        key = jax.random.key(seed)
        H, NH = (128, 16)
        B, N, S = (4, 128, 77)
        MLP = int(H * 4.0)
        ks = jax.random.split(key, 20)
        s = 1.0 / np.sqrt(H)
        return {'x': jax.random.normal(ks[0], (B, N, H), jnp.float32), 'c': jax.random.normal(ks[1], (B, H), jnp.float32), 'context': jax.random.normal(ks[2], (B, S, H), jnp.float32), 'W_mod': jax.random.normal(ks[3], (H, 6 * H), jnp.float32) * s, 'b_mod': jnp.zeros((6 * H,), jnp.float32), 'W_qkv': jax.random.normal(ks[4], (H, 3 * H), jnp.float32) * s, 'b_qkv': jnp.zeros((3 * H,), jnp.float32), 'W_proj': jax.random.normal(ks[5], (H, H), jnp.float32) * s, 'b_proj': jnp.zeros((H,), jnp.float32), 'W_qc': jax.random.normal(ks[6], (H, H), jnp.float32) * s, 'b_qc': jnp.zeros((H,), jnp.float32), 'W_kvc': jax.random.normal(ks[7], (H, 2 * H), jnp.float32) * s, 'b_kvc': jnp.zeros((2 * H,), jnp.float32), 'W_cproj': jax.random.normal(ks[8], (H, H), jnp.float32) * s, 'b_cproj': jnp.zeros((H,), jnp.float32), 'W_mlp1': jax.random.normal(ks[9], (H, MLP), jnp.float32) * s, 'b_mlp1': jnp.zeros((MLP,), jnp.float32), 'W_mlp2': jax.random.normal(ks[10], (MLP, H), jnp.float32) * (1.0 / np.sqrt(MLP)), 'b_mlp2': jnp.zeros((H,), jnp.float32)}
    _L1_xcond_all = _L1_xcond_setup()
    _L1_xcond_in = {k: v for k, v in _L1_xcond_all.items() if k in ('W_mod', 'b_mod', 'W_qkv', 'b_qkv', 'W_proj', 'b_proj', 'W_qc', 'b_qc', 'W_kvc', 'b_kvc', 'W_cproj', 'b_cproj', 'W_mlp1', 'b_mlp1', 'W_mlp2', 'b_mlp2')}
    del _L1_xcond_all

    def _L2_xcond_setup():
        import jax, jax.numpy as jnp
        import numpy as np
        D = 128
        H = 16
        HD = D // H
        MLP = 4 * D
        EPS = 1e-06
        SCALE = HD ** (-0.5)

        def _p(key, shape, s=0.02):
            return jax.random.normal(key, shape, dtype=jnp.float32) * s

        def _ln(x):
            mu = jnp.mean(x, axis=-1, keepdims=True)
            var = jnp.var(x, axis=-1, keepdims=True)
            return (x - mu) * jax.lax.rsqrt(var + EPS)

        def _heads(t):
            B, L, _ = t.shape
            return t.reshape(B, L, H, HD).transpose(0, 2, 1, 3)

        def _attend(q, k, v):
            attn = jnp.einsum('bhnd,bhsd->bhns', q, k) * SCALE
            attn = jax.nn.softmax(attn, axis=-1)
            o = jnp.einsum('bhns,bhsd->bhnd', attn, v)
            B, _, N, _ = q.shape
            return o.transpose(0, 2, 1, 3).reshape(B, N, D)
        key = jax.random.key(seed)
        ks = jax.random.split(key, 24)
        B, N, S = (4, 128, 77)
        return {'x': jax.random.normal(ks[0], (B, N, D), dtype=jnp.float32), 't_emb': jax.random.normal(ks[1], (B, D), dtype=jnp.float32), 'context': jax.random.normal(ks[2], (B, S, D), dtype=jnp.float32), 'adaln_w': _p(ks[3], (D, 6 * D)), 'adaln_b': _p(ks[4], (6 * D,)), 'qkv_w': _p(ks[5], (D, 3 * D)), 'qkv_b': _p(ks[6], (3 * D,)), 'sa_proj_w': _p(ks[7], (D, D)), 'sa_proj_b': _p(ks[8], (D,)), 'q_w': _p(ks[9], (D, D)), 'q_b': _p(ks[10], (D,)), 'kv_w': _p(ks[11], (D, 2 * D)), 'kv_b': _p(ks[12], (2 * D,)), 'ca_proj_w': _p(ks[13], (D, D)), 'ca_proj_b': _p(ks[14], (D,)), 'fc1_w': _p(ks[15], (D, MLP)), 'fc1_b': _p(ks[16], (MLP,)), 'fc2_w': _p(ks[17], (MLP, D)), 'fc2_b': _p(ks[18], (D,))}
    _L2_xcond_all = _L2_xcond_setup()
    _L2_xcond_in = {k: v for k, v in _L2_xcond_all.items() if k in ('adaln_w', 'adaln_b', 'qkv_w', 'qkv_b', 'sa_proj_w', 'sa_proj_b', 'q_w', 'q_b', 'kv_w', 'kv_b', 'ca_proj_w', 'ca_proj_b', 'fc1_w', 'fc1_b', 'fc2_w', 'fc2_b')}
    del _L2_xcond_all

    def _L3_xcond_setup():
        import jax, jax.numpy as jnp
        import numpy as np
        H = 128
        RH = 2 * H
        E = 3
        B, T, P = (8, 256, 64)
        LN_EPS = 1e-05

        def _layer_norm(x, gamma, beta):
            mu = jnp.mean(x, axis=-1, keepdims=True)
            var = jnp.mean(jnp.square(x - mu), axis=-1, keepdims=True)
            return (x - mu) * jax.lax.rsqrt(var + LN_EPS) * gamma + beta
        key = jax.random.key(seed)
        ks = jax.random.split(key, 24)
        s = lambda fan_in: 1.0 / np.sqrt(fan_in)
        inp = {'mix_hidden_states': jax.random.normal(ks[0], (B, T, H), jnp.float32), 'global_anchor': jax.random.normal(ks[1], (B, H), jnp.float32), 'prototype_bank': jax.random.normal(ks[2], (B, P, H), jnp.float32), 'ln_gamma': jnp.ones((H,), jnp.float32), 'ln_beta': jnp.zeros((H,), jnp.float32), 'Wq': jax.random.normal(ks[3], (H, H), jnp.float32) * s(H), 'Wk': jax.random.normal(ks[4], (H, H), jnp.float32) * s(H), 'Wv': jax.random.normal(ks[5], (H, H), jnp.float32) * s(H), 'router_W': jax.random.normal(ks[6], (3 * H, E), jnp.float32) * s(3 * H), 'router_b': jnp.zeros((E,), jnp.float32), 'e_w1': jax.random.normal(ks[7], (E, 3 * H, RH), jnp.float32) * s(3 * H), 'e_b1': jnp.zeros((E, RH), jnp.float32), 'e_w2': jax.random.normal(ks[8], (E, RH, H), jnp.float32) * s(RH), 'e_b2': jnp.zeros((E, H), jnp.float32), 'gate_w1': jax.random.normal(ks[9], (3 * H, H), jnp.float32) * s(3 * H), 'gate_b1': jnp.zeros((H,), jnp.float32), 'gate_w2': jax.random.normal(ks[10], (H, H), jnp.float32) * s(H), 'gate_b2': jnp.zeros((H,), jnp.float32), 'out_w': jax.random.normal(ks[11], (H, H), jnp.float32) * s(H), 'out_b': jnp.zeros((H,), jnp.float32)}
        return inp
    _L3_xcond_all = _L3_xcond_setup()
    _L3_xcond_in = {k: v for k, v in _L3_xcond_all.items() if k in ('ln_gamma', 'ln_beta', 'Wq', 'Wk', 'Wv', 'router_W', 'router_b', 'e_w1', 'e_b1', 'e_w2', 'e_b2', 'gate_w1', 'gate_b1', 'gate_w2', 'gate_b2', 'out_w', 'out_b')}
    del _L3_xcond_all
    return {'x': x, 'cond_1024': cond_1024, 'ctx_1024': ctx_1024, 'L0_xcond_w_ada': _L0_xcond_in['w_ada'], 'L0_xcond_b_ada': _L0_xcond_in['b_ada'], 'L0_xcond_w_qkv': _L0_xcond_in['w_qkv'], 'L0_xcond_b_qkv': _L0_xcond_in['b_qkv'], 'L0_xcond_w_so': _L0_xcond_in['w_so'], 'L0_xcond_b_so': _L0_xcond_in['b_so'], 'L0_xcond_w_q': _L0_xcond_in['w_q'], 'L0_xcond_b_q': _L0_xcond_in['b_q'], 'L0_xcond_w_kv': _L0_xcond_in['w_kv'], 'L0_xcond_b_kv': _L0_xcond_in['b_kv'], 'L0_xcond_w_co': _L0_xcond_in['w_co'], 'L0_xcond_b_co': _L0_xcond_in['b_co'], 'L0_xcond_w_m1': _L0_xcond_in['w_m1'], 'L0_xcond_b_m1': _L0_xcond_in['b_m1'], 'L0_xcond_w_m2': _L0_xcond_in['w_m2'], 'L0_xcond_b_m2': _L0_xcond_in['b_m2'], 'L1_xcond_W_mod': _L1_xcond_in['W_mod'], 'L1_xcond_b_mod': _L1_xcond_in['b_mod'], 'L1_xcond_W_qkv': _L1_xcond_in['W_qkv'], 'L1_xcond_b_qkv': _L1_xcond_in['b_qkv'], 'L1_xcond_W_proj': _L1_xcond_in['W_proj'], 'L1_xcond_b_proj': _L1_xcond_in['b_proj'], 'L1_xcond_W_qc': _L1_xcond_in['W_qc'], 'L1_xcond_b_qc': _L1_xcond_in['b_qc'], 'L1_xcond_W_kvc': _L1_xcond_in['W_kvc'], 'L1_xcond_b_kvc': _L1_xcond_in['b_kvc'], 'L1_xcond_W_cproj': _L1_xcond_in['W_cproj'], 'L1_xcond_b_cproj': _L1_xcond_in['b_cproj'], 'L1_xcond_W_mlp1': _L1_xcond_in['W_mlp1'], 'L1_xcond_b_mlp1': _L1_xcond_in['b_mlp1'], 'L1_xcond_W_mlp2': _L1_xcond_in['W_mlp2'], 'L1_xcond_b_mlp2': _L1_xcond_in['b_mlp2'], 'L2_xcond_adaln_w': _L2_xcond_in['adaln_w'], 'L2_xcond_adaln_b': _L2_xcond_in['adaln_b'], 'L2_xcond_qkv_w': _L2_xcond_in['qkv_w'], 'L2_xcond_qkv_b': _L2_xcond_in['qkv_b'], 'L2_xcond_sa_proj_w': _L2_xcond_in['sa_proj_w'], 'L2_xcond_sa_proj_b': _L2_xcond_in['sa_proj_b'], 'L2_xcond_q_w': _L2_xcond_in['q_w'], 'L2_xcond_q_b': _L2_xcond_in['q_b'], 'L2_xcond_kv_w': _L2_xcond_in['kv_w'], 'L2_xcond_kv_b': _L2_xcond_in['kv_b'], 'L2_xcond_ca_proj_w': _L2_xcond_in['ca_proj_w'], 'L2_xcond_ca_proj_b': _L2_xcond_in['ca_proj_b'], 'L2_xcond_fc1_w': _L2_xcond_in['fc1_w'], 'L2_xcond_fc1_b': _L2_xcond_in['fc1_b'], 'L2_xcond_fc2_w': _L2_xcond_in['fc2_w'], 'L2_xcond_fc2_b': _L2_xcond_in['fc2_b'], 'L3_xcond_ln_gamma': _L3_xcond_in['ln_gamma'], 'L3_xcond_ln_beta': _L3_xcond_in['ln_beta'], 'L3_xcond_Wq': _L3_xcond_in['Wq'], 'L3_xcond_Wk': _L3_xcond_in['Wk'], 'L3_xcond_Wv': _L3_xcond_in['Wv'], 'L3_xcond_router_W': _L3_xcond_in['router_W'], 'L3_xcond_router_b': _L3_xcond_in['router_b'], 'L3_xcond_e_w1': _L3_xcond_in['e_w1'], 'L3_xcond_e_b1': _L3_xcond_in['e_b1'], 'L3_xcond_e_w2': _L3_xcond_in['e_w2'], 'L3_xcond_e_b2': _L3_xcond_in['e_b2'], 'L3_xcond_gate_w1': _L3_xcond_in['gate_w1'], 'L3_xcond_gate_b1': _L3_xcond_in['gate_b1'], 'L3_xcond_gate_w2': _L3_xcond_in['gate_w2'], 'L3_xcond_gate_b2': _L3_xcond_in['gate_b2'], 'L3_xcond_out_w': _L3_xcond_in['out_w'], 'L3_xcond_out_b': _L3_xcond_in['out_b']}

def reference(x, cond_1024, ctx_1024, L0_xcond_w_ada, L0_xcond_b_ada, L0_xcond_w_qkv, L0_xcond_b_qkv, L0_xcond_w_so, L0_xcond_b_so, L0_xcond_w_q, L0_xcond_b_q, L0_xcond_w_kv, L0_xcond_b_kv, L0_xcond_w_co, L0_xcond_b_co, L0_xcond_w_m1, L0_xcond_b_m1, L0_xcond_w_m2, L0_xcond_b_m2, L1_xcond_W_mod, L1_xcond_b_mod, L1_xcond_W_qkv, L1_xcond_b_qkv, L1_xcond_W_proj, L1_xcond_b_proj, L1_xcond_W_qc, L1_xcond_b_qc, L1_xcond_W_kvc, L1_xcond_b_kvc, L1_xcond_W_cproj, L1_xcond_b_cproj, L1_xcond_W_mlp1, L1_xcond_b_mlp1, L1_xcond_W_mlp2, L1_xcond_b_mlp2, L2_xcond_adaln_w, L2_xcond_adaln_b, L2_xcond_qkv_w, L2_xcond_qkv_b, L2_xcond_sa_proj_w, L2_xcond_sa_proj_b, L2_xcond_q_w, L2_xcond_q_b, L2_xcond_kv_w, L2_xcond_kv_b, L2_xcond_ca_proj_w, L2_xcond_ca_proj_b, L2_xcond_fc1_w, L2_xcond_fc1_b, L2_xcond_fc2_w, L2_xcond_fc2_b, L3_xcond_ln_gamma, L3_xcond_ln_beta, L3_xcond_Wq, L3_xcond_Wk, L3_xcond_Wv, L3_xcond_router_W, L3_xcond_router_b, L3_xcond_e_w1, L3_xcond_e_b1, L3_xcond_e_w2, L3_xcond_e_b2, L3_xcond_gate_w1, L3_xcond_gate_b1, L3_xcond_gate_w2, L3_xcond_gate_b2, L3_xcond_out_w, L3_xcond_out_b):
    import jax
    import jax.numpy as jnp

    def _L0_xcond_ref(x, mod, context, w_ada, b_ada, w_qkv, b_qkv, w_so, b_so, w_q, b_q, w_kv, b_kv, w_co, b_co, w_m1, b_m1, w_m2, b_m2):
        import jax, jax.numpy as jnp
        import numpy as np
        C = 128
        H = 16
        D = C // H
        WIN = 64
        SHIFT = 32
        TOPK = 16
        HID = 512
        EPS = 1e-06

        def _ln(x):
            x32 = x.astype(jnp.float32)
            m = x32.mean(-1, keepdims=True)
            v = jnp.mean((x32 - m) ** 2, axis=-1, keepdims=True)
            return ((x32 - m) * jax.lax.rsqrt(v + EPS)).astype(x.dtype)

        def _self_attn(h, w_qkv, b_qkv, w_so, b_so):
            B, L, _ = h.shape
            qkv = h @ w_qkv + b_qkv
            qkv = jnp.roll(qkv, -SHIFT, axis=1)
            nw = L // WIN
            qkv = qkv.reshape(B, nw, WIN, 3, H, D)
            q, k, v = (qkv[:, :, :, 0], qkv[:, :, :, 1], qkv[:, :, :, 2])
            scores = jnp.einsum('bnqhd,bnkhd->bnhqk', q, k) / jnp.sqrt(jnp.float32(D)).astype(h.dtype)
            attn = jax.nn.softmax(scores, axis=-1)
            o = jnp.einsum('bnhqk,bnkhd->bnqhd', attn, v).reshape(B, L, C)
            o = jnp.roll(o, SHIFT, axis=1)
            return o @ w_so + b_so

        def _topk_cross_attn(h, ctx, w_q, b_q, w_kv, b_kv, w_co, b_co):
            B, L, _ = h.shape
            Lc = ctx.shape[1]
            q = (h @ w_q + b_q).reshape(B, L, H, D)
            kv = (ctx @ w_kv + b_kv).reshape(B, Lc, 2, H, D)
            k, v = (kv[:, :, 0], kv[:, :, 1])
            scores = jnp.einsum('bqhd,bkhd->bhqk', q, k) / jnp.sqrt(jnp.float32(D)).astype(h.dtype)
            top_s, top_i = jax.lax.top_k(scores, TOPK)
            attn = jax.nn.softmax(top_s, axis=-1)
            v_bh = jnp.transpose(v, (0, 2, 1, 3))
            vg = jnp.take_along_axis(v_bh[:, :, None, :, :], top_i[..., None], axis=3)
            o = jnp.einsum('bhqk,bhqkd->bqhd', attn, vg).reshape(B, L, C)
            return o @ w_co + b_co

        def _swiglu(h, w_m1, b_m1, w_m2, b_m2):
            u = h @ w_m1 + b_m1
            a, b = (u[..., :HID], u[..., HID:])
            return jax.nn.silu(a) * b @ w_m2 + b_m2
        m = jax.nn.silu(mod) @ w_ada + b_ada
        sh_msa, sc_msa, g_msa, sh_mca, sc_mca, g_mca, sh_mlp, sc_mlp, g_mlp = [m[:, i * C:(i + 1) * C][:, None, :] for i in range(9)]
        h = _ln(x) * (1 + sc_msa) + sh_msa
        h = _self_attn(h, w_qkv, b_qkv, w_so, b_so)
        x = x + h * g_msa
        h = _ln(x) * (1 + sc_mca) + sh_mca
        h = _topk_cross_attn(h, context, w_q, b_q, w_kv, b_kv, w_co, b_co)
        x = x + h * g_mca
        h = _ln(x) * (1 + sc_mlp) + sh_mlp
        h = _swiglu(h, w_m1, b_m1, w_m2, b_m2)
        x = x + h * g_mlp
        return x

    def _L1_xcond_ref(x, c, context, W_mod, b_mod, W_qkv, b_qkv, W_proj, b_proj, W_qc, b_qc, W_kvc, b_kvc, W_cproj, b_cproj, W_mlp1, b_mlp1, W_mlp2, b_mlp2):
        import jax, jax.numpy as jnp
        import numpy as np
        LN_EPS = 1e-06

        def _ln(x):
            mu = jnp.mean(x, axis=-1, keepdims=True)
            var = jnp.var(x, axis=-1, keepdims=True)
            return (x - mu) * jax.lax.rsqrt(var + LN_EPS)
        B, N, H = x.shape
        NH = 16
        hd = H // NH
        scale = hd ** (-0.5)
        c_proj = jax.nn.silu(c) @ W_mod + b_mod
        shift_a, scale_a, gate_a, shift_m, scale_m, gate_m = jnp.split(c_proj, 6, axis=-1)

        def modulate(t, shift, sc):
            return t * (1 + sc[:, None]) + shift[:, None]
        x_norm = modulate(_ln(x), shift_a, scale_a)
        qkv = x_norm @ W_qkv + b_qkv
        q, k, v = jnp.split(qkv, 3, axis=-1)
        q = q.reshape(B, N, NH, hd).transpose(0, 2, 1, 3)
        k = k.reshape(B, N, NH, hd).transpose(0, 2, 1, 3)
        v = v.reshape(B, N, NH, hd).transpose(0, 2, 1, 3)
        attn_w = jax.nn.softmax(jnp.einsum('bhqd,bhkd->bhqk', q, k) * scale, axis=-1)
        attn_out = jnp.einsum('bhqk,bhkd->bhqd', attn_w, v)
        attn_out = attn_out.transpose(0, 2, 1, 3).reshape(B, N, H)
        attn_out = attn_out @ W_proj + b_proj
        x = x + gate_a[:, None] * attn_out
        S = context.shape[1]
        q_c = _ln(x) @ W_qc + b_qc
        kv_c = _ln(context) @ W_kvc + b_kvc
        k_c, v_c = jnp.split(kv_c, 2, axis=-1)
        q_c = q_c.reshape(B, N, NH, hd).transpose(0, 2, 1, 3)
        k_c = k_c.reshape(B, S, NH, hd).transpose(0, 2, 1, 3)
        v_c = v_c.reshape(B, S, NH, hd).transpose(0, 2, 1, 3)
        c_attn_w = jax.nn.softmax(jnp.einsum('bhqd,bhsd->bhqs', q_c, k_c) * scale, axis=-1)
        c_attn_out = jnp.einsum('bhqs,bhsd->bhqd', c_attn_w, v_c)
        c_attn_out = c_attn_out.transpose(0, 2, 1, 3).reshape(B, N, H)
        c_attn_out = c_attn_out @ W_cproj + b_cproj
        x = x + c_attn_out
        x_norm2 = modulate(_ln(x), shift_m, scale_m)
        h = jax.nn.gelu(x_norm2 @ W_mlp1 + b_mlp1)
        h = h @ W_mlp2 + b_mlp2
        x = x + gate_m[:, None] * h
        return x

    def _L2_xcond_ref(x, t_emb, context, adaln_w, adaln_b, qkv_w, qkv_b, sa_proj_w, sa_proj_b, q_w, q_b, kv_w, kv_b, ca_proj_w, ca_proj_b, fc1_w, fc1_b, fc2_w, fc2_b):
        import jax, jax.numpy as jnp
        import numpy as np
        D = 128
        H = 16
        HD = D // H
        MLP = 4 * D
        EPS = 1e-06
        SCALE = HD ** (-0.5)

        def _p(key, shape, s=0.02):
            return jax.random.normal(key, shape, dtype=jnp.float32) * s

        def _ln(x):
            mu = jnp.mean(x, axis=-1, keepdims=True)
            var = jnp.var(x, axis=-1, keepdims=True)
            return (x - mu) * jax.lax.rsqrt(var + EPS)

        def _heads(t):
            B, L, _ = t.shape
            return t.reshape(B, L, H, HD).transpose(0, 2, 1, 3)

        def _attend(q, k, v):
            attn = jnp.einsum('bhnd,bhsd->bhns', q, k) * SCALE
            attn = jax.nn.softmax(attn, axis=-1)
            o = jnp.einsum('bhns,bhsd->bhnd', attn, v)
            B, _, N, _ = q.shape
            return o.transpose(0, 2, 1, 3).reshape(B, N, D)
        B, N, _ = x.shape
        S = context.shape[1]
        mod = jax.nn.silu(t_emb) @ adaln_w + adaln_b
        sh_sa, sc_sa, g_sa, sh_ff, sc_ff, g_ff = jnp.split(mod[:, None, :], 6, axis=-1)
        xm = _ln(x) * (1.0 + sc_sa) + sh_sa
        qkv = (xm @ qkv_w + qkv_b).reshape(B, N, 3, H, HD)
        q = qkv[:, :, 0].transpose(0, 2, 1, 3)
        k = qkv[:, :, 1].transpose(0, 2, 1, 3)
        v = qkv[:, :, 2].transpose(0, 2, 1, 3)
        x_sa = _attend(q, k, v) @ sa_proj_w + sa_proj_b
        x = x + g_sa * x_sa
        xn = _ln(x)
        q = _heads(xn @ q_w + q_b)
        kv = (context @ kv_w + kv_b).reshape(B, S, 2, H, HD)
        k = kv[:, :, 0].transpose(0, 2, 1, 3)
        v = kv[:, :, 1].transpose(0, 2, 1, 3)
        x_ca = _attend(q, k, v) @ ca_proj_w + ca_proj_b
        x = x + x_ca
        xm = _ln(x) * (1.0 + sc_ff) + sh_ff
        h = jax.nn.gelu(xm @ fc1_w + fc1_b, approximate=True)
        x_ff = h @ fc2_w + fc2_b
        x = x + g_ff * x_ff
        return x

    def _L3_xcond_ref(mix_hidden_states, global_anchor, prototype_bank, ln_gamma, ln_beta, Wq, Wk, Wv, router_W, router_b, e_w1, e_b1, e_w2, e_b2, gate_w1, gate_b1, gate_w2, gate_b2, out_w, out_b):
        import jax, jax.numpy as jnp
        import numpy as np
        H = 128
        RH = 2 * H
        E = 3
        B, T, P = (8, 256, 64)
        LN_EPS = 1e-05

        def _layer_norm(x, gamma, beta):
            mu = jnp.mean(x, axis=-1, keepdims=True)
            var = jnp.mean(jnp.square(x - mu), axis=-1, keepdims=True)
            return (x - mu) * jax.lax.rsqrt(var + LN_EPS) * gamma + beta
        x = mix_hidden_states
        nx = _layer_norm(x, ln_gamma, ln_beta)
        q = nx @ Wq
        k = prototype_bank @ Wk
        v = prototype_bank @ Wv
        scores = jnp.einsum('bth,bph->btp', q, k) * H ** (-0.5)
        weights = jax.nn.softmax(scores, axis=-1)
        evidence = jnp.einsum('btp,bph->bth', weights, v)
        anchor = jnp.broadcast_to(global_anchor[:, None, :], nx.shape)
        combined = jnp.concatenate([nx, evidence, anchor], axis=-1)
        router_logits = combined @ router_W + router_b
        router_probs = jax.nn.softmax(router_logits, axis=-1)
        h = jax.nn.silu(jnp.einsum('btc,ecr->bter', combined, e_w1) + e_b1)
        expert_out = jnp.einsum('bter,erh->bteh', h, e_w2) + e_b2
        routed = jnp.sum(expert_out * router_probs[..., None], axis=-2)
        g = jax.nn.sigmoid(jax.nn.silu(combined @ gate_w1 + gate_b1) @ gate_w2 + gate_b2)
        refined_delta = g * (routed @ out_w + out_b)
        return x + refined_delta
    x = _L0_xcond_ref(x, cond_1024, ctx_1024, L0_xcond_w_ada, L0_xcond_b_ada, L0_xcond_w_qkv, L0_xcond_b_qkv, L0_xcond_w_so, L0_xcond_b_so, L0_xcond_w_q, L0_xcond_b_q, L0_xcond_w_kv, L0_xcond_b_kv, L0_xcond_w_co, L0_xcond_b_co, L0_xcond_w_m1, L0_xcond_b_m1, L0_xcond_w_m2, L0_xcond_b_m2)
    x = _L1_xcond_ref(x, cond_1024, ctx_1024, L1_xcond_W_mod, L1_xcond_b_mod, L1_xcond_W_qkv, L1_xcond_b_qkv, L1_xcond_W_proj, L1_xcond_b_proj, L1_xcond_W_qc, L1_xcond_b_qc, L1_xcond_W_kvc, L1_xcond_b_kvc, L1_xcond_W_cproj, L1_xcond_b_cproj, L1_xcond_W_mlp1, L1_xcond_b_mlp1, L1_xcond_W_mlp2, L1_xcond_b_mlp2)
    x = _L2_xcond_ref(x, cond_1024, ctx_1024, L2_xcond_adaln_w, L2_xcond_adaln_b, L2_xcond_qkv_w, L2_xcond_qkv_b, L2_xcond_sa_proj_w, L2_xcond_sa_proj_b, L2_xcond_q_w, L2_xcond_q_b, L2_xcond_kv_w, L2_xcond_kv_b, L2_xcond_ca_proj_w, L2_xcond_ca_proj_b, L2_xcond_fc1_w, L2_xcond_fc1_b, L2_xcond_fc2_w, L2_xcond_fc2_b)
    x = _L3_xcond_ref(x, cond_1024, ctx_1024, L3_xcond_ln_gamma, L3_xcond_ln_beta, L3_xcond_Wq, L3_xcond_Wk, L3_xcond_Wv, L3_xcond_router_W, L3_xcond_router_b, L3_xcond_e_w1, L3_xcond_e_b1, L3_xcond_e_w2, L3_xcond_e_b2, L3_xcond_gate_w1, L3_xcond_gate_b1, L3_xcond_gate_w2, L3_xcond_gate_b2, L3_xcond_out_w, L3_xcond_out_b)
    return x

_drawn_inputs = setup_inputs


def setup_inputs(seed=0):
    import zlib

    import numpy as np

    out = dict(_drawn_inputs(seed))
    spreads = {'L0_xcond_b_ada': (0.0, 0.428),
     'L0_xcond_b_qkv': (0.0, 0.8),
     'L0_xcond_b_so': (0.0, 0.459),
     'L0_xcond_b_q': (0.0, 0.8),
     'L0_xcond_b_kv': (0.0, 0.8),
     'L0_xcond_b_co': (0.0, 0.488),
     'L0_xcond_b_m1': (0.0, 0.8),
     'L0_xcond_b_m2': (0.0, 0.418),
     'L1_xcond_b_mod': (0.0, 0.28),
     'L1_xcond_b_qkv': (0.0, 0.697),
     'L1_xcond_b_proj': (0.0, 0.769),
     'L1_xcond_b_qc': (0.0, 2.0),
     'L1_xcond_b_kvc': (0.0, 0.48),
     'L1_xcond_b_cproj': (0.0, 0.532),
     'L1_xcond_b_mlp1': (0.0, 0.8),
     'L1_xcond_b_mlp2': (0.0, 0.8),
     'L3_xcond_ln_gamma': (1.0, 0.6),
     'L3_xcond_ln_beta': (0.0, 2.0),
     'L3_xcond_router_b': (0.0, 2.0),
     'L3_xcond_e_b1': (0.0, 2.0),
     'L3_xcond_e_b2': (0.0, 2.0),
     'L3_xcond_gate_b1': (0.0, 2.0),
     'L3_xcond_gate_b2': (0.0, 2.0),
     'L3_xcond_out_b': (0.0, 0.8)}
    factors = {'L0_xcond_w_qkv': 8.0,
     'L0_xcond_w_so': 8.0,
     'L0_xcond_w_q': 8.0,
     'L0_xcond_w_kv': 8.0,
     'L0_xcond_w_co': 8.0,
     'L0_xcond_w_m1': 8.0,
     'L0_xcond_w_m2': 8.0,
     'L2_xcond_adaln_w': 8.0,
     'L2_xcond_adaln_b': 8.0,
     'L2_xcond_qkv_w': 8.0,
     'L2_xcond_qkv_b': 8.0,
     'L2_xcond_sa_proj_w': 8.0,
     'L2_xcond_sa_proj_b': 25.571,
     'L2_xcond_q_w': 38.748,
     'L2_xcond_q_b': 64.0,
     'L2_xcond_kv_w': 2.945,
     'L2_xcond_kv_b': 50.033,
     'L2_xcond_ca_proj_w': 2.934,
     'L2_xcond_ca_proj_b': 31.12,
     'L2_xcond_fc1_w': 8.0,
     'L2_xcond_fc1_b': 8.0,
     'L2_xcond_fc2_w': 8.0,
     'L2_xcond_fc2_b': 36.157,
     'L3_xcond_Wq': 8.0,
     'L3_xcond_Wk': 8.0,
     'L3_xcond_Wv': 7.152,
     'L3_xcond_router_W': 4.125,
     'L3_xcond_e_w1': 3.125,
     'L3_xcond_gate_w1': 8.0,
     'L3_xcond_gate_w2': 7.595}
    for name, (base, spread) in spreads.items():
        noise = np.random.default_rng([zlib.crc32(name.encode()), seed]).standard_normal(out[name].shape)
        drawn = base * np.exp(spread * noise) if base else spread * noise
        out[name] = jnp.asarray(drawn.astype(out[name].dtype))
    for name, factor in factors.items():
        out[name] = (out[name] * factor).astype(out[name].dtype)
    return out
```

```python
from contextlib import ExitStack

import concourse.bass as bass
from concourse import mybir

F32 = mybir.dt.float32
ALU = mybir.AluOpType
ACT = mybir.ActivationFunctionType
AX = mybir.AxisListType

B, T, C = 64, 128, 128
S = 77
H, D = 16, 8
WIN, SHIFT = 64, 32
HID = 512
G = 4
NG = B // G
GT = G * T
TOPK = 16
E = 3
RH = 2 * C
NEG = -3.0e38
SCALE = float(D) ** -0.5
BANK = 512

W_WIDTH = {
    "qkv0": 3 * C, "so0": C, "q0": C, "kv0": 2 * C, "co0": C, "m1_0": 2 * HID, "m2_0": 4 * C,
    "qkv1": 3 * C, "so1": C, "q1": C, "kv1": 2 * C, "co1": C, "m1_1": HID, "m2_1": 4 * C,
    "qkv2": 3 * C, "so2": C, "q2": C, "kv2": 2 * C, "co2": C, "m1_2": HID, "m2_2": 4 * C,
    "q3": C, "k3": C, "v3": C, "rw": 3 * E, "e1": E * 3 * RH, "e2": E * 2 * C,
    "g1": 3 * C, "g2": C, "ow": C,
}
W_AT = {}
for _n, _w in W_WIDTH.items():
    W_AT[_n] = sum(W_WIDTH[k] for k in W_AT)
W_COLS = sum(W_WIDTH.values())
B_WIDTH = {
    "mod": 21, "qkv0": 3, "so0": 1, "q0": 1, "kv0": 2, "co0": 1, "m1_0": 8, "m2_0": 1,
    "qkv1": 3, "so1": 1, "q1": 1, "kv1": 2, "co1": 1, "m1_1": 4, "m2_1": 1,
    "qkv2": 3, "so2": 1, "q2": 1, "kv2": 2, "co2": 1, "m1_2": 4, "m2_2": 1,
    "gamma": 1, "beta": 1, "e1": 6, "g1": 1, "g2": 1, "ow": 1,
}
B_AT = {}
for _n, _w in B_WIDTH.items():
    B_AT[_n] = sum(B_WIDTH[k] for k in B_AT)
B_COLS = sum(B_WIDTH.values())
SH_A = [0, 9, 15]
SC_A, G_A = [1, 10, 16], [2, 11, 17]
SH_C0, SC_C0, G_C0 = 3, 4, 5
SH_M, SC_M, G_M = [6, 12, 18], [7, 13, 19], [8, 14, 20]
GATED = [("so0", 2), ("co0", 5), ("m2_0", 8), ("so1", 11), ("m2_1", 14), ("so2", 17), ("m2_2", 20)]


def after(engine, sem, value):
    if isinstance(value, int) and value <= 0:
        return
    assert isinstance(value, int) or value.min_val > 0
    engine.wait_ge(sem, value)


def after_alone(engine, sem, value):
    after(engine, sem, value)
    if not isinstance(value, int):
        engine.nop(nofuse=True)


class Resident:
    pass


def resident(nc, ctx):
    r = Resident()

    def sb(name, shape):
        return ctx.enter_context(nc.sbuf_tensor(name, shape, F32))

    r.x = sb("x_res", [T, B, C])
    r.ctxT = sb("ctxT", [C, B, S])
    r.w = sb("weights", [C, W_COLS])
    r.bias = sb("bias_cols", [C, B_COLS])
    r.mod = sb("mod", [C, 21, B])
    r.gb = sb("gate_bias", [C, len(GATED), B])
    r.anchor = sb("anchor", [C, 7, B])
    r.anchor_rt = sb("anchor_rt", [E, B])
    r.ident = sb("ident", [C, C])
    r.neg_half = sb("neg_half", [T, G])

    def W(name, c0=0, n=C):
        return r.w[:, W_AT[name] + c0:W_AT[name] + c0 + n]

    def bcol(name, k=0):
        return r.bias[:, B_AT[name] + k:B_AT[name] + k + 1]

    r.W, r.bcol = W, bcol
    return r


def setup_phase(nc, r, io):
    with nc.cleanup_on_exit(), ExitStack() as ctx:
        def sb(name, shape):
            return ctx.enter_context(nc.sbuf_tensor(name, shape, F32))

        def sem(name):
            return nc.alloc_semaphore(name)

        wmod = sb("wmod", [C, 21 * C])
        cond = sb("cond", [B, C])
        condT = sb("condT", [C, B])
        siluT = sb("siluT", [C, B])
        ctx_in = sb("ctx_in", [S, 2, G, C])
        ctx_n = sb("ctx_n", [S, 2, G, C])
        stats = sb("stats", [S, 2, G, 6])
        mv = sb("mv", [S, 2, G, 2])
        vareps = sb("vareps", [S, 2, G])
        rstd = sb("rstd", [S, 2, G])
        rb = sb("rb", [E, 1])
        modps = ctx.enter_context(nc.psum_tensor("modps", [C, 4, BANK], F32))
        cps = ctx.enter_context(nc.psum_tensor("cps", [C, 2, BANK], F32))
        nps = ctx.enter_context(nc.psum_tensor("nps", [C, 2, BANK], F32))
        x_in, w_in, bias_in, cond_in, misc_in = (sem(n) for n in ("x_in", "w_in", "bias_in", "cond_in", "misc_in"))
        ctx_ready = [sem("ctx_ready0"), sem("ctx_ready1")]
        ident_ready, const_ready, kbd_ready = sem("ident_ready"), sem("const_ready"), sem("kbd_ready")
        cond_t, cond_c, silu_c = sem("cond_t"), sem("cond_c"), sem("silu_c")
        mod_ps, mod_done, gb_done = sem("mod_ps"), sem("mod_done"), sem("gb_done")
        raw_ps, raw_out, nrm_ps, nrm_out = sem("raw_ps"), sem("raw_out"), sem("nrm_ps"), sem("nrm_out")
        st_done, mv_done, ve_done, rstd_done, xn_done = (sem(n) for n in ("st_done", "mv_done", "ve_done", "rstd_done", "xn_done"))
        block = ctx.enter_context(nc.Block())
        ctx_v = io["ctx"].rearrange("b s c -> s b c")
        x_v = io["x"].rearrange("b t c -> t b c")
        NA = 16

        @block.sync
        def _(sp):
            sp.dma_start(cond[:, :], io["cond"]).then_inc(cond_in, 16)
            sp.dma_start(r.bias[:, :], io["bias"]).then_inc(bias_in, 16)
            sp.dma_start(rb[:, :], io["router_b"].rearrange("(e a) -> e a", a=1)).then_inc(misc_in, 16)
            sp.dma_start(wmod[:, :], io["wmod"]).then_inc(w_in, 16)
            for g in range(2):
                sp.dma_start(ctx_in[:, g], ctx_v[:, G * g:G * g + G, :]).then_inc(ctx_ready[g], 16)
            sp.dma_start(r.w[:, :], io["weights"]).then_inc(w_in, 16)
            for k in range(B // NA):
                sp.dma_start(r.x[0:T - SHIFT, NA * k:NA * k + NA, :],
                             x_v[SHIFT:T, NA * k:NA * k + NA, :]).then_inc(x_in, 16)
                sp.dma_start(r.x[T - SHIFT:T, NA * k:NA * k + NA, :],
                             x_v[0:SHIFT, NA * k:NA * k + NA, :]).then_inc(x_in, 16)
            with sp.Fori(0, NG // 2 - 1) as t:
                for p in range(2):
                    after_alone(sp, raw_ps, 2 * t + (p + 1))
                    after_alone(sp, xn_done, 2 * t + (p + 1))
                    sp.dma_start(ctx_in[:, p], ctx_v[:, bass.ds(8 * t + (8 + 4 * p), G), :]
                                 ).then_inc(ctx_ready[p], 16)
            sp.wait_ge(x_in, 32 * (B // NA))

        @block.gpsimd
        def _(pool):
            nc.gpsimd.memset(r.ident[:, :], 0.0).then_inc(const_ready, 1)
            nc.gpsimd.memset(r.neg_half[:, :], -0.5).then_inc(const_ready, 1)
            pool.wait_ge(const_ready, 2)
            nc.gpsimd.affine_select(out=r.ident[:, :], in_=r.ident[:, :], compare_op=ALU.not_equal,
                                    fill=1.0, base=0, pattern=[[-1, C]], channel_multiplier=1
                                    ).then_inc(ident_ready, 1)
            with pool.Fori(0, NG // 2) as t:
                for p in range(2):
                    pool.wait_ge(ve_done, 2 * t + (p + 1))
                    nc.gpsimd.tensor_tensor(rstd[:, p], vareps[:, p], r.neg_half[0:S, :],
                                            ALU.pow).then_inc(rstd_done, 1)

        @block.scalar
        def _(act):
            act.wait_ge(cond_t, 1)
            nc.scalar.copy(condT[:, :], modps[:, 3, 0:B]).then_inc(cond_c, 1)
            nc.scalar.activation(siluT[:, :], modps[:, 3, 0:B], ACT.Silu).then_inc(silu_c, 1)
            with act.Fori(0, NG // 2) as t:
                for p in range(2):
                    after_alone(act, raw_ps, 2 * t + (p + 1))
                    nc.scalar.copy(r.ctxT[:, bass.ds(8 * t + 4 * p, G), :],
                                   cps[:, p, 0:G * S].rearrange("c (b s) -> c b s", s=S)).then_inc(raw_out, 1)
                    after_alone(act, nrm_ps, 2 * t + (p + 1))
                    nc.scalar.copy(r.ctxnT[:, bass.ds(8 * t + 4 * p, G), :],
                                   nps[:, p, 0:G * S].rearrange("c (b s) -> c b s", s=S)).then_inc(nrm_out, 1)

        @block.vector
        def _(dve):
            nc.vector.memset(r.kbd[:, :, :], 0.0).then_inc(kbd_ready, 1)
            dve.wait_ge(bias_in, 16)
            dve.wait_ge(mod_ps, 1)
            for k in range(21):
                plus = 1.0 if k in SC_A + [SC_C0] + SC_M else 0.0
                last = nc.vector.tensor_scalar(r.mod[:, k, :], modps[:, k // 8, (k % 8) * B:(k % 8 + 1) * B],
                                               r.bcol("mod", k), plus, ALU.add, ALU.add)
            last.then_inc(mod_done, 1)
            dve.wait_ge(mod_done, 1)
            for n, (name, k) in enumerate(GATED):
                nc.vector.tensor_scalar(r.gb[:, n, :], r.mod[:, k, :], r.bcol(name), None,
                                        ALU.mult).then_inc(gb_done, 1)
            dve.wait_ge(mod_ps, 2)
            dve.wait_ge(misc_in, 16)
            for k in range(7):
                bias = r.bcol("e1", k) if k < 6 else r.bcol("g1")
                last = nc.vector.tensor_scalar(r.anchor[:, k, :], modps[:, 3, k * B:(k + 1) * B],
                                               bias, None, ALU.add)
            last = nc.vector.tensor_scalar(r.anchor_rt[:, :], modps[0:E, 3, 7 * B:8 * B], rb[:, 0:1],
                                           None, ALU.add).then_inc(gb_done, 1)
            def normalise_context(t):
                for p in range(2):
                    dve.wait_ge(ctx_ready[p], 16 * t + 16)
                    for b in range(G):
                        last = nc.vector.bn_stats(stats[:, p, b, :], ctx_in[:, p, b, :])
                    last.then_inc(st_done, 1)
                    after_alone(dve, st_done, 2 * t + (p + 1))
                    for b in range(G):
                        last = nc.vector.bn_aggr(mv[:, p, b, :], stats[:, p, b, :])
                    last.then_inc(mv_done, 1)
                    dve.wait_ge(mv_done, 2 * t + (p + 1))
                    nc.vector.tensor_scalar(vareps[:, p], mv[:, p, :, 1], 1e-6, None, ALU.add
                                            ).then_inc(ve_done, 1)
                    dve.wait_ge(rstd_done, 2 * t + (p + 1))
                    after(dve, nrm_ps, 2 * t)
                    for b in range(G):
                        last = nc.vector.tensor_scalar(ctx_n[:, p, b, :], ctx_in[:, p, b, :],
                                                       mv[:, p, b, 0:1], rstd[:, p, b:b + 1],
                                                       ALU.subtract, ALU.mult)
                    last.then_inc(xn_done, 1)

            normalise_context(0)
            with dve.Fori(1, NG // 2) as t:
                normalise_context(t)

        @block.tensor
        def _(pe):
            pe.wait_ge(ident_ready, 1)
            pe.wait_ge(cond_in, 16)
            nc.tensor.transpose(modps[:, 3, 0:B], cond[:, :], r.ident[0:B, 0:B]).then_inc(cond_t, 1)
            pe.wait_ge(silu_c, 1)
            pe.wait_ge(w_in, 32)
            for k in range(21):
                last = nc.tensor.matmul(modps[:, k // 8, (k % 8) * B:(k % 8 + 1) * B],
                                        wmod[:, k * C:(k + 1) * C], siluT[:, :], start=True, stop=True)
            last.then_inc(mod_ps, 1)
            for k in range(6):
                e, c = divmod(k, 2)
                nc.tensor.matmul(modps[:, 3, k * B:(k + 1) * B],
                                 r.W("e1", (e * 3 + 2) * RH + c * C), condT[:, :], start=True, stop=True)
            nc.tensor.matmul(modps[:, 3, 6 * B:7 * B], r.W("g1", 2 * C), condT[:, :], start=True, stop=True)
            nc.tensor.matmul(modps[0:E, 3, 7 * B:8 * B], r.W("rw", 2 * E, E), condT[:, :],
                             start=True, stop=True).then_inc(mod_ps, 1)
            def transpose_context(t):
                for p in range(2):
                    pe.wait_ge(ctx_ready[p], 16 * t + 16)
                    after(pe, raw_out, 2 * t)
                    for b in range(G):
                        last = nc.tensor.transpose(cps[:, p, b * S:(b + 1) * S], ctx_in[:, p, b, :],
                                                   r.ident[0:S, 0:S])
                    last.then_inc(raw_ps, 1)
                    pe.wait_ge(xn_done, 2 * t + (p + 1))
                    after(pe, nrm_out, 2 * t)
                    for b in range(G):
                        last = nc.tensor.transpose(nps[:, p, b * S:(b + 1) * S], ctx_n[:, p, b, :],
                                                   r.ident[0:S, 0:S])
                    last.then_inc(nrm_ps, 1)

            transpose_context(0)
            with pe.Fori(1, NG // 2) as t:
                transpose_context(t)


def attention_phase(nc, r, layer, kind):
    window, cross, topk = kind == "window", kind in ("cross", "topk"), kind == "topk"
    keys = S if cross else T
    NU = 2 if window else 4
    NS = G * NU
    HU = H // NU
    cols = HU * WIN if window else HU * keys
    rows = T if window else keys
    VM = 18 if window else 9
    XT, KP, QP, VP, ONT, PROJ, PGT = (0, 1, 2, 3, 5, 6, 7) if window else (0, 3, 5, 7, 9, 11, 14)
    STATS, AGGR, APPLY = ((2, 2, 3, 3), 4, (6, 6, 7, 7)) if window else ((1, 2, 3, 5), 6, (9, 10, 11, 15))
    LT = 3 if topk else 2
    LV, LO = LT + 1, LT + 2
    name_o = f"{'co' if cross else 'so'}{layer}"
    gate = dict(GATED).get(name_o)
    n_gb = [n for n, _ in GATED].index(name_o) if gate is not None else None
    if kind == "topk":
        scale_at, shift_at = SC_C0, SH_C0
    elif cross:
        scale_at = shift_at = None
    else:
        scale_at, shift_at = SC_A[layer], SH_A[layer]
    wq = r.W(f"q{layer}") if cross else r.W(f"qkv{layer}", 0)
    wk = r.W(f"kv{layer}", 0) if cross else r.W(f"qkv{layer}", C)
    wv = r.W(f"kv{layer}", C) if cross else r.W(f"qkv{layer}", 2 * C)
    bq = r.bcol(f"q{layer}") if cross else r.bcol(f"qkv{layer}", 0)
    bk = r.bcol(f"kv{layer}", 0) if cross else r.bcol(f"qkv{layer}", 1)
    bv = r.bcol(f"kv{layer}", 1) if cross else r.bcol(f"qkv{layer}", 2)
    source = r.ctxnT if layer == 1 else r.ctxT

    with nc.cleanup_on_exit(), ExitStack() as ctx:
        tag = f"{kind}{layer}_"

        def sb(name, shape):
            return ctx.enter_context(nc.sbuf_tensor(tag + name, shape, F32))

        def ps(name, shape):
            return ctx.enter_context(nc.psum_tensor(tag + name, shape, F32))

        def sem(name):
            return nc.alloc_semaphore(tag + name)

        stats, mv = sb("stats", [T, G, 6]), sb("mv", [T, G, 2])
        vareps, rstd = sb("vareps", [T, G]), sb("rstd", [T, G])
        xn = sb("xn", [T, G, C])
        hT = sb("hT", [C, GT])
        ctxs = sb("ctxs", [C, G * S]) if cross else None
        qT, kT = sb("qT", [C, 2, GT]), sb("kT", [C, 2, G * keys])
        vp = sb("vp", [T, 2, G, 2, 8, VM]) if window else sb("vp", [T, 2, G, H, VM])
        top = sb("top", [T, 2, HU, 8]) if topk else None
        top2 = sb("top2", [T, 2, HU, 8]) if topk else None
        work = sb("work", [T, 4, cols]) if topk else None
        mask = sb("mask", [T, 2, cols]) if topk else None
        mx = sb("mx", [T, 2, HU])
        dif = sb("dif", [T, 2, HU if topk else cols])
        prob = sb("prob", [T, 4, cols])
        pT = sb("pT", [T, 2, BANK])
        oT = sb("oT", [T, 2, NU * T])
        rden = sb("rden", [T, 2, H])
        on = sb("on", [T, G, C])
        onT, pg = sb("onT", [C, GT]), sb("pg", [C, GT])
        s_ps = ps("s", [T, 2, BANK])
        t_ps = ps("t", [T, 2, BANK])
        o_ps = ps("o", [T, 2, BANK])
        l_ps = ps("l", [T, BANK])
        r_ps = ps("r", [T, BANK])

        s_scores, s_max, s_dif, s_exp = sem("scores"), sem("max"), sem("dif"), sem("exp")
        s_probT, s_pT, s_pv = sem("probT"), sem("pT"), sem("pv")
        s_picked = sem("picked")
        s_top, s_cut, s_top2, s_cut2 = sem("top"), sem("cut"), sem("top2"), sem("cut2")
        s_mask = sem("mask")
        s_oT, s_otr, s_rden, s_norm = sem("oT"), sem("otr"), sem("rden"), sem("norm")
        s_stats, s_mv, s_var, s_rstd, s_xn = sem("stats"), sem("mv"), sem("var"), sem("rstd"), sem("xn")
        s_xT, s_hT, s_kps, s_kT, s_qps, s_qT = sem("xT"), sem("hT"), sem("kps"), sem("kT"), sem("qps"), sem("qT")
        s_vps, s_v = sem("vps"), sem("v")
        s_kbd = [sem("kbd0"), sem("kbd1")]
        s_ctx = sem("ctx")
        s_onps, s_onT, s_pjps, s_pg, s_pgps, s_x = sem("onps"), sem("onT"), sem("pjps"), sem("pg"), sem("pgps"), sem("x")
        s_init, s_zero = sem("init"), sem("zero")
        NV = 2 if window else 1
        KB = 16 * H
        block = ctx.enter_context(nc.Block())

        def iterations(engine, body, prologue):
            prologue()
            body(0, 0, True, True, True, True)
            body(1, 1, False, True, True, True)
            with engine.Fori(1, NG // 2 - 1) as t:
                body(2 * t, 0, False, True, True, True)
                body(2 * t + 1, 1, False, True, True, True)
            body(NG - 2, 0, False, True, True, False)
            body(NG - 1, 1, False, True, False, False)
            body(NG, 0, False, False, False, False)

        def lagged(u, lag, first, units):
            c = u - lag
            return c if (units if c >= 0 else not first) else None

        def sequence_hooks(u, first, units):
            c = lagged(u, NU + LO, first, units)
            return c // NU if c is not None and c % NU == 0 else None

        @block.sync
        def _(sp):
            def stage_context(g):
                after_alone(sp, s_vps, g)
                sp.dma_start(ctxs[:, :].rearrange("c (b s) -> c b s", s=S),
                             source[:, bass.ds(G * g, G), :]).then_inc(s_ctx, 16)

            def spread_keys(g, half, par, scores_done):
                after_alone(sp, s_kT, g + 1)
                after_alone(sp, s_scores, scores_done)
                c0, n = half * 2 * keys, 2 * keys
                for h in range(H):
                    sp.dma_start(r.kbd[D * h:D * h + D, h, c0:c0 + n],
                                 kT[D * h:D * h + D, par, c0:c0 + n]).then_inc(s_kbd[half], 16)

            def prologue():
                if cross:
                    stage_context(0)
                spread_keys(0, 0, 0, 0)
                spread_keys(0, 1, 0, 0)
                if cross:
                    stage_context(1)

            def body(i, par, first, units, pre, ln):
                if not pre:
                    return
                spread_keys(i + 1, 0, 1 - par, NS * i + NS // 2)
                if cross and ln:
                    stage_context(i + 2)
                spread_keys(i + 1, 1, 1 - par, NS * i + NS)

            iterations(sp, body, prologue)

        @block.gpsimd
        def _(pool):
            nc.gpsimd.memset(vp[:, :], 0.0).then_inc(s_init, 1)
            pool.wait_ge(s_init, 1)
            if window:
                nc.gpsimd.memset(vp[0:WIN, :, :, :, :, D:D + 1], 1.0).then_inc(s_init, 1)
                nc.gpsimd.memset(vp[WIN:T, :, :, :, :, 2 * D + 1:2 * D + 2], 1.0).then_inc(s_init, 1)
                pool.wait_ge(s_init, 3)
            else:
                nc.gpsimd.memset(vp[:, :, :, :, D:D + 1], 1.0).then_inc(s_init, 1)
                pool.wait_ge(s_init, 2)

            def rstd_of(g):
                pool.wait_ge(s_var, g + 1)
                nc.gpsimd.tensor_tensor(rstd[:, :], vareps[:, :], r.neg_half[:, :], ALU.pow).then_inc(s_rstd, 1)

            def scale_maximum(i, u):
                n = NS * i + u
                after(pool, s_exp, n - 1)
                after_alone(pool, s_top, n + 1)
                nc.gpsimd.tensor_scalar(dif[:, u % 2, :], top[:, u % 2, :, 0], -SCALE, None, ALU.mult
                                        ).then_inc(s_dif, 1)

            def pick(i, u):
                n = NS * i + u
                after_alone(pool, s_cut2, n + 1)
                nc.gpsimd.tensor_scalar(mask[:, u % 2, :], work[:, u % 4, :], NEG / 2, None, ALU.is_le
                                        ).then_inc(s_mask, 1)
                pool.wait_ge(s_mask, n + 1)
                pool.wait_ge(s_exp, n + 1)
                nc.gpsimd.tensor_tensor(prob[:, u % 4, :], prob[:, u % 4, :], mask[:, u % 2, :],
                                        ALU.mult).then_inc(s_picked, 1)

            def prologue():
                rstd_of(0)
                rstd_of(1)

            def body(i, par, first, units, pre, ln):
                for u in range(NS if units else 1):
                    if topk and units:
                        scale_maximum(i, u)
                    c = lagged(u, 1, first, units)
                    if topk and c is not None:
                        pick(i, c)
                    if ln and u == AGGR:
                        rstd_of(i + 2)

            iterations(pool, body, prologue)

        @block.scalar
        def _(act):
            def modulate(g, bs=range(G)):
                if scale_at is None:
                    if bs[-1] < G - 1:
                        return
                    after(act, s_xT, g + 1)
                    nc.scalar.copy(hT[:, :], l_ps[:, :]).then_inc(s_hT, 1)
                    return
                after_alone(act, s_xT, g + 1)
                for b in bs:
                    last = nc.scalar.activation(
                        hT[:, b * T:(b + 1) * T], l_ps[:, b * T:(b + 1) * T], ACT.Identity,
                        scale=r.mod[:, scale_at, bass.ds(G * g + b, 1)],
                        bias=r.mod[:, shift_at, bass.ds(G * g + b, 1)])
                if bs[-1] == G - 1:
                    last.then_inc(s_hT, 1)

            def keys_out(g, par):
                after(act, s_kbd[1], KB * (g - 1))
                after(act, s_kbd[0], KB * (g - 1))
                act.wait_ge(s_kps, g + 1)
                nc.scalar.activation(kT[:, par, :], l_ps[:, 0:G * keys], ACT.Identity, bias=bk
                                     ).then_inc(s_kT, 1)

            def queries_out(g, par):
                act.wait_ge(s_qps, g + 1)
                nc.scalar.activation(qT[:, par, :], l_ps[:, :], ACT.Identity, bias=bq).then_inc(s_qT, 1)

            def prologue():
                modulate(0)
                keys_out(0, 0)
                queries_out(0, 0)

            def body(i, par, first, units, pre, ln):
                for u in range(NS if units else PGT + 1):
                    c = lagged(u, LT, first, units)
                    if c is not None:
                        n = NS * i + c
                        after(act, s_pv, n - 1)
                        act.wait_ge(s_probT, n + 1)
                        nc.scalar.copy(pT[0:rows, c % 2, :], t_ps[0:rows, c % 2, :]).then_inc(s_pT, 1)
                    c = lagged(u, LO, first, units)
                    if c is not None and c % NU == NU - 1:
                        m = G * i + c // NU
                        b = c // NU
                        after(act, s_otr, m - 1)
                        act.wait_ge(s_pv, NS * i + c + 1)
                        nc.scalar.copy(oT[:, b % 2, :], o_ps[:, b % 2, 0:NU * T]).then_inc(s_oT, 1)
                    if units:
                        n = NS * i + u
                        after(act, s_probT, n - 3)
                        if topk:
                            act.wait_ge(s_cut, n + 1)
                            act.wait_ge(s_dif, n + 1)
                            for h in range(HU):
                                last = nc.scalar.activation(prob[:, u % 4, h * keys:(h + 1) * keys],
                                                            s_ps[:, u % 2, h * keys:(h + 1) * keys], ACT.Exp,
                                                            scale=SCALE, bias=dif[:, u % 2, h:h + 1])
                            last.then_inc(s_exp, 1)
                        else:
                            act.wait_ge(s_dif, n + 1)
                            nc.scalar.activation(prob[:, u % 4, :], dif[:, u % 2, :], ACT.Exp, scale=SCALE
                                                 ).then_inc(s_exp, 1)
                    if pre and window and u == XT:
                        modulate(i + 1)
                    if pre and not window and u == XT:
                        modulate(i + 1, range(0, G // 2))
                    if pre and not window and u == XT + 1:
                        modulate(i + 1, range(G // 2, G))
                    if pre and u == KP:
                        keys_out(i + 1, 1 - par)
                    if pre and u == QP:
                        queries_out(i + 1, 1 - par)
                    if not first and u == ONT:
                        act.wait_ge(s_onps, i)
                        nc.scalar.activation(onT[:, :], l_ps[:, :], ACT.Identity, bias=bv).then_inc(s_onT, 1)
                    if not first and gate is None and u == PROJ:
                        act.wait_ge(s_pjps, i)
                        nc.scalar.activation(pg[:, :], l_ps[:, :], ACT.Identity, bias=r.bcol(name_o)
                                             ).then_inc(s_pg, 1)
                    if not first and gate is not None:
                        bs = {PROJ: range(G)} if window else {PROJ: range(0, 2), PROJ + 1: range(2, G)}
                        if u in bs:
                            after_alone(act, s_pjps, i)
                            for b in bs[u]:
                                at = G * i - G + b
                                last = nc.scalar.activation(
                                    pg[:, b * T:(b + 1) * T], l_ps[:, b * T:(b + 1) * T], ACT.Identity,
                                    scale=r.mod[:, gate, bass.ds(at, 1)],
                                    bias=r.gb[:, n_gb, bass.ds(at, 1)])
                            if bs[u][-1] == G - 1:
                                last.then_inc(s_pg, 1)

            iterations(act, body, prologue)

        @block.vector
        def _(dve):
            nc.vector.memset(o_ps[:, :, :], 0.0).then_inc(s_zero, 1)

            def ln_stats(g, bs=range(G)):
                for b in bs:
                    last = nc.vector.bn_stats(stats[:, b, :], r.x[:, bass.ds(G * g + b, 1), :])
                if bs[-1] == G - 1:
                    last.then_inc(s_stats, 1)

            def ln_variance(g):
                after_alone(dve, s_stats, g + 1)
                for b in range(G):
                    last = nc.vector.bn_aggr(mv[:, b, :], stats[:, b, :])
                last.then_inc(s_mv, 1)
                dve.wait_ge(s_mv, g + 1)
                nc.vector.tensor_scalar(vareps[:, :], mv[:, :, 1], 1e-6, None, ALU.add).then_inc(s_var, 1)

            def ln_apply(g, bs=range(G)):
                if bs[0] == 0:
                    after(dve, s_xT, g)
                    dve.wait_ge(s_rstd, g + 1)
                for b in bs:
                    last = nc.vector.tensor_scalar(xn[:, b:b + 1, :], r.x[:, bass.ds(G * g + b, 1), :],
                                                   mv[:, b, 0:1], rstd[:, b:b + 1], ALU.subtract, ALU.mult)
                if bs[-1] == G - 1:
                    last.then_inc(s_xn, 1)

            def values_out(g, par, w):
                dve.wait_ge(s_vps, NV * g + w + 1)
                if window:
                    for a in range(2):
                        p0 = WIN * a
                        last = nc.vector.tensor_copy(
                            vp[p0:p0 + WIN, par, :, w, :, (D + 1) * a:(D + 1) * a + D],
                            l_ps[p0:p0 + WIN, :].rearrange("p (b h d) -> p b h d", b=G, d=2 * D)
                            [:, :, :, D * a:D * a + D])
                    last.then_inc(s_v, 1)
                else:
                    nc.vector.tensor_copy(vp[0:keys, par, :, :, 0:D],
                                          l_ps[0:keys, :].rearrange("p (b h d) -> p b h d", b=G, d=D)
                                          ).then_inc(s_v, 1)

            def max_and_difference(i, u):
                n = NS * i + u
                sc = s_ps[:, u % 2, 0:cols].rearrange("p (h k) -> p h k", h=HU)
                after(dve, s_exp, n - 1)
                dve.wait_ge(s_scores, n + 1)
                nc.vector.tensor_reduce(mx[:, u % 2, :], sc, AX.X, ALU.max).then_inc(s_max, 1)
                dve.wait_ge(s_max, n + 1)
                m = mx[:, u % 2, :].rearrange("p (h a) -> p h a", a=1)
                nc.vector.tensor_tensor(dif[:, u % 2, :].rearrange("p (h k) -> p h k", h=HU), sc,
                                        m.broadcast_to([T, HU, cols // HU]), ALU.subtract).then_inc(s_dif, 1)

            def find_top(i, u, first, units):
                c = lagged(u, 1, first, units)
                n = NS * i + u
                wk_ = [work[:, k, :].rearrange("p (h k) -> p h k", h=HU) for k in range(4)]
                sc = s_ps[:, u % 2, 0:cols].rearrange("p (h k) -> p h k", h=HU)
                if units:
                    after_alone(dve, s_dif, n - 1)
                    after_alone(dve, s_scores, n + 1)
                    for h in range(HU):
                        last = nc.vector.max(top[:, u % 2, h, :], sc[:, h, :])
                    last.then_inc(s_top, 1)
                if c is not None:
                    after_alone(dve, s_cut, n)
                    for h in range(HU):
                        last = nc.vector.max(top2[:, c % 2, h, :], wk_[c % 4][:, h, :])
                    last.then_inc(s_top2, 1)
                if units:
                    after_alone(dve, s_top, n + 1)
                    after_alone(dve, s_picked, n - 3)
                    for h in range(HU):
                        last = nc.vector.match_replace(wk_[u % 4][:, h, :], top[:, u % 2, h, :], sc[:, h, :], NEG)
                    last.then_inc(s_cut, 1)
                if c is not None:
                    after_alone(dve, s_top2, n)
                    for h in range(HU):
                        last = nc.vector.match_replace(wk_[c % 4][:, h, :], top2[:, c % 2, h, :],
                                                       wk_[c % 4][:, h, :], NEG)
                    last.then_inc(s_cut2, 1)

            def normalise(i, b):
                m = G * i + b
                dve.wait_ge(s_otr, m + 1)
                rv = rden[:, b % 2, :]
                if window:
                    src = r_ps[:, 0:NU * T].rearrange("p (q c) -> p q c", c=32)
                    nc.vector.reciprocal(rv.rearrange("p (q a) -> p q a", a=2),
                                         src[:, :, D:2 * D + 2:D + 1]).then_inc(s_rden, 1)
                else:
                    src = r_ps[:, :].rearrange("p (h c) -> p h c", c=32)
                    nc.vector.reciprocal(rv, src[:, :, D]).then_inc(s_rden, 1)
                if b % G == 0:
                    after(dve, s_onps, i)
                dve.wait_ge(s_rden, m + 1)
                out = on[:, b % G, :].rearrange("p (h d) -> p h d", d=D)
                if window:
                    for a in range(2):
                        last = nc.vector.tensor_tensor(
                            out[:, a::2, :], src[:, :, (D + 1) * a:(D + 1) * a + D],
                            rv[:, a::2].rearrange("p (q a) -> p q a", a=1).broadcast_to([T, H // 2, D]), ALU.mult)
                else:
                    last = nc.vector.tensor_tensor(
                        out, src[:, :, 0:D],
                        rv.rearrange("p (h a) -> p h a", a=1).broadcast_to([T, H, D]), ALU.mult)
                last.then_inc(s_norm, 1)

            def prologue():
                ln_stats(0)
                ln_variance(0)
                ln_apply(0)
                ln_stats(1)
                ln_variance(1)
                ln_apply(1)
                for w in range(NV):
                    values_out(0, 0, w)

            def body(i, par, first, units, pre, ln):
                for u in range(NS if units else PGT + 1):
                    if topk:
                        find_top(i, u, first, units) if units or u == 0 else None
                    elif units:
                        max_and_difference(i, u)
                    if pre and u in (VP, VP + 1)[:NV]:
                        values_out(i + 1, 1 - par, u - VP)
                    if ln and u in STATS:
                        ln_stats(i + 2, [b for b in range(G) if STATS[b] == u])
                    if ln and u == AGGR:
                        ln_variance(i + 2)
                    if ln and u in APPLY:
                        ln_apply(i + 2, [b for b in range(G) if APPLY[b] == u])
                    b = sequence_hooks(u, first, units)
                    if b is not None:
                        normalise(i, b)
                    if not first and u == PGT:
                        after_alone(dve, s_pgps, i)
                        xg = r.x[:, bass.ds(G * i - G, G), :]
                        nc.vector.tensor_tensor(xg, r_ps[:, :].rearrange("p (b c) -> p b c", b=G), xg,
                                                ALU.add).then_inc(s_x, 1)

            iterations(dve, body, prologue)

        @block.tensor
        def _(pe):
            def transpose_xn(g):
                after(pe, s_v, NV * g)
                after(pe, s_pg, g - 2)
                pe.wait_ge(s_xn, g + 1)
                for b in range(G):
                    last = nc.tensor.transpose(l_ps[:, b * T:(b + 1) * T], xn[:, b, :], r.ident[:, :])
                last.then_inc(s_xT, 1)

            def project_keys(g):
                if cross:
                    pe.wait_ge(s_ctx, 16 * g + 16)
                pe.wait_ge(s_hT, g + 1)
                nc.tensor.matmul(l_ps[:, 0:G * keys], wk, ctxs[:, :] if cross else hT[:, :],
                                 start=True, stop=True).then_inc(s_kps, 1)

            def project_queries(g):
                pe.wait_ge(s_kT, g + 1)
                nc.tensor.matmul(l_ps[:, :], wq, hT[:, :], start=True, stop=True).then_inc(s_qps, 1)

            def project_values(g, w):
                if w == 0:
                    pe.wait_ge(s_qT, g + 1)
                else:
                    pe.wait_ge(s_v, NV * g + w)
                for b in range(G):
                    if window:
                        for a in range(2):
                            last = nc.tensor.matmul(l_ps[WIN * a:WIN * a + WIN, b * C:(b + 1) * C],
                                                    hT[:, b * T + WIN * w:b * T + WIN * w + WIN], wv,
                                                    start=True, stop=True)
                    else:
                        lhs = ctxs[:, b * S:(b + 1) * S] if cross else hT[:, b * T:(b + 1) * T]
                        last = nc.tensor.matmul(l_ps[0:keys, b * C:(b + 1) * C], lhs, wv,
                                                start=True, stop=True)
                last.then_inc(s_vps, 1)

            def scores(i, u, par):
                n = NS * i + u
                if u == 0:
                    pe.wait_ge(s_qT, i + 1)
                    pe.wait_ge(s_kbd[0], KB * i + KB)
                if u == NS // 2:
                    pe.wait_ge(s_kbd[1], KB * i + KB)
                if topk:
                    after(pe, s_exp, n - 1)
                else:
                    after(pe, s_dif, n - 1)
                b, g = divmod(u, NU)
                if window:
                    for w in range(2):
                        c0 = b * T + WIN * w
                        last = nc.tensor.matmul(s_ps[WIN * w:WIN * w + WIN, u % 2, 0:cols],
                                                qT[:, par, c0:c0 + WIN],
                                                r.kbd[:, HU * g:HU * g + HU, c0:c0 + WIN],
                                                start=True, stop=True)
                else:
                    last = nc.tensor.matmul(s_ps[:, u % 2, 0:cols], qT[:, par, b * T:(b + 1) * T],
                                            r.kbd[:, HU * g:HU * g + HU, b * keys:(b + 1) * keys],
                                            start=True, stop=True)
                last.then_inc(s_scores, 1)

            def transpose_probs(i, c):
                n = NS * i + c
                after(pe, s_pT, n - 1)
                pe.wait_ge(s_picked if topk else s_exp, n + 1)
                for j in range(4):
                    last = nc.tensor.transpose(t_ps[0:rows, c % 2, j * T:(j + 1) * T],
                                               prob[:, c % 4, j * rows:(j + 1) * rows], r.ident[:, :])
                last.then_inc(s_probT, 1)

            def values_times_probs(i, c, par):
                n = NS * i + c
                b, g = divmod(c, NU)
                if g == 0:
                    after(pe, s_oT, G * i + b - 1)
                if c % NS == 0:
                    pe.wait_ge(s_v, NV * i + NV) if c == 0 else None
                pe.wait_ge(s_pT, n + 1)
                b %= G
                for j in range(4):
                    if window:
                        for w in range(2):
                            last = nc.tensor.matmul(
                                o_ps[32 * j:32 * j + VM, b % 2, g * T + WIN * w:g * T + WIN * w + WIN],
                                vp[:, par, b, w, 4 * g + j, :],
                                pT[:, c % 2, j * T + WIN * w:j * T + WIN * w + WIN],
                                start=True, stop=True, tile_position=(0, 32 * j))
                    else:
                        last = nc.tensor.matmul(o_ps[32 * j:32 * j + VM, b % 2, g * T:(g + 1) * T],
                                                vp[0:keys, par, b, HU * g + j, :],
                                                pT[0:keys, c % 2, j * T:(j + 1) * T],
                                                start=True, stop=True, tile_position=(0, 32 * j))
                last.then_inc(s_pv, 1)

            def output_to_rows(i, b):
                m = G * i + b
                pe.wait_ge(s_oT, m + 1)
                if b % G == (1 if window else 2):
                    after(pe, s_x, i if b > 0 else i - 1)
                after(pe, s_norm, m)
                for g in range(NU):
                    last = nc.tensor.transpose(r_ps[:, g * T:(g + 1) * T], oT[:, b % 2, g * T:(g + 1) * T],
                                               r.ident[:, :])
                last.then_inc(s_otr, 1)

            def prologue():
                pe.wait_ge(s_init, 3 if window else 2)
                pe.wait_ge(s_zero, 1)
                transpose_xn(0)
                project_keys(0)
                project_queries(0)
                for w in range(NV):
                    project_values(0, w)

            def body(i, par, first, units, pre, ln):
                for u in range(NS if units else PGT + 1):
                    if units:
                        scores(i, u, par)
                    c = lagged(u, LT, first, units)
                    if c is not None:
                        transpose_probs(i, c)
                    c = lagged(u, LV, first, units)
                    if c is not None:
                        values_times_probs(i, c, par if c >= 0 else 1 - par)
                    if pre and u == XT:
                        transpose_xn(i + 1)
                    if pre and u == KP:
                        project_keys(i + 1)
                    if pre and u == QP:
                        project_queries(i + 1)
                    if pre and u in (VP, VP + 1)[:NV]:
                        project_values(i + 1, u - VP)
                    if not first and u == ONT:
                        after(pe, s_v, NV * i + 2 * NV if pre else NV * NG)
                        after(pe, s_pg, i - 1)
                        pe.wait_ge(s_norm, G * i)
                        for b in range(G):
                            last = nc.tensor.transpose(l_ps[:, b * T:(b + 1) * T], on[:, b, :], r.ident[:, :])
                        last.then_inc(s_onps, 1)
                    b = sequence_hooks(u, first, units)
                    if b is not None:
                        output_to_rows(i, b)
                    if not first and u == PROJ:
                        pe.wait_ge(s_onT, i)
                        nc.tensor.matmul(l_ps[:, :], r.W(name_o), onT[:, :], start=True, stop=True
                                         ).then_inc(s_pjps, 1)
                    if not first and u == PGT:
                        after(pe, s_norm, G * i + (1 if window else 2) if units else G * i)
                        pe.wait_ge(s_pg, i)
                        for b in range(G):
                            last = nc.tensor.transpose(r_ps[:, b * C:(b + 1) * C], pg[:, b * T:(b + 1) * T],
                                                       r.ident[:, :])
                        last.then_inc(s_pgps, 1)

            iterations(pe, body, prologue)


def mlp_phase(nc, r, layer):
    swiglu = layer == 0
    NC = HID // C
    name = f"m2_{layer}"
    gate = dict(GATED)[name]
    n_gb = [n for n, _ in GATED].index(name)
    with nc.cleanup_on_exit(), ExitStack() as ctx:
        tag = f"mlp{layer}_"

        def sb(name, shape):
            return ctx.enter_context(nc.sbuf_tensor(tag + name, shape, F32))

        def ps(name, shape):
            return ctx.enter_context(nc.psum_tensor(tag + name, shape, F32))

        def sem(name):
            return nc.alloc_semaphore(tag + name)

        stats, mv = sb("stats", [T, G, 6]), sb("mv", [T, G, 2])
        vareps, rstd = sb("vareps", [T, G]), sb("rstd", [T, G])
        xn, hT = sb("xn", [T, G, C]), sb("hT", [C, GT])
        half = sb("half", [C, 2, GT]) if swiglu else None
        hid = sb("hid", [C, NC, GT])
        pg = sb("pg", [C, GT])
        l_ps, y_ps, r_ps = ps("l", [C, BANK]), ps("y", [C, BANK]), ps("r", [T, BANK])
        u_ps = ps("u", [C, 4, BANK])
        s_stats, s_mv, s_var, s_rstd, s_xn = sem("stats"), sem("mv"), sem("var"), sem("rstd"), sem("xn")
        s_xT, s_hT, s_pg, s_pgps, s_x = sem("xT"), sem("hT"), sem("pg"), sem("pgps"), sem("x")
        s_up, s_half, s_hid, s_down = sem("up"), sem("half"), sem("hid"), sem("down")
        block = ctx.enter_context(nc.Block())

        def iterations(engine, body, prologue):
            prologue()
            body(0, True, True, True, True)
            body(1, False, True, True, True)
            with engine.Fori(2, NG - 2) as g:
                body(g, False, True, True, True)
            body(NG - 2, False, True, True, False)
            body(NG - 1, False, True, False, False)
            body(NG, False, False, False, False)

        @block.gpsimd
        def _(pool):
            def rstd_of(g):
                pool.wait_ge(s_var, g + 1)
                nc.gpsimd.tensor_tensor(rstd[:, :], vareps[:, :], r.neg_half[:, :], ALU.pow).then_inc(s_rstd, 1)

            rstd_of(0)
            rstd_of(1)
            with pool.Fori(2, NG) as g:
                rstd_of(g)

        @block.vector
        def _(dve):
            def ln_stats(g):
                for b in range(G):
                    last = nc.vector.bn_stats(stats[:, b, :], r.x[:, bass.ds(G * g + b, 1), :])
                last.then_inc(s_stats, 1)
                after_alone(dve, s_stats, g + 1)
                for b in range(G):
                    last = nc.vector.bn_aggr(mv[:, b, :], stats[:, b, :])
                last.then_inc(s_mv, 1)
                dve.wait_ge(s_mv, g + 1)
                nc.vector.tensor_scalar(vareps[:, :], mv[:, :, 1], 1e-6, None, ALU.add).then_inc(s_var, 1)

            def ln_apply(g):
                after(dve, s_xT, g)
                dve.wait_ge(s_rstd, g + 1)
                for b in range(G):
                    last = nc.vector.tensor_scalar(xn[:, b:b + 1, :], r.x[:, bass.ds(G * g + b, 1), :],
                                                   mv[:, b, 0:1], rstd[:, b:b + 1], ALU.subtract, ALU.mult)
                last.then_inc(s_xn, 1)

            def prologue():
                ln_stats(0)
                ln_apply(0)
                ln_stats(1)
                ln_apply(1)

            def body(g, first, work, nxt, nxt2):
                for c in range(NC):
                    if work and swiglu:
                        n = NC * g + c
                        after(dve, s_down, n - 3)
                        dve.wait_ge(s_half, n + 1)
                        nc.vector.scalar_tensor_tensor(hid[:, c, :], u_ps[:, (2 * c + 1) % 4, :],
                                                       r.bcol("m1_0", NC + c), half[:, c % 2, :],
                                                       ALU.add, ALU.mult).then_inc(s_hid, 1)
                    if c == 1 and not first:
                        after_alone(dve, s_pgps, g)
                        xg = r.x[:, bass.ds(G * g - G, G), :]
                        nc.vector.tensor_tensor(xg, r_ps[:, :].rearrange("p (b c) -> p b c", b=G), xg,
                                                ALU.add).then_inc(s_x, 1)
                    if c == 2 and nxt2:
                        ln_stats(g + 2)
                if nxt2:
                    ln_apply(g + 2)

            iterations(dve, body, prologue)

        @block.scalar
        def _(act):
            def modulate(g):
                after_alone(act, s_xT, g + 1)
                for b in range(G):
                    last = nc.scalar.activation(
                        hT[:, b * T:(b + 1) * T], l_ps[:, b * T:(b + 1) * T], ACT.Identity,
                        scale=r.mod[:, SC_M[layer], bass.ds(G * g + b, 1)],
                        bias=r.mod[:, SH_M[layer], bass.ds(G * g + b, 1)])
                last.then_inc(s_hT, 1)

            def body(g, first, work, nxt, nxt2):
                if not work:
                    return
                for c in range(NC):
                    n = NC * g + c
                    if swiglu:
                        after(act, s_hid, n - 1)
                        act.wait_ge(s_up, n + 1)
                        nc.scalar.activation(half[:, c % 2, :], u_ps[:, (2 * c) % 4, :], ACT.Silu,
                                             bias=r.bcol("m1_0", c)).then_inc(s_half, 1)
                    else:
                        after(act, s_down, n - 3)
                        act.wait_ge(s_up, n + 1)
                        nc.scalar.activation(hid[:, c, :], u_ps[:, c, :], ACT.Gelu_apprx_tanh,
                                             bias=r.bcol(f"m1_{layer}", c)).then_inc(s_hid, 1)
                if nxt:
                    modulate(g + 1)
                after_alone(act, s_down, NC * g + NC)
                for b in range(G):
                    last = nc.scalar.activation(
                        pg[:, b * T:(b + 1) * T], y_ps[:, b * T:(b + 1) * T], ACT.Identity,
                        scale=r.mod[:, gate, bass.ds(G * g + b, 1)],
                        bias=r.gb[:, n_gb, bass.ds(G * g + b, 1)])
                last.then_inc(s_pg, 1)

            iterations(act, body, lambda: modulate(0))

        @block.tensor
        def _(pe):
            def transpose_xn(g):
                after(pe, s_hT, g)
                pe.wait_ge(s_xn, g + 1)
                for b in range(G):
                    last = nc.tensor.transpose(l_ps[:, b * T:(b + 1) * T], xn[:, b, :], r.ident[:, :])
                last.then_inc(s_xT, 1)

            def up(g, c):
                n = NC * g + c
                after(pe, s_hid, n - 1 if swiglu else n - 3)
                if c == 0:
                    pe.wait_ge(s_hT, g + 1)
                if swiglu:
                    nc.tensor.matmul(u_ps[:, (2 * c) % 4, :], r.W("m1_0", c * C), hT[:, :],
                                     start=True, stop=True)
                    nc.tensor.matmul(u_ps[:, (2 * c + 1) % 4, :], r.W("m1_0", HID + c * C), hT[:, :],
                                     start=True, stop=True).then_inc(s_up, 1)
                else:
                    nc.tensor.matmul(u_ps[:, c, :], r.W(f"m1_{layer}", c * C), hT[:, :],
                                     start=True, stop=True).then_inc(s_up, 1)

            def down(g, c):
                if c == 0:
                    after(pe, s_pg, g)
                pe.wait_ge(s_hid, NC * g + c + 1)
                nc.tensor.matmul(y_ps[:, :], r.W(name, c * C), hid[:, c, :],
                                 start=(c == 0), stop=(c == NC - 1)).then_inc(s_down, 1)

            def body(g, first, work, nxt, nxt2):
                for c in range(NC):
                    if work:
                        up(g, c)
                        if c:
                            down(g, c - 1)
                    if c == 1 and not first:
                        after(pe, s_x, g - 1)
                        pe.wait_ge(s_pg, g)
                        for b in range(G):
                            last = nc.tensor.transpose(r_ps[:, b * C:(b + 1) * C], pg[:, b * T:(b + 1) * T],
                                                       r.ident[:, :])
                        last.then_inc(s_pgps, 1)
                if nxt:
                    transpose_xn(g + 1)
                if work:
                    down(g, NC - 1)

            iterations(pe, body, lambda: transpose_xn(0))


def evidence_phase(nc, r, st):
    K4 = G * S
    scale = float(C) ** -0.5
    with nc.cleanup_on_exit(), ExitStack() as ctx:
        tag = "evid_"

        def sb(name, shape):
            return ctx.enter_context(nc.sbuf_tensor(tag + name, shape, F32))

        def ps(name, shape):
            return ctx.enter_context(nc.psum_tensor(tag + name, shape, F32))

        def sem(name):
            return nc.alloc_semaphore(tag + name)

        stats, mv = sb("stats", [T, G, 6]), sb("mv", [T, G, 2])
        vareps, rstd = sb("vareps", [T, G]), sb("rstd", [T, G])
        xn = sb("xn", [T, G, C])
        ctxs = sb("ctxs", [C, K4])
        qT, kT, v = sb("qT", [C, GT]), sb("kT", [C, K4]), sb("v", [S, G, C])
        mx, dif, prob, pn = sb("mx", [T, G]), sb("dif", [T, K4]), sb("prob", [T, K4]), sb("pn", [T, K4])
        den, rden = sb("den", [T, G]), sb("rden", [T, G])
        pT = sb("pT", [S, GT])
        rl = sb("rl", [E, GT])
        rmx, rdif, rexp = sb("rmx", [T, G]), sb("rdif", [T, G * E]), sb("rexp", [T, G * E])
        rden2, rrd = sb("rden2", [T, G]), sb("rrd", [T, G])
        l_ps, s_ps, t_ps, e_ps = ps("l", [C, BANK]), ps("s", [T, BANK]), ps("t", [S, BANK]), ps("e", [C, BANK])
        rt_ps, rr_ps = ps("rt", [E, BANK]), ps("rr", [T, BANK])
        s_stats, s_mv, s_var, s_rstd, s_xn = sem("stats"), sem("mv"), sem("var"), sem("rstd"), sem("xn")
        s_xT, s_nx, s_kps, s_kT, s_qps, s_qT, s_vps, s_v = (sem(n) for n in ("xT", "nx", "kps", "kT", "qps", "qT", "vps", "v"))
        s_ctx, s_scores, s_max, s_dif, s_exp, s_den, s_rden, s_pn = (
            sem(n) for n in ("ctx", "scores", "max", "dif", "exp", "den", "rden", "pn"))
        s_tps, s_pT, s_eps, s_ev = sem("tps"), sem("pT"), sem("eps"), sem("ev")
        s_rtps, s_rl, s_rrps, s_rmax, s_rdif, s_rexp, s_rsum, s_rrd, s_probs = (
            sem(n) for n in ("rtps", "rl", "rrps", "rmax", "rdif", "rexp", "rsum", "rrd", "probs"))
        block = ctx.enter_context(nc.Block())

        def iterations(engine, body, prologue):
            prologue()
            body(0, False, True, True, True)
            body(1, True, True, True, True)
            with engine.Fori(2, NG - 2) as g:
                body(g, True, True, True, True)
            body(NG - 2, True, True, True, False)
            body(NG - 1, True, True, False, False)
            body(NG, True, False, False, False)

        def by_batch(ap, n):
            return ap.rearrange("p (b k) -> p b k", k=n)

        def spread(ap, n):
            return ap.rearrange("p (b a) -> p b a", a=1).broadcast_to([T, G, n])

        @block.sync
        def _(sp):
            def stage_context(g):
                after_alone(sp, s_vps, g)
                sp.dma_start(by_batch(ctxs[:, :], S), r.ctxT[:, bass.ds(G * g, G), :]).then_inc(s_ctx, 16)

            stage_context(0)
            with sp.Fori(1, NG) as g:
                stage_context(g)

        @block.gpsimd
        def _(pool):
            def rstd_of(g):
                pool.wait_ge(s_var, g + 1)
                nc.gpsimd.tensor_tensor(rstd[:, :], vareps[:, :], r.neg_half[:, :], ALU.pow).then_inc(s_rstd, 1)

            rstd_of(0)
            with pool.Fori(1, NG) as g:
                rstd_of(g)

        @block.vector
        def _(dve):
            def layer_norm(g):
                for b in range(G):
                    last = nc.vector.bn_stats(stats[:, b, :], r.x[:, bass.ds(G * g + b, 1), :])
                last.then_inc(s_stats, 1)
                after_alone(dve, s_stats, g + 1)
                for b in range(G):
                    last = nc.vector.bn_aggr(mv[:, b, :], stats[:, b, :])
                last.then_inc(s_mv, 1)
                dve.wait_ge(s_mv, g + 1)
                nc.vector.tensor_scalar(vareps[:, :], mv[:, :, 1], 1e-5, None, ALU.add).then_inc(s_var, 1)
                after(dve, s_xT, g)
                dve.wait_ge(s_rstd, g + 1)
                for b in range(G):
                    last = nc.vector.tensor_scalar(xn[:, b:b + 1, :], r.x[:, bass.ds(G * g + b, 1), :],
                                                   mv[:, b, 0:1], rstd[:, b:b + 1], ALU.subtract, ALU.mult)
                last.then_inc(s_xn, 1)

            def values_out(g):
                dve.wait_ge(s_vps, g + 1)
                nc.vector.tensor_copy(v[:, :, :], l_ps[0:S, :].rearrange("p (b c) -> p b c", b=G)
                                      ).then_inc(s_v, 1)

            def prologue():
                layer_norm(0)
                values_out(0)
                layer_norm(1)

            def body(i, router, work, nxt, nxt2):
                if work:
                    dve.wait_ge(s_scores, i + 1)
                    nc.vector.tensor_reduce(mx[:, :], by_batch(s_ps[:, 0:K4], S), AX.X, ALU.max).then_inc(s_max, 1)
                    dve.wait_ge(s_max, i + 1)
                    nc.vector.tensor_tensor(by_batch(dif[:, :], S), by_batch(s_ps[:, 0:K4], S),
                                            spread(mx[:, :], S), ALU.subtract).then_inc(s_dif, 1)
                if router:
                    dve.wait_ge(s_rrps, i)
                    nc.vector.tensor_reduce(rmx[:, :], by_batch(rr_ps[:, 0:G * E], E), AX.X, ALU.max).then_inc(s_rmax, 1)
                    dve.wait_ge(s_rmax, i)
                    nc.vector.tensor_tensor(by_batch(rdif[:, :], E), by_batch(rr_ps[:, 0:G * E], E),
                                            spread(rmx[:, :], E), ALU.subtract).then_inc(s_rdif, 1)
                if work:
                    dve.wait_ge(s_exp, i + 1)
                    nc.vector.tensor_reduce(den[:, :], by_batch(prob[:, :], S), AX.X, ALU.add).then_inc(s_den, 1)
                    dve.wait_ge(s_den, i + 1)
                    nc.vector.reciprocal(rden[:, :], den[:, :]).then_inc(s_rden, 1)
                    dve.wait_ge(s_rden, i + 1)
                    after(dve, s_tps, i)
                    nc.vector.tensor_tensor(by_batch(pn[:, :], S), by_batch(prob[:, :], S),
                                            spread(rden[:, :], S), ALU.mult).then_inc(s_pn, 1)
                if router:
                    dve.wait_ge(s_rexp, i)
                    nc.vector.tensor_reduce(rden2[:, :], by_batch(rexp[:, :], E), AX.X, ALU.add).then_inc(s_rsum, 1)
                    dve.wait_ge(s_rsum, i)
                    nc.vector.reciprocal(rrd[:, :], rden2[:, :]).then_inc(s_rrd, 1)
                    dve.wait_ge(s_rrd, i)
                    nc.vector.tensor_tensor(st.probs[:, bass.ds(G * i - G, G), :], by_batch(rexp[:, :], E),
                                            spread(rrd[:, :], E), ALU.mult).then_inc(s_probs, 1)
                if nxt:
                    values_out(i + 1)
                if nxt2:
                    layer_norm(i + 2)
                if work:
                    after(dve, s_rrps, i)
                    after_alone(dve, s_rtps, i + 1)
                    nc.vector.tensor_tensor(
                        by_batch(rl[:, :], T), by_batch(rt_ps[:, :], T),
                        r.anchor_rt[:, bass.ds(G * i, G)].rearrange("p (b a) -> p b a", a=1)
                        .broadcast_to([E, G, T]), ALU.add).then_inc(s_rl, 1)

            iterations(dve, body, prologue)

        @block.scalar
        def _(act):
            def prepare(g):
                after_alone(act, s_xT, g + 1)
                nc.scalar.activation(st.nx[:, bass.ds(G * g, G), :],
                                     l_ps[:, :].rearrange("p (b k) -> p b k", b=G), ACT.Identity,
                                     scale=r.bcol("gamma"), bias=r.bcol("beta")).then_inc(s_nx, 1)
                act.wait_ge(s_kps, g + 1)
                nc.scalar.copy(kT[:, :], l_ps[:, 0:K4]).then_inc(s_kT, 1)
                act.wait_ge(s_qps, g + 1)
                nc.scalar.copy(qT[:, :], l_ps[:, :]).then_inc(s_qT, 1)

            def body(i, router, work, nxt, nxt2):
                if work:
                    after(act, s_pn, i)
                    act.wait_ge(s_dif, i + 1)
                    nc.scalar.activation(prob[:, :], dif[:, :], ACT.Exp, scale=scale).then_inc(s_exp, 1)
                if router:
                    after(act, s_probs, i - 1)
                    act.wait_ge(s_rdif, i)
                    nc.scalar.activation(rexp[:, :], rdif[:, :], ACT.Exp).then_inc(s_rexp, 1)
                if nxt:
                    prepare(i + 1)
                if work:
                    act.wait_ge(s_tps, i + 1)
                    nc.scalar.copy(pT[:, :], t_ps[:, :]).then_inc(s_pT, 1)
                    after_alone(act, s_eps, i + 1)
                    nc.scalar.copy(st.ev[:, bass.ds(G * i, G), :],
                                   e_ps[:, :].rearrange("p (b k) -> p b k", b=G)).then_inc(s_ev, 1)

            iterations(act, body, lambda: prepare(0))

        @block.tensor
        def _(pe):
            def project(g):
                after(pe, s_v, g)
                pe.wait_ge(s_xn, g + 1)
                for b in range(G):
                    last = nc.tensor.transpose(l_ps[:, b * T:(b + 1) * T], xn[:, b, :], r.ident[:, :])
                last.then_inc(s_xT, 1)
                pe.wait_ge(s_ctx, 16 * g + 16)
                pe.wait_ge(s_nx, g + 1)
                nc.tensor.matmul(l_ps[:, 0:K4], r.W("k3"), ctxs[:, :], start=True, stop=True).then_inc(s_kps, 1)
                pe.wait_ge(s_kT, g + 1)
                nc.tensor.matmul(l_ps[:, :], r.W("q3"), st.nx[:, bass.ds(G * g, G), :],
                                 start=True, stop=True).then_inc(s_qps, 1)

            def project_values(g):
                pe.wait_ge(s_qT, g + 1)
                for b in range(G):
                    last = nc.tensor.matmul(l_ps[0:S, b * C:(b + 1) * C], ctxs[:, b * S:(b + 1) * S], r.W("v3"),
                                            start=True, stop=True)
                last.then_inc(s_vps, 1)

            def prologue():
                project(0)
                project_values(0)

            def body(i, router, work, nxt, nxt2):
                if work:
                    pe.wait_ge(s_qT, i + 1)
                    after(pe, s_dif, i)
                    for b in range(G):
                        last = nc.tensor.matmul(s_ps[:, b * S:(b + 1) * S], qT[:, b * T:(b + 1) * T],
                                                kT[:, b * S:(b + 1) * S], start=True, stop=True)
                    last.then_inc(s_scores, 1)
                if router:
                    pe.wait_ge(s_rl, i)
                    after_alone(pe, s_rdif, i - 1)
                    for b in range(G):
                        last = nc.tensor.transpose(rr_ps[:, b * E:(b + 1) * E], rl[:, b * T:(b + 1) * T],
                                                   r.ident[0:E, 0:E])
                    last.then_inc(s_rrps, 1)
                if nxt:
                    project(i + 1)
                if work:
                    after(pe, s_pT, i)
                    pe.wait_ge(s_pn, i + 1)
                    for b in range(G):
                        last = nc.tensor.transpose(t_ps[:, b * T:(b + 1) * T], pn[:, b * S:(b + 1) * S],
                                                   r.ident[:, :])
                    last.then_inc(s_tps, 1)
                    after(pe, s_ev, i)
                    pe.wait_ge(s_pT, i + 1)
                    pe.wait_ge(s_v, i + 1)
                    for b in range(G):
                        last = nc.tensor.matmul(e_ps[:, b * T:(b + 1) * T], v[:, b, :], pT[:, b * T:(b + 1) * T],
                                                start=True, stop=True)
                    last.then_inc(s_eps, 1)
                if nxt:
                    project_values(i + 1)
                if work:
                    after(pe, s_rl, i)
                    pe.wait_ge(s_ev, i + 1)
                    nc.tensor.matmul(rt_ps[:, :], r.W("rw", 0, E), st.nx[:, bass.ds(G * i, G), :],
                                     start=True, stop=False)
                    nc.tensor.matmul(rt_ps[:, :], r.W("rw", E, E), st.ev[:, bass.ds(G * i, G), :],
                                     start=False, stop=True).then_inc(s_rtps, 1)

            iterations(pe, body, prologue)


def expert_phase(nc, r, st, io):
    with nc.cleanup_on_exit(), ExitStack() as ctx:
        tag = "expert_"

        def sb(name, shape):
            return ctx.enter_context(nc.sbuf_tensor(tag + name, shape, F32))

        def ps(name, shape):
            return ctx.enter_context(nc.psum_tensor(tag + name, shape, F32))

        def sem(name):
            return nc.alloc_semaphore(tag + name)

        b2 = sb("b2", [T, E * C])
        g2h = sb("g2h", [C, 1])
        g1 = sb("g1", [C, GT])
        hid = sb("hid", [C, 2 * E, GT])
        th, gt = sb("th", [C, GT]), sb("gt", [C, 2, GT])
        eo, acc = sb("eo", [T, 2, E * C]), sb("acc", [T, 2, 2, C])
        routed, roT = sb("routed", [T, G, C]), sb("roT", [C, GT])
        delta = sb("delta", [C, GT])
        y = sb("y", [T, 2, G, C])
        u_ps, e_ps = ps("u", [C, 3, BANK]), ps("e", [T, 2, BANK])
        g_ps, l_ps, r_ps = ps("g", [C, BANK]), ps("l", [C, BANK]), ps("r", [T, BANK])
        s_b2, s_g2h = sem("b2"), sem("g2h")
        s_up, s_hid = sem("up"), sem("hid")
        s_eps, s_eo, s_acc, s_routed = sem("eps"), sem("eo"), sem("acc"), sem("routed")
        s_gps, s_th, s_gt = sem("gps"), sem("th"), sem("gt")
        s_rps, s_roT, s_ops, s_delta, s_dps, s_y = (sem(n) for n in ("rps", "roT", "ops", "delta", "dps", "y"))
        s_store = [sem("store0"), sem("store1")]
        NK = 1 + 2 * E
        block = ctx.enter_context(nc.Block())
        out_v = io["out"].rearrange("b t c -> t b c")

        def iterations(engine, body):
            body(0, 0, False, True)
            for i in range(1, 4):
                body(i, i % 2, True, True)
            with engine.Fori(2, NG // 2) as t:
                body(2 * t, 0, True, True)
                body(2 * t + 1, 1, True, True)
            body(NG, 0, True, False)

        @block.sync
        def _(sp):
            sp.dma_start(b2[:, :], io["e_b2"].rearrange("(a n) -> a n", a=1).broadcast_to([T, E * C])
                         ).then_inc(s_b2, 16)

            def store(g, p):
                after_alone(sp, s_y, g + 1)
                sp.dma_start(out_v[SHIFT:T, bass.ds(G * g, G), :], y[0:T - SHIFT, p]).then_inc(s_store[p], 16)
                sp.dma_start(out_v[0:SHIFT, bass.ds(G * g, G), :], y[T - SHIFT:T, p]).then_inc(s_store[p], 16)

            with sp.Fori(0, NG // 2) as t:
                store(2 * t, 0)
                store(2 * t + 1, 1)
            sp.wait_ge(s_b2, 16)
            sp.wait_ge(s_store[0], 16 * NG)
            sp.wait_ge(s_store[1], 16 * NG)

        @block.gpsimd
        def _(pool):
            nc.gpsimd.tensor_scalar(g2h[:, :], r.bcol("g2"), 0.5, None, ALU.mult).then_inc(s_g2h, 1)

            def gate(g, p):
                after(pool, s_delta, g - 1)
                after_alone(pool, s_th, g + 1)
                nc.gpsimd.tensor_scalar(gt[:, p, :], th[:, :], 0.5, 0.5, ALU.mult, ALU.add).then_inc(s_gt, 1)

            gate(0, 0)
            gate(1, 1)
            with pool.Fori(1, NG // 2) as t:
                gate(2 * t, 0)
                gate(2 * t + 1, 1)

        @block.vector
        def _(dve):
            dve.wait_ge(s_b2, 16)

            def body(i, par, finish, work):
                if finish:
                    dve.wait_ge(s_gt, i)
                    dve.wait_ge(s_ops, i)
                    nc.vector.scalar_tensor_tensor(delta[:, :], l_ps[:, :], r.bcol("ow"), gt[:, 1 - par, :],
                                                   ALU.add, ALU.mult).then_inc(s_delta, 1)
                    after(dve, s_store[1 - par], 16 * (i - 1 - (1 - par)))
                    dve.wait_ge(s_dps, i)
                    nc.vector.tensor_tensor(y[:, 1 - par], r_ps[:, :].rearrange("p (b c) -> p b c", b=G),
                                            r.x[:, bass.ds(G * i - G, G), :], ALU.add).then_inc(s_y, 1)
                if not work:
                    return
                for b in range(G):
                    m = G * i + b
                    dve.wait_ge(s_eps, m + 1)
                    nc.vector.tensor_tensor(eo[:, b % 2, :], e_ps[:, b % 2, 0:E * C], b2[:, :], ALU.add
                                            ).then_inc(s_eo, 1)
                    p = [st.probs[:, bass.ds(m, 1), e] for e in range(E)]
                    dve.wait_ge(s_eo, m + 1)
                    nc.vector.tensor_scalar(acc[:, b % 2, 0, :], eo[:, b % 2, 0:C], p[0], None, ALU.mult
                                            ).then_inc(s_acc, 1)
                    dve.wait_ge(s_acc, 2 * m + 1)
                    nc.vector.scalar_tensor_tensor(acc[:, b % 2, 1, :], eo[:, b % 2, C:2 * C], p[1],
                                                   acc[:, b % 2, 0, :], ALU.mult, ALU.add).then_inc(s_acc, 1)
                    if b == 0:
                        after(dve, s_rps, i)
                    dve.wait_ge(s_acc, 2 * m + 2)
                    nc.vector.scalar_tensor_tensor(routed[:, b, :], eo[:, b % 2, 2 * C:3 * C], p[2],
                                                   acc[:, b % 2, 1, :], ALU.mult, ALU.add).then_inc(s_routed, 1)

            iterations(dve, body)

        @block.scalar
        def _(act):
            act.wait_ge(s_g2h, 1)

            def body(i, par, finish, work):
                def hidden(k):
                    after_alone(act, s_up, NK * i + k + 1)
                    out = g1 if k == 0 else hid[:, k - 1]
                    for b in range(G):
                        last = nc.scalar.activation(
                            out[:, b * T:(b + 1) * T], u_ps[:, (k + par * NK) % 3, b * T:(b + 1) * T], ACT.Silu,
                            bias=r.anchor[:, 6 if k == 0 else k - 1, bass.ds(G * i + b, 1)])
                    last.then_inc(s_hid, 1)

                if work:
                    hidden(0)
                    hidden(1)
                if finish:
                    act.wait_ge(s_rps, i)
                    nc.scalar.copy(roT[:, :], l_ps[:, :]).then_inc(s_roT, 1)
                if work:
                    for k in range(2, NK):
                        hidden(k)
                    after(act, s_gt, i)
                    act.wait_ge(s_gps, i + 1)
                    nc.scalar.activation(th[:, :], g_ps[:, :], ACT.Tanh, scale=0.5, bias=g2h[:, 0:1]
                                         ).then_inc(s_th, 1)

            iterations(act, body)

        @block.tensor
        def _(pe):
            def body(i, par, finish, work):
                def up(k):
                    n = NK * i + k
                    after(pe, s_hid, n - 1 if par == 0 and k < 2 else n - 2)
                    w = ("g1", 0, C) if k == 0 else ("e1", ((k - 1) // 2) * 3 * RH + (k - 1) % 2 * C, RH)
                    bank = u_ps[:, (k + par * NK) % 3, :]
                    nc.tensor.matmul(bank, r.W(w[0], w[1]), st.nx[:, bass.ds(G * i, G), :],
                                     start=True, stop=False)
                    nc.tensor.matmul(bank, r.W(w[0], w[1] + w[2]), st.ev[:, bass.ds(G * i, G), :],
                                     start=False, stop=True).then_inc(s_up, 1)

                if work:
                    up(0)
                    up(1)
                if finish:
                    pe.wait_ge(s_routed, G * i)
                    after(pe, s_delta, i - 1)
                    for b in range(G):
                        last = nc.tensor.transpose(l_ps[:, b * T:(b + 1) * T], routed[:, b, :], r.ident[:, :])
                    last.then_inc(s_rps, 1)
                if work:
                    up(2)
                    after(pe, s_th, i)
                    pe.wait_ge(s_hid, NK * i + 1)
                    nc.tensor.matmul(g_ps[:, :], r.W("g2"), g1[:, :], start=True, stop=True).then_inc(s_gps, 1)
                if finish:
                    pe.wait_ge(s_roT, i)
                    nc.tensor.matmul(l_ps[:, :], r.W("ow"), roT[:, :], start=True, stop=True).then_inc(s_ops, 1)
                if work:
                    up(3)
                    up(4)
                if finish:
                    after(pe, s_y, i - 1)
                    pe.wait_ge(s_delta, i)
                    for b in range(G):
                        last = nc.tensor.transpose(r_ps[:, b * C:(b + 1) * C], delta[:, b * T:(b + 1) * T],
                                                   r.ident[:, :])
                    last.then_inc(s_dps, 1)
                if work:
                    up(5)
                    up(6)
                    for b in range(G):
                        m = G * i + b
                        after(pe, s_eo, m - 1)
                        if b == 0:
                            pe.wait_ge(s_hid, NK * i + NK)
                        for e in range(E):
                            for c in range(2):
                                last = nc.tensor.matmul(e_ps[:, b % 2, e * C:(e + 1) * C],
                                                        hid[:, 2 * e + c, b * T:(b + 1) * T],
                                                        r.W("e2", (2 * e + c) * C), start=(c == 0), stop=(c == 1))
                        last.then_inc(s_eps, 1)

            iterations(pe, body)


def build(nc, io):
    with ExitStack() as ctx:
        r = resident(nc, ctx)
        with ExitStack() as first:
            r.ctxnT = first.enter_context(nc.sbuf_tensor("ctxnT", [C, B, S], F32))
            r.kbd = first.enter_context(nc.sbuf_tensor("kbd", [C, H, GT], F32))
            setup_phase(nc, r, io)
            for layer in range(3):
                attention_phase(nc, r, layer, "window" if layer == 0 else "self")
                attention_phase(nc, r, layer, "topk" if layer == 0 else "cross")
                mlp_phase(nc, r, layer)
        st = Resident()
        st.nx = ctx.enter_context(nc.sbuf_tensor("nx", [C, B, T], F32))
        st.ev = ctx.enter_context(nc.sbuf_tensor("ev", [C, B, T], F32))
        st.probs = ctx.enter_context(nc.sbuf_tensor("probs", [T, B, E], F32))
        evidence_phase(nc, r, st)
        expert_phase(nc, r, st, io)


def packed(inputs):
    import numpy as np

    def a(name):
        return np.asarray(inputs[name])

    def rows(w):
        n = w.shape[0] // C
        return w.reshape(n, C, w.shape[1]).transpose(1, 0, 2).reshape(C, n * w.shape[1])

    def columns(*vectors):
        return np.concatenate([v.reshape(-1, C) for v in vectors]).T

    L0, L1, L2, L3 = "L0_xcond_", "L1_xcond_", "L2_xcond_", "L3_xcond_"
    e_w1, e_w2 = a(L3 + "e_w1"), a(L3 + "e_w2")
    matrices = {
        "qkv0": a(L0 + "w_qkv"), "so0": a(L0 + "w_so"), "q0": a(L0 + "w_q"), "kv0": a(L0 + "w_kv"),
        "co0": a(L0 + "w_co"), "m1_0": a(L0 + "w_m1"), "m2_0": rows(a(L0 + "w_m2")),
        "qkv1": a(L1 + "W_qkv"), "so1": a(L1 + "W_proj"), "q1": a(L1 + "W_qc"), "kv1": a(L1 + "W_kvc"),
        "co1": a(L1 + "W_cproj"), "m1_1": a(L1 + "W_mlp1"), "m2_1": rows(a(L1 + "W_mlp2")),
        "qkv2": a(L2 + "qkv_w"), "so2": a(L2 + "sa_proj_w"), "q2": a(L2 + "q_w"), "kv2": a(L2 + "kv_w"),
        "co2": a(L2 + "ca_proj_w"), "m1_2": a(L2 + "fc1_w"), "m2_2": rows(a(L2 + "fc2_w")),
        "q3": a(L3 + "Wq"), "k3": a(L3 + "Wk"), "v3": a(L3 + "Wv"), "rw": rows(a(L3 + "router_W")),
        "e1": np.concatenate([rows(w) for w in e_w1], axis=1),
        "e2": np.concatenate([rows(w) for w in e_w2], axis=1),
        "g1": rows(a(L3 + "gate_w1")), "g2": a(L3 + "gate_w2"), "ow": a(L3 + "out_w"),
    }
    vectors = {
        "mod": columns(a(L0 + "b_ada"), a(L1 + "b_mod"), a(L2 + "adaln_b")),
        "qkv0": columns(a(L0 + "b_qkv")), "so0": columns(a(L0 + "b_so")), "q0": columns(a(L0 + "b_q")),
        "kv0": columns(a(L0 + "b_kv")), "co0": columns(a(L0 + "b_co")), "m1_0": columns(a(L0 + "b_m1")),
        "m2_0": columns(a(L0 + "b_m2")),
        "qkv1": columns(a(L1 + "b_qkv")), "so1": columns(a(L1 + "b_proj")), "q1": columns(a(L1 + "b_qc")),
        "kv1": columns(a(L1 + "b_kvc")), "co1": columns(a(L1 + "b_cproj")), "m1_1": columns(a(L1 + "b_mlp1")),
        "m2_1": columns(a(L1 + "b_mlp2")),
        "qkv2": columns(a(L2 + "qkv_b")), "so2": columns(a(L2 + "sa_proj_b")), "q2": columns(a(L2 + "q_b")),
        "kv2": columns(a(L2 + "kv_b")), "co2": columns(a(L2 + "ca_proj_b")), "m1_2": columns(a(L2 + "fc1_b")),
        "m2_2": columns(a(L2 + "fc2_b")),
        "gamma": columns(a(L3 + "ln_gamma")), "beta": columns(a(L3 + "ln_beta")),
        "e1": columns(a(L3 + "e_b1").reshape(-1)), "g1": columns(a(L3 + "gate_b1")),
        "g2": columns(a(L3 + "gate_b2")), "ow": columns(a(L3 + "out_b")),
    }
    assert all(matrices[n].shape == (C, w) for n, w in W_WIDTH.items())
    assert all(vectors[n].shape == (C, w) for n, w in B_WIDTH.items())
    return {
        "x": a("x"), "cond": a("cond_1024"), "ctx": a("ctx_1024"),
        "weights": np.concatenate([matrices[n] for n in W_WIDTH], axis=1),
        "wmod": np.concatenate([a(L0 + "w_ada"), a(L1 + "W_mod"), a(L2 + "adaln_w")], axis=1),
        "bias": np.concatenate([vectors[n] for n in B_WIDTH], axis=1),
        "router_b": a(L3 + "router_b"), "e_b2": a(L3 + "e_b2").reshape(-1),
    }


def kernel(**inputs):
    import numpy as np
    import concourse.bacc as bacc
    from concourse.bass_utils import run_bass_kernel_spmd

    nc = bacc.Bacc("TRN2", target_bir_lowering=False, num_devices=1)
    arrays = {f"in_{k}": np.ascontiguousarray(v) for k, v in packed(inputs).items()}
    io = {k[3:]: nc.dram_tensor(k, v.shape, mybir.dt.from_np(v.dtype), kind="ExternalInput").ap()
          for k, v in arrays.items()}
    io["out"] = nc.dram_tensor("out_x", (B, T, C), F32, kind="ExternalOutput").ap()
    build(nc, io)
    return run_bass_kernel_spmd(nc, [arrays], core_ids=[0]).results[0]["out_x"]
```

```python
from contextlib import ExitStack

import concourse.bass as bass
from concourse import mybir

F32 = mybir.dt.float32
F32R = mybir.dt.float32r
ALU = mybir.AluOpType
ACT = mybir.ActivationFunctionType
AX = mybir.AxisListType

B, T, C = 64, 128, 128
S = 77
H, D = 16, 8
WIN, SHIFT = 64, 32
HID = 512
G = 4
NG = B // G
GT = G * T
TOPK = 16
E = 3
RH = 2 * C
NEG = -3.0e38
SCALE = float(D) ** -0.5
BANK = 512

W_WIDTH = {
    "qkv0": 3 * C, "so0": C, "q0": C, "kv0": 2 * C, "co0": C, "m1_0": 2 * HID, "m2_0": 4 * C,
    "qkv1": 3 * C, "so1": C, "q1": C, "kv1": 2 * C, "co1": C, "m1_1": HID, "m2_1": 4 * C,
    "qkv2": 3 * C, "so2": C, "q2": C, "kv2": 2 * C, "co2": C, "m1_2": HID, "m2_2": 4 * C,
    "q3": C, "k3": C, "v3": C, "rw": 3 * E,
}
W_AT = {}
for _n, _w in W_WIDTH.items():
    W_AT[_n] = sum(W_WIDTH[k] for k in W_AT)
W3_WIDTH = {"e1": E * 3 * RH, "e2": E * 2 * C, "g1": 3 * C, "g2": C, "ow": C}
for _n, _w in W3_WIDTH.items():
    W_AT[_n] = sum(W3_WIDTH[k] for k in W_AT if k in W3_WIDTH)
B_WIDTH = {
    "mod": 21, "qkv0": 3, "so0": 1, "q0": 1, "kv0": 2, "co0": 1, "m1_0": 8, "m2_0": 1,
    "qkv1": 3, "so1": 1, "q1": 1, "kv1": 2, "co1": 1, "m1_1": 4, "m2_1": 1,
    "qkv2": 3, "so2": 1, "q2": 1, "kv2": 2, "co2": 1, "m1_2": 4, "m2_2": 1,
    "gamma": 1, "beta": 1, "e1": 6, "g1": 1, "g2": 1, "ow": 1,
}
B_AT = {}
for _n, _w in B_WIDTH.items():
    B_AT[_n] = sum(B_WIDTH[k] for k in B_AT)
B_COLS = sum(B_WIDTH.values())
SH_A = [0, 9, 15]
SC_A, G_A = [1, 10, 16], [2, 11, 17]
SH_C0, SC_C0, G_C0 = 3, 4, 5
SH_M, SC_M, G_M = [6, 12, 18], [7, 13, 19], [8, 14, 20]
GATED = [("so0", 2), ("co0", 5), ("m2_0", 8), ("so1", 11), ("m2_1", 14), ("so2", 17), ("m2_2", 20)]


def after(engine, sem, value):
    if isinstance(value, int) and value <= 0:
        return
    assert isinstance(value, int) or value.min_val > 0
    engine.wait_ge(sem, value)


def after_alone(engine, sem, value):
    after(engine, sem, value)
    if not isinstance(value, int):
        engine.nop(nofuse=True)


class Resident:
    pass


def resident(nc, ctx):
    r = Resident()

    def sb(name, shape):
        return ctx.enter_context(nc.sbuf_tensor(name, shape, F32))

    r.x = sb("x_res", [T, B, C])
    r.ctxT = sb("ctxT", [C, B, S])
    r.w = sb("weights", [C, sum(W_WIDTH.values())])
    r.bias = sb("bias_cols", [C, B_COLS])
    r.mod = sb("mod", [C, 21, B])
    r.gb = sb("gate_bias", [C, len(GATED), B])
    r.condT = sb("condT", [C, B])
    r.anchor_rt = sb("anchor_rt", [E, B])
    r.ident = sb("ident", [C, C])
    r.neg_half = sb("neg_half", [T, G])

    def W(name, c0=0, n=C):
        w = r.w3 if name in W3_WIDTH else r.w
        return w[:, W_AT[name] + c0:W_AT[name] + c0 + n]

    def bcol(name, k=0):
        return r.bias[:, B_AT[name] + k:B_AT[name] + k + 1]

    r.W, r.bcol = W, bcol
    return r


def setup_phase(nc, r, io):
    with nc.cleanup_on_exit(), ExitStack() as ctx:
        def sb(name, shape):
            return ctx.enter_context(nc.sbuf_tensor(name, shape, F32))

        def sem(name):
            return nc.alloc_semaphore(name)

        P = 4
        wmod = sb("wmod", [C, 21 * C])
        cond = sb("cond", [B, C])
        siluT = sb("siluT", [C, B])
        ctx_in = sb("ctx_in", [S, P, G, C])
        ctx_n = sb("ctx_n", [S, P, G, C])
        stats = sb("stats", [S, P, G, 6])
        mv = sb("mv", [S, P, G, 2])
        vareps = sb("vareps", [S, P, G])
        rstd = sb("rstd", [S, P, G])
        rb = sb("rb", [E, 1])
        modps = ctx.enter_context(nc.psum_tensor("modps", [C, 4, BANK], F32))
        cps = ctx.enter_context(nc.psum_tensor("cps", [C, 2, BANK], F32))
        nps = ctx.enter_context(nc.psum_tensor("nps", [C, 2, BANK], F32))
        wmod_in = sem("wmod_in")
        x_in, w_in, bias_in, cond_in, misc_in = (sem(n) for n in ("x_in", "w_in", "bias_in", "cond_in", "misc_in"))
        ctx_ready = [sem(f"ctx_ready{p}") for p in range(P)]
        ident_ready, const_ready, kbd_ready = sem("ident_ready"), sem("const_ready"), sem("kbd_ready")
        cond_t, cond_c, silu_c = sem("cond_t"), sem("cond_c"), sem("silu_c")
        mod_ps, mod_done, gb_done = sem("mod_ps"), sem("mod_done"), sem("gb_done")
        raw_ps, raw_out, nrm_ps, nrm_out = sem("raw_ps"), sem("raw_out"), sem("nrm_ps"), sem("nrm_out")
        st_done, mv_done, ve_done, rstd_done, xn_done = (sem(n) for n in ("st_done", "mv_done", "ve_done", "rstd_done", "xn_done"))
        block = ctx.enter_context(nc.Block())
        ctx_v = io["ctx"].rearrange("b s c -> s b c")
        x_v = io["x"].rearrange("b t c -> t b c")
        NA = 16

        @block.sync
        def _(sp):
            sp.dma_start(cond[:, :], io["cond"]).then_inc(cond_in, 16)
            sp.dma_start(r.bias[:, :], io["bias"]).then_inc(bias_in, 16)
            sp.dma_start(rb[:, :], io["router_b"].rearrange("(e a) -> e a", a=1)).then_inc(misc_in, 16)
            for g in range(P):
                sp.dma_start(ctx_in[:, g], ctx_v[:, G * g:G * g + G, :]).then_inc(ctx_ready[g], 16)
            with sp.Fori(0, NG // P - 1) as t:
                for p in range(P):
                    after_alone(sp, raw_ps, P * t + (p + 1))
                    after_alone(sp, xn_done, P * t + (p + 1))
                    sp.dma_start(ctx_in[:, p], ctx_v[:, bass.ds(G * P * t + (G * P + G * p), G), :]
                                 ).then_inc(ctx_ready[p], 16)
            sp.wait_ge(x_in, 32 * (B // NA))

        @block.gpsimd
        def _(pool):
            nc.gpsimd.memset(r.ident[:, :], 0.0).then_inc(const_ready, 1)
            nc.gpsimd.memset(r.neg_half[:, :], -0.5).then_inc(const_ready, 1)
            pool.wait_ge(const_ready, 2)
            nc.gpsimd.affine_select(out=r.ident[:, :], in_=r.ident[:, :], compare_op=ALU.not_equal,
                                    fill=1.0, base=0, pattern=[[-1, C]], channel_multiplier=1
                                    ).then_inc(ident_ready, 1)
            with pool.Fori(0, NG // P) as t:
                for p in range(P):
                    pool.wait_ge(ve_done, P * t + (p + 1))
                    nc.gpsimd.tensor_tensor(rstd[:, p], vareps[:, p], r.neg_half[0:S, :],
                                            ALU.pow).then_inc(rstd_done, 1)

        @block.scalar
        def _(act):
            act.dma_start(wmod[:, :], io["wmod"]).then_inc(wmod_in, 16)
            act.dma_start(r.w[:, :], io["weights"]).then_inc(w_in, 16)
            for k in range(B // NA):
                act.dma_start(r.x[0:T - SHIFT, NA * k:NA * k + NA, :],
                              x_v[SHIFT:T, NA * k:NA * k + NA, :]).then_inc(x_in, 16)
                act.dma_start(r.x[T - SHIFT:T, NA * k:NA * k + NA, :],
                              x_v[0:SHIFT, NA * k:NA * k + NA, :]).then_inc(x_in, 16)
            act.wait_ge(cond_t, 1)
            nc.scalar.copy(r.condT[:, :], modps[:, 3, 0:B]).then_inc(cond_c, 1)
            nc.scalar.activation(siluT[:, :], modps[:, 3, 0:B], ACT.Silu).then_inc(silu_c, 1)
            with act.Fori(0, NG // P) as t:
                for p in range(P):
                    after_alone(act, raw_ps, P * t + (p + 1))
                    nc.scalar.copy(r.ctxT[:, bass.ds(G * P * t + G * p, G), :],
                                   cps[:, p % 2, 0:G * S].rearrange("c (b s) -> c b s", s=S)).then_inc(raw_out, 1)
                    after_alone(act, nrm_ps, P * t + (p + 1))
                    nc.scalar.copy(r.ctxnT[:, bass.ds(G * P * t + G * p, G), :],
                                   nps[:, p % 2, 0:G * S].rearrange("c (b s) -> c b s", s=S)).then_inc(nrm_out, 1)

        @block.vector
        def _(dve):
            nc.vector.memset(r.kbd[:, :, :], 0.0).then_inc(kbd_ready, 1)
            def normalise_context(t):
                for p in range(P):
                    dve.wait_ge(ctx_ready[p], 16 * t + 16)
                    for b in range(G):
                        last = nc.vector.bn_stats(stats[:, p, b, :], ctx_in[:, p, b, :])
                    last.then_inc(st_done, 1)
                    after_alone(dve, st_done, P * t + (p + 1))
                    for b in range(G):
                        last = nc.vector.bn_aggr(mv[:, p, b, :], stats[:, p, b, :])
                    last.then_inc(mv_done, 1)
                    dve.wait_ge(mv_done, P * t + (p + 1))
                    nc.vector.tensor_scalar(vareps[:, p], mv[:, p, :, 1], 1e-6, None, ALU.add
                                            ).then_inc(ve_done, 1)
                for p in range(P):
                    dve.wait_ge(rstd_done, P * t + (p + 1))
                    after(dve, nrm_ps, P * t + p - (P - 1))
                    for b in range(G):
                        last = nc.vector.tensor_scalar(ctx_n[:, p, b, :], ctx_in[:, p, b, :],
                                                       mv[:, p, b, 0:1], rstd[:, p, b:b + 1],
                                                       ALU.subtract, ALU.mult)
                    last.then_inc(xn_done, 1)

            normalise_context(0)
            with dve.Fori(1, NG // P) as t:
                normalise_context(t)

            dve.wait_ge(bias_in, 16)
            dve.wait_ge(mod_ps, 1)
            for k in range(21):
                plus = 1.0 if k in SC_A + [SC_C0] + SC_M else 0.0
                last = nc.vector.tensor_scalar(r.mod[:, k, :], modps[:, k // 8, (k % 8) * B:(k % 8 + 1) * B],
                                               r.bcol("mod", k), plus, ALU.add, ALU.add)
            last.then_inc(mod_done, 1)
            dve.wait_ge(mod_done, 1)
            for n, (name, k) in enumerate(GATED):
                nc.vector.tensor_scalar(r.gb[:, n, :], r.mod[:, k, :], r.bcol(name), None,
                                        ALU.mult).then_inc(gb_done, 1)
            dve.wait_ge(mod_ps, 2)
            dve.wait_ge(misc_in, 16)
            nc.vector.tensor_scalar(r.anchor_rt[:, :], modps[0:E, 3, 7 * B:8 * B], rb[:, 0:1],
                                           None, ALU.add).then_inc(gb_done, 1)

        @block.tensor
        def _(pe):
            pe.wait_ge(ident_ready, 1)
            pe.wait_ge(cond_in, 16)
            nc.tensor.transpose(modps[:, 3, 0:B], cond[:, :], r.ident[0:B, 0:B]).then_inc(cond_t, 1)
            pe.wait_ge(silu_c, 1)
            def transpose_context(t):
                for p in range(P):
                    pe.wait_ge(ctx_ready[p], 16 * t + 16)
                    after(pe, raw_out, P * t + p - 1)
                    for b in range(G):
                        last = nc.tensor.transpose(cps[:, p % 2, b * S:(b + 1) * S], ctx_in[:, p, b, :],
                                                   r.ident[0:S, 0:S])
                    last.then_inc(raw_ps, 1)
                    pe.wait_ge(xn_done, P * t + (p + 1))
                    after(pe, nrm_out, P * t + p - 1)
                    for b in range(G):
                        last = nc.tensor.transpose(nps[:, p % 2, b * S:(b + 1) * S], ctx_n[:, p, b, :],
                                                   r.ident[0:S, 0:S])
                    last.then_inc(nrm_ps, 1)

            transpose_context(0)
            with pe.Fori(1, NG // P) as t:
                transpose_context(t)

            pe.wait_ge(wmod_in, 16)
            for k in range(21):
                last = nc.tensor.matmul(modps[:, k // 8, (k % 8) * B:(k % 8 + 1) * B],
                                        wmod[:, k * C:(k + 1) * C], siluT[:, :], start=True, stop=True)
            last.then_inc(mod_ps, 1)
            pe.wait_ge(w_in, 16)
            nc.tensor.matmul(modps[0:E, 3, 7 * B:8 * B], r.W("rw", 2 * E, E), r.condT[:, :],
                             start=True, stop=True).then_inc(mod_ps, 1)


def product3(nc, out, w, x, start=True, stop=True):
    nc.tensor.matmul(out, w[1], x[0], start=start, stop=False)
    nc.tensor.matmul(out, w[0], x[1], start=False, stop=False)
    return nc.tensor.matmul(out, w[0], x[0], start=False, stop=stop)


def attention_phase(nc, r, layer, kind):
    window, cross, topk = kind == "window", kind in ("cross", "topk"), kind == "topk"
    split = layer > 0
    keys = S if cross else T
    KW = keys + keys % 2 if split else keys
    NU = 2 if window else 4
    NS = G * NU
    HU = H // NU
    cols = HU * WIN if window else HU * keys
    rows = T if window else keys
    VM = 18 if window else 9
    XT, KP, QP, VP, ONT, PROJ, PGT = (0, 1, 2, 3, 5, 6, 7) if window else (0, 3, 5, 7, 9, 11, 14)
    STATS, AGGR, APPLY = ((2, 2, 3, 3), 4, (6, 6, 7, 7)) if window else ((1, 2, 3, 5), 6, (9, 10, 11, 15))
    LE = 1 if split else 0
    LT = 3 if topk or split else 2
    LV, LO = LT + 1, LT + 2
    name_o = f"{'co' if cross else 'so'}{layer}"
    gate = dict(GATED).get(name_o)
    n_gb = [n for n, _ in GATED].index(name_o) if gate is not None else None
    if kind == "topk":
        scale_at, shift_at = SC_C0, SH_C0
    elif cross:
        scale_at = shift_at = None
    else:
        scale_at, shift_at = SC_A[layer], SH_A[layer]
    wq = r.W(f"q{layer}") if cross else r.W(f"qkv{layer}", 0)
    wk = r.W(f"kv{layer}", 0) if cross else r.W(f"qkv{layer}", C)
    wv = r.W(f"kv{layer}", C) if cross else r.W(f"qkv{layer}", 2 * C)
    bq = r.bcol(f"q{layer}") if cross else r.bcol(f"qkv{layer}", 0)
    bk = r.bcol(f"kv{layer}", 0) if cross else r.bcol(f"qkv{layer}", 1)
    bv = r.bcol(f"kv{layer}", 1) if cross else r.bcol(f"qkv{layer}", 2)
    source = r.ctxnT if layer == 1 else r.ctxT

    with nc.cleanup_on_exit(), ExitStack() as ctx:
        tag = f"{kind}{layer}_"

        def sb(name, shape, dtype=F32):
            return ctx.enter_context(nc.sbuf_tensor(tag + name, shape, dtype))

        def ps(name, shape):
            return ctx.enter_context(nc.psum_tensor(tag + name, shape, F32))

        def sem(name):
            return nc.alloc_semaphore(tag + name)

        stats, mv = sb("stats", [T, G, 6]), sb("mv", [T, G, 2])
        vareps, rstd = sb("vareps", [T, G]), sb("rstd", [T, G])
        xn = sb("xn", [T, G, C])
        hT = sb("hT", [C, GT])
        ctxs = sb("ctxs", [C, G * KW]) if cross else None
        if split:
            qT, kT = sb("qT", [C, 2, GT], F32R), sb("kT", [C, 2, G * KW], F32R)
        else:
            qT, kT = sb("qT", [C, 2, GT]), sb("kT", [C, 2, G * keys])
        vp = sb("vp", [T, 2, G, 2, 8, VM]) if window else sb("vp", [T, 2, G, H, VM])
        top = sb("top", [T, 2, HU, 8]) if topk else None
        top2 = sb("top2", [T, 2, HU, 8]) if topk else None
        work = sb("work", [T, 4, cols]) if topk else None
        mask = sb("mask", [T, 2, cols]) if topk else None
        mx = sb("mx", [T, 2, HU])
        nmx = sb("nmx", [T, 2, HU]) if topk else None
        prob = sb("prob", [T, 4, cols])
        pT = sb("pT", [T, 2, BANK])
        oT = sb("oT", [T, 2, NU * T])
        rden = sb("rden", [T, 2, H])
        on = sb("on", [T, G, C])
        onT = sb("onT", [C, GT])
        pg = onT
        s_ps = ps("s", [T, 2, BANK])
        t_ps = ps("t", [T, 2, BANK])
        o_ps = ps("o", [T, 2, BANK])
        l_ps = ps("l", [T, BANK])
        r_ps = ps("r", [T, BANK])

        s_scores, s_max, s_dif, s_exp = sem("scores"), sem("max"), sem("dif"), sem("exp")
        s_probT, s_pT, s_pv = sem("probT"), sem("pT"), sem("pv")
        s_picked = sem("picked")
        s_top, s_cut, s_top2, s_cut2 = sem("top"), sem("cut"), sem("top2"), sem("cut2")
        s_mask = sem("mask")
        s_oT, s_otr, s_rden, s_norm = sem("oT"), sem("otr"), sem("rden"), sem("norm")
        s_stats, s_mv, s_var, s_rstd, s_xn = sem("stats"), sem("mv"), sem("var"), sem("rstd"), sem("xn")
        s_xT, s_hT, s_kps, s_kT, s_qps, s_qT = sem("xT"), sem("hT"), sem("kps"), sem("kT"), sem("qps"), sem("qT")
        s_vps, s_v = sem("vps"), sem("v")
        s_quarter = [sem(f"quarter{q}") for q in range(4)]
        s_half1 = sem("half1")
        s_klo, s_qlo = sem("klo"), sem("qlo")
        s_ctx = sem("ctx")
        s_onps, s_onT, s_pjps, s_pg, s_pgps, s_x = sem("onps"), sem("onT"), sem("pjps"), sem("pg"), sem("pgps"), sem("x")
        s_init, s_zero = sem("init"), sem("zero")
        n_init = 3 if window or KW > keys else 2
        NV = 2 if window else 1
        QB = 16 * (H // 4 + 1 if split else H // 4)
        HB = 16 * (4 if split else H)
        block = ctx.enter_context(nc.Block())

        def iterations(engine, body, prologue):
            prologue()
            body(0, 0, True, True, True, True)
            body(1, 1, False, True, True, True)
            with engine.Fori(1, NG // 2 - 1) as t:
                body(2 * t, 0, False, True, True, True)
                body(2 * t + 1, 1, False, True, True, True)
            body(NG - 2, 0, False, True, True, False)
            body(NG - 1, 1, False, True, False, False)
            body(NG, 0, False, False, False, False)

        def lagged(u, lag, first, units):
            c = u - lag
            return c if (units if c >= 0 else not first) else None

        def sequence_hooks(u, first, units):
            c = lagged(u, NU + LO, first, units)
            return c // NU if c is not None and c % NU == 0 else None

        @block.sync
        def _(sp):
            def stage_context(g):
                after_alone(sp, s_vps, g)
                sp.dma_start(ctxs[:, :].rearrange("c (b s) -> c b s", s=KW)[:, :, 0:S],
                             source[:, bass.ds(G * g, G), :]).then_inc(s_ctx, 16)

            def spread_keys(g, half, par, scores_done):
                after_alone(sp, s_kT, g + 1)
                after_alone(sp, s_scores, scores_done)
                c0, n = half * 2 * keys, 2 * keys
                for h in range(H):
                    sp.dma_start(r.kbd[D * h:D * h + D, h, c0:c0 + n],
                                 kT[D * h:D * h + D, par, c0:c0 + n]
                                 ).then_inc(s_half1 if half else s_quarter[h // 4], 16)

            def spread_split_keys(g, par, q, scores_done):
                after_alone(sp, s_klo, g + 1)
                after_alone(sp, s_scores, scores_done)
                for h in range(4 * q, 4 * q + 4):
                    sp.dma_start(r.kbd[D * h:D * h + D, par, h % 4, :, 0:G * KW].bitcast(F32),
                                 kT[D * h:D * h + D, :, :].bitcast(F32)).then_inc(s_quarter[q], 16)

            def spread_split_queries(g, half, q, scores_done):
                after_alone(sp, s_qlo, g + 1)
                after_alone(sp, s_scores, scores_done)
                c0, n = half * 2 * T, 2 * T
                sp.dma_start(r.qz[32 * q:32 * q + 32, q, :, c0:c0 + n].bitcast(F32),
                             qT[32 * q:32 * q + 32, :, c0:c0 + n].bitcast(F32)
                             ).then_inc(s_half1 if half else s_quarter[q], 16)

            def prologue():
                if cross:
                    stage_context(0)
                if split:
                    for q in range(4):
                        spread_split_keys(0, 0, q, 0)
                    for half in range(2):
                        for q in range(4):
                            spread_split_queries(0, half, q, 0)
                else:
                    spread_keys(0, 0, 0, 0)
                    spread_keys(0, 1, 0, 0)
                if cross:
                    stage_context(1)

            def body(i, par, first, units, pre, ln):
                if not pre:
                    return
                if split:
                    for q in range(4):
                        spread_split_keys(i + 1, 1 - par, q, NS * i)
                    if cross and ln:
                        stage_context(i + 2)
                    for half in range(2):
                        for q in range(4):
                            spread_split_queries(i + 1, half, q, NS * i + (NS // 2) * (half + 1))
                    return
                spread_keys(i + 1, 0, 1 - par, NS * i + NS // 2)
                if cross and ln:
                    stage_context(i + 2)
                spread_keys(i + 1, 1, 1 - par, NS * i + NS)

            iterations(sp, body, prologue)

        @block.gpsimd
        def _(pool):
            nc.gpsimd.memset(vp[:, :], 0.0).then_inc(s_init, 1)
            pool.wait_ge(s_init, 1)
            if window:
                nc.gpsimd.memset(vp[0:WIN, :, :, :, :, D:D + 1], 1.0).then_inc(s_init, 1)
                nc.gpsimd.memset(vp[WIN:T, :, :, :, :, 2 * D + 1:2 * D + 2], 1.0).then_inc(s_init, 1)
                pool.wait_ge(s_init, 3)
            else:
                nc.gpsimd.memset(vp[:, :, :, :, D:D + 1], 1.0).then_inc(s_init, 1)
                if KW > keys:
                    nc.gpsimd.memset(ctxs[:, :].rearrange("c (b s) -> c b s", s=KW)[:, :, S:KW], 0.0
                                     ).then_inc(s_init, 1)
                pool.wait_ge(s_init, n_init)

            def rstd_of(g):
                pool.wait_ge(s_var, g + 1)
                nc.gpsimd.tensor_tensor(rstd[:, :], vareps[:, :], r.neg_half[:, :], ALU.pow).then_inc(s_rstd, 1)

            def scale_maximum(i, u):
                n = NS * i + u
                after(pool, s_exp, n - 1)
                after_alone(pool, s_top, n + 1)
                nc.gpsimd.tensor_scalar(nmx[:, u % 2, :], top[:, u % 2, :, 0], -SCALE, None, ALU.mult
                                        ).then_inc(s_dif, 1)

            def pick(i, u):
                n = NS * i + u
                after_alone(pool, s_cut2, n + 1)
                nc.gpsimd.tensor_scalar(mask[:, u % 2, :], work[:, u % 4, :], NEG / 2, None, ALU.is_le
                                        ).then_inc(s_mask, 1)
                pool.wait_ge(s_mask, n + 1)
                pool.wait_ge(s_exp, n + 1)
                nc.gpsimd.tensor_tensor(prob[:, u % 4, :], prob[:, u % 4, :], mask[:, u % 2, :],
                                        ALU.mult).then_inc(s_picked, 1)

            def prologue():
                rstd_of(0)
                rstd_of(1)

            def body(i, par, first, units, pre, ln):
                for u in range(NS if units else 1):
                    if topk and units:
                        scale_maximum(i, u)
                    c = lagged(u, 1, first, units)
                    if topk and c is not None:
                        pick(i, c)
                    if ln and u == AGGR:
                        rstd_of(i + 2)

            iterations(pool, body, prologue)

        @block.scalar
        def _(act):
            def modulate(g, bs=range(G)):
                if scale_at is None:
                    if bs[-1] < G - 1:
                        return
                    after(act, s_xT, g + 1)
                    nc.scalar.copy(hT[:, :], l_ps[:, :]).then_inc(s_hT, 1)
                    return
                after_alone(act, s_xT, g + 1)
                for b in bs:
                    last = nc.scalar.activation(
                        hT[:, b * T:(b + 1) * T], l_ps[:, b * T:(b + 1) * T], ACT.Identity,
                        scale=r.mod[:, scale_at, bass.ds(G * g + b, 1)],
                        bias=r.mod[:, shift_at, bass.ds(G * g + b, 1)])
                if bs[-1] == G - 1:
                    last.then_inc(s_hT, 1)

            def keys_out(g, par):
                if split:
                    for q in range(4):
                        after(act, s_quarter[q], QB * g)
                    act.wait_ge(s_kps, g + 1)
                    nc.scalar.activation(kT[:, 0, :], l_ps[:, 0:G * KW], ACT.Identity, bias=bk
                                         ).then_inc(s_kT, 1)
                    return
                after(act, s_half1, HB * (g - 1))
                for q in range(4):
                    after(act, s_quarter[q], QB * (g - 1))
                act.wait_ge(s_kps, g + 1)
                nc.scalar.activation(kT[:, par, :], l_ps[:, 0:G * keys], ACT.Identity, bias=bk
                                     ).then_inc(s_kT, 1)

            def values_out(g, par):
                if topk:
                    act.wait_ge(s_vps, g + 1)
                    nc.scalar.copy(vp[0:keys, par, :, :, 0:D],
                                   l_ps[0:keys, :].rearrange("p (b h d) -> p b h d", b=G, d=D)).then_inc(s_v, 1)

            def queries_out(g, par):
                if split:
                    for q in range(4):
                        after(act, s_quarter[q], QB * g)
                    after(act, s_half1, HB * g)
                act.wait_ge(s_qps, g + 1)
                nc.scalar.activation(qT[:, 0 if split else par, :], l_ps[:, :], ACT.Identity, bias=bq
                                     ).then_inc(s_qT, 1)

            def prologue():
                modulate(0)
                keys_out(0, 0)
                queries_out(0, 0)
                values_out(0, 0)

            def body(i, par, first, units, pre, ln):
                for u in range(NS if units else PGT + 1):
                    c = lagged(u, LT, first, units)
                    if c is not None:
                        n = NS * i + c
                        after(act, s_pv, n - 1)
                        act.wait_ge(s_probT, n + 1)
                        nc.scalar.copy(pT[0:rows, c % 2, :], t_ps[0:rows, c % 2, :]).then_inc(s_pT, 1)
                    c = lagged(u, LO, first, units)
                    if c is not None and c % NU == NU - 1:
                        m = G * i + c // NU
                        b = c // NU
                        after(act, s_otr, m - 1)
                        act.wait_ge(s_pv, NS * i + c + 1)
                        nc.scalar.copy(oT[:, b % 2, :], o_ps[:, b % 2, 0:NU * T]).then_inc(s_oT, 1)
                    if units and topk:
                        n = NS * i + u
                        after(act, s_probT, n - 3)
                        act.wait_ge(s_cut, n + 1)
                        act.wait_ge(s_dif, n + 1)
                        for h in range(HU):
                            last = nc.scalar.activation(prob[:, u % 4, h * keys:(h + 1) * keys],
                                                        s_ps[:, u % 2, h * keys:(h + 1) * keys], ACT.Exp,
                                                        scale=SCALE, bias=nmx[:, u % 2, h:h + 1])
                        last.then_inc(s_exp, 1)
                    c = lagged(u, LE, first, units)
                    if c is not None and not topk:
                        act.wait_ge(s_dif, NS * i + c + 1)
                        nc.scalar.activation(prob[:, c % 4, :], prob[:, c % 4, :], ACT.Exp, scale=SCALE
                                             ).then_inc(s_exp, 1)
                    if pre and window and u == XT:
                        modulate(i + 1)
                    if pre and not window and u == XT:
                        modulate(i + 1, range(0, G // 2))
                    if pre and not window and u == XT + 1:
                        modulate(i + 1, range(G // 2, G))
                    if pre and u == KP:
                        keys_out(i + 1, 1 - par)
                    if pre and u == QP:
                        queries_out(i + 1, 1 - par)
                    if pre and u == VP:
                        values_out(i + 1, 1 - par)
                    if not first and u == ONT:
                        after(act, s_pgps, i - 1)
                        act.wait_ge(s_onps, i)
                        nc.scalar.activation(onT[:, :], l_ps[:, :], ACT.Identity, bias=bv).then_inc(s_onT, 1)
                    if not first and gate is None and u == PROJ:
                        act.wait_ge(s_pjps, i)
                        nc.scalar.activation(pg[:, :], l_ps[:, :], ACT.Identity, bias=r.bcol(name_o)
                                             ).then_inc(s_pg, 1)
                    if not first and gate is not None:
                        bs = {PROJ: range(G)} if window else {PROJ: range(0, 2), PROJ + 1: range(2, G)}
                        if u in bs:
                            after_alone(act, s_pjps, i)
                            for b in bs[u]:
                                at = G * i - G + b
                                last = nc.scalar.activation(
                                    pg[:, b * T:(b + 1) * T], l_ps[:, b * T:(b + 1) * T], ACT.Identity,
                                    scale=r.mod[:, gate, bass.ds(at, 1)],
                                    bias=r.gb[:, n_gb, bass.ds(at, 1)])
                            if bs[u][-1] == G - 1:
                                last.then_inc(s_pg, 1)

            iterations(act, body, prologue)

        @block.vector
        def _(dve):
            nc.vector.memset(o_ps[:, :, :], 0.0).then_inc(s_zero, 1)

            def low_parts(g, out, hi, done, bias, n, signal):
                dve.wait_ge(done, g + 1)
                nc.vector.scalar_tensor_tensor(out, l_ps[:, 0:n], bias, hi, ALU.add, ALU.subtract
                                               ).then_inc(signal, 1)

            def low_keys(g):
                if split:
                    low_parts(g, kT[:, 1, :], kT[:, 0, :].bitcast(F32), s_kT, bk, G * KW, s_klo)

            def low_queries(g):
                if split:
                    low_parts(g, qT[:, 1, :], qT[:, 0, :].bitcast(F32), s_qT, bq, GT, s_qlo)

            def ln_stats(g, bs=range(G)):
                for b in bs:
                    last = nc.vector.bn_stats(stats[:, b, :], r.x[:, bass.ds(G * g + b, 1), :])
                if bs[-1] == G - 1:
                    last.then_inc(s_stats, 1)

            def ln_variance(g):
                after_alone(dve, s_stats, g + 1)
                for b in range(G):
                    last = nc.vector.bn_aggr(mv[:, b, :], stats[:, b, :])
                last.then_inc(s_mv, 1)
                dve.wait_ge(s_mv, g + 1)
                nc.vector.tensor_scalar(vareps[:, :], mv[:, :, 1], 1e-6, None, ALU.add).then_inc(s_var, 1)

            def ln_apply(g, bs=range(G)):
                if bs[0] == 0:
                    after(dve, s_xT, g)
                    dve.wait_ge(s_rstd, g + 1)
                for b in bs:
                    last = nc.vector.tensor_scalar(xn[:, b:b + 1, :], r.x[:, bass.ds(G * g + b, 1), :],
                                                   mv[:, b, 0:1], rstd[:, b:b + 1], ALU.subtract, ALU.mult)
                if bs[-1] == G - 1:
                    last.then_inc(s_xn, 1)

            def values_out(g, par, w):
                if topk:
                    return
                dve.wait_ge(s_vps, NV * g + w + 1)
                if window:
                    for a in range(2):
                        p0 = WIN * a
                        last = nc.vector.tensor_copy(
                            vp[p0:p0 + WIN, par, :, w, :, (D + 1) * a:(D + 1) * a + D],
                            l_ps[p0:p0 + WIN, :].rearrange("p (b h d) -> p b h d", b=G, d=2 * D)
                            [:, :, :, D * a:D * a + D])
                    last.then_inc(s_v, 1)
                else:
                    nc.vector.tensor_copy(vp[0:keys, par, :, :, 0:D],
                                          l_ps[0:keys, :].rearrange("p (b h d) -> p b h d", b=G, d=D)
                                          ).then_inc(s_v, 1)

            def max_and_difference(i, u):
                n = NS * i + u
                SW = WIN if window else KW
                sc = s_ps[:, u % 2, 0:HU * SW].rearrange("p (h k) -> p h k", h=HU)[:, :, 0:cols // HU]
                after(dve, s_probT, n - 3)
                dve.wait_ge(s_scores, n + 1)
                nc.vector.tensor_reduce(mx[:, u % 2, :], sc, AX.X, ALU.max).then_inc(s_max, 1)
                dve.wait_ge(s_max, n + 1)
                m = mx[:, u % 2, :].rearrange("p (h a) -> p h a", a=1)
                nc.vector.tensor_tensor(prob[:, u % 4, :].rearrange("p (h k) -> p h k", h=HU), sc,
                                        m.broadcast_to([T, HU, cols // HU]), ALU.subtract).then_inc(s_dif, 1)

            def find_top(i, u, first, units):
                c = lagged(u, 1, first, units)
                n = NS * i + u
                wk_ = [work[:, k, :].rearrange("p (h k) -> p h k", h=HU) for k in range(4)]
                sc = s_ps[:, u % 2, 0:cols].rearrange("p (h k) -> p h k", h=HU)
                if units:
                    after_alone(dve, s_dif, n - 1)
                    after_alone(dve, s_scores, n + 1)
                    for h in range(HU):
                        last = nc.vector.max(top[:, u % 2, h, :], sc[:, h, :])
                    last.then_inc(s_top, 1)
                if c is not None:
                    after_alone(dve, s_cut, n)
                    for h in range(HU):
                        last = nc.vector.max(top2[:, c % 2, h, :], wk_[c % 4][:, h, :])
                    last.then_inc(s_top2, 1)
                if units:
                    after_alone(dve, s_top, n + 1)
                    after_alone(dve, s_picked, n - 3)
                    for h in range(HU):
                        last = nc.vector.match_replace(wk_[u % 4][:, h, :], top[:, u % 2, h, :], sc[:, h, :], NEG)
                    last.then_inc(s_cut, 1)
                if c is not None:
                    after_alone(dve, s_top2, n)
                    for h in range(HU):
                        last = nc.vector.match_replace(wk_[c % 4][:, h, :], top2[:, c % 2, h, :],
                                                       wk_[c % 4][:, h, :], NEG)
                    last.then_inc(s_cut2, 1)

            def normalise(i, b):
                m = G * i + b
                dve.wait_ge(s_otr, m + 1)
                rv = rden[:, b % 2, :]
                if window:
                    src = r_ps[:, 0:NU * T].rearrange("p (q c) -> p q c", c=32)
                    nc.vector.reciprocal(rv.rearrange("p (q a) -> p q a", a=2),
                                         src[:, :, D:2 * D + 2:D + 1]).then_inc(s_rden, 1)
                else:
                    src = r_ps[:, :].rearrange("p (h c) -> p h c", c=32)
                    nc.vector.reciprocal(rv, src[:, :, D]).then_inc(s_rden, 1)
                if b % G == 0:
                    after(dve, s_onps, i)
                dve.wait_ge(s_rden, m + 1)
                out = on[:, b % G, :].rearrange("p (h d) -> p h d", d=D)
                if window:
                    for a in range(2):
                        last = nc.vector.tensor_tensor(
                            out[:, a::2, :], src[:, :, (D + 1) * a:(D + 1) * a + D],
                            rv[:, a::2].rearrange("p (q a) -> p q a", a=1).broadcast_to([T, H // 2, D]), ALU.mult)
                else:
                    last = nc.vector.tensor_tensor(
                        out, src[:, :, 0:D],
                        rv.rearrange("p (h a) -> p h a", a=1).broadcast_to([T, H, D]), ALU.mult)
                last.then_inc(s_norm, 1)

            def prologue():
                ln_stats(0)
                ln_variance(0)
                ln_apply(0)
                low_keys(0)
                low_queries(0)
                ln_stats(1)
                ln_variance(1)
                ln_apply(1)
                for w in range(NV):
                    values_out(0, 0, w)

            def body(i, par, first, units, pre, ln):
                for u in range(NS if units else PGT + 1):
                    if topk:
                        find_top(i, u, first, units) if units or u == 0 else None
                    elif units:
                        max_and_difference(i, u)
                    if pre and u == KP:
                        low_keys(i + 1)
                    if pre and u == QP:
                        low_queries(i + 1)
                    if pre and u in (VP, VP + 1)[:NV]:
                        values_out(i + 1, 1 - par, u - VP)
                    if ln and u in STATS:
                        ln_stats(i + 2, [b for b in range(G) if STATS[b] == u])
                    if ln and u == AGGR:
                        ln_variance(i + 2)
                    if ln and u in APPLY:
                        ln_apply(i + 2, [b for b in range(G) if APPLY[b] == u])
                    b = sequence_hooks(u, first, units)
                    if b is not None:
                        normalise(i, b)
                    if not first and u == PGT:
                        after_alone(dve, s_pgps, i)
                        xg = r.x[:, bass.ds(G * i - G, G), :]
                        nc.vector.tensor_tensor(xg, r_ps[:, :].rearrange("p (b c) -> p b c", b=G), xg,
                                                ALU.add).then_inc(s_x, 1)

            iterations(dve, body, prologue)

        @block.tensor
        def _(pe):
            def transpose_xn(g):
                after(pe, s_v, NV * g)
                after(pe, s_pg, g - 2)
                pe.wait_ge(s_xn, g + 1)
                for b in range(G):
                    last = nc.tensor.transpose(l_ps[:, b * T:(b + 1) * T], xn[:, b, :], r.ident[:, :])
                last.then_inc(s_xT, 1)

            def project_keys(g):
                if cross:
                    pe.wait_ge(s_ctx, 16 * g + 16)
                pe.wait_ge(s_hT, g + 1)
                nc.tensor.matmul(l_ps[:, 0:G * KW], wk, ctxs[:, :] if cross else hT[:, :],
                                 start=True, stop=True).then_inc(s_kps, 1)

            def project_queries(g):
                pe.wait_ge(s_klo if split else s_kT, g + 1)
                nc.tensor.matmul(l_ps[:, :], wq, hT[:, :], start=True, stop=True).then_inc(s_qps, 1)

            def project_values(g, w):
                if w == 0:
                    pe.wait_ge(s_qlo if split else s_qT, g + 1)
                else:
                    pe.wait_ge(s_v, NV * g + w)
                for b in range(G):
                    if window:
                        for a in range(2):
                            last = nc.tensor.matmul(l_ps[WIN * a:WIN * a + WIN, b * C:(b + 1) * C],
                                                    hT[:, b * T + WIN * w:b * T + WIN * w + WIN], wv,
                                                    start=True, stop=True)
                    else:
                        lhs = ctxs[:, b * KW:b * KW + S] if cross else hT[:, b * T:(b + 1) * T]
                        last = nc.tensor.matmul(l_ps[0:keys, b * C:(b + 1) * C], lhs, wv,
                                                start=True, stop=True)
                last.then_inc(s_vps, 1)

            def scores(i, u, par):
                n = NS * i + u
                if u == 0 and not split:
                    pe.wait_ge(s_qT, i + 1)
                if split and u == 0:
                    for q in range(4):
                        pe.wait_ge(s_quarter[q], QB * i + QB)
                if not split and u < NU:
                    for q in range(4 // NU * u, 4 // NU * (u + 1)):
                        pe.wait_ge(s_quarter[q], QB * i + QB)
                if u == NS // 2:
                    pe.wait_ge(s_half1, HB * i + HB)
                if topk:
                    after(pe, s_exp, n - 1)
                else:
                    after(pe, s_dif, n - 1)
                b, g = divmod(u, NU)
                if split:
                    last = product3(nc, s_ps[:, u % 2, 0:HU * KW],
                                    [r.qz[:, g, k, b * T:(b + 1) * T] for k in range(2)],
                                    [r.kbd[:, par, :, k, b * KW:(b + 1) * KW] for k in range(2)])
                elif window:
                    for w in range(2):
                        c0 = b * T + WIN * w
                        last = nc.tensor.matmul(s_ps[WIN * w:WIN * w + WIN, u % 2, 0:cols],
                                                qT[:, par, c0:c0 + WIN],
                                                r.kbd[:, HU * g:HU * g + HU, c0:c0 + WIN],
                                                start=True, stop=True)
                else:
                    last = nc.tensor.matmul(s_ps[:, u % 2, 0:cols], qT[:, par, b * T:(b + 1) * T],
                                            r.kbd[:, HU * g:HU * g + HU, b * keys:(b + 1) * keys],
                                            start=True, stop=True)
                last.then_inc(s_scores, 1)

            def transpose_probs(i, c):
                n = NS * i + c
                after(pe, s_pT, n - 1)
                pe.wait_ge(s_picked if topk else s_exp, n + 1)
                for j in range(4):
                    last = nc.tensor.transpose(t_ps[0:rows, c % 2, j * T:(j + 1) * T],
                                               prob[:, c % 4, j * rows:(j + 1) * rows], r.ident[:, :])
                last.then_inc(s_probT, 1)

            def values_times_probs(i, c, par):
                n = NS * i + c
                b, g = divmod(c, NU)
                if g == 0:
                    after(pe, s_oT, G * i + b - 1)
                if c % NS == 0:
                    pe.wait_ge(s_v, NV * i + NV) if c == 0 else None
                pe.wait_ge(s_pT, n + 1)
                b %= G
                for j in range(4):
                    if window:
                        for w in range(2):
                            last = nc.tensor.matmul(
                                o_ps[32 * j:32 * j + VM, b % 2, g * T + WIN * w:g * T + WIN * w + WIN],
                                vp[:, par, b, w, 4 * g + j, :],
                                pT[:, c % 2, j * T + WIN * w:j * T + WIN * w + WIN],
                                start=True, stop=True, tile_position=(0, 32 * j))
                    else:
                        last = nc.tensor.matmul(o_ps[32 * j:32 * j + VM, b % 2, g * T:(g + 1) * T],
                                                vp[0:keys, par, b, HU * g + j, :],
                                                pT[0:keys, c % 2, j * T:(j + 1) * T],
                                                start=True, stop=True, tile_position=(0, 32 * j))
                last.then_inc(s_pv, 1)

            def output_to_rows(i, b):
                m = G * i + b
                pe.wait_ge(s_oT, m + 1)
                if b % G == (1 if window else 2):
                    after(pe, s_x, i if b > 0 else i - 1)
                after(pe, s_norm, m)
                for g in range(NU):
                    last = nc.tensor.transpose(r_ps[:, g * T:(g + 1) * T], oT[:, b % 2, g * T:(g + 1) * T],
                                               r.ident[:, :])
                last.then_inc(s_otr, 1)

            def prologue():
                pe.wait_ge(s_init, n_init)
                pe.wait_ge(s_zero, 1)
                transpose_xn(0)
                project_keys(0)
                project_queries(0)
                for w in range(NV):
                    project_values(0, w)

            def body(i, par, first, units, pre, ln):
                for u in range(NS if units else PGT + 1):
                    if units:
                        scores(i, u, par)
                    c = lagged(u, LT, first, units)
                    if c is not None:
                        transpose_probs(i, c)
                    c = lagged(u, LV, first, units)
                    if c is not None:
                        values_times_probs(i, c, par if c >= 0 else 1 - par)
                    if pre and u == XT:
                        transpose_xn(i + 1)
                    if pre and u == KP:
                        project_keys(i + 1)
                    if pre and u == QP:
                        project_queries(i + 1)
                    if pre and u in (VP, VP + 1)[:NV]:
                        project_values(i + 1, u - VP)
                    if not first and u == ONT:
                        after(pe, s_v, NV * i + 2 * NV if pre else NV * NG)
                        after(pe, s_pg, i - 1)
                        pe.wait_ge(s_norm, G * i)
                        for b in range(G):
                            last = nc.tensor.transpose(l_ps[:, b * T:(b + 1) * T], on[:, b, :], r.ident[:, :])
                        last.then_inc(s_onps, 1)
                    b = sequence_hooks(u, first, units)
                    if b is not None:
                        output_to_rows(i, b)
                    if not first and u == PROJ:
                        pe.wait_ge(s_onT, i)
                        nc.tensor.matmul(l_ps[:, :], r.W(name_o), onT[:, :], start=True, stop=True
                                         ).then_inc(s_pjps, 1)
                    if not first and u == PGT:
                        after(pe, s_norm, G * i + (1 if window else 2) if units else G * i)
                        pe.wait_ge(s_pg, i)
                        for b in range(G):
                            last = nc.tensor.transpose(r_ps[:, b * C:(b + 1) * C], pg[:, b * T:(b + 1) * T],
                                                       r.ident[:, :])
                        last.then_inc(s_pgps, 1)

            iterations(pe, body, prologue)


def split_weights(nc, copy, engine, parts, w, done, base):
    copy(parts[:, 0, :], w).then_inc(done, 1)
    engine.wait_ge(done, base + 1)
    nc.vector.tensor_tensor(parts[:, 1, :], w, parts[:, 0, :].bitcast(F32), ALU.subtract).then_inc(done, 1)


def mlp_phase(nc, r, layer):
    swiglu = layer == 0
    NC = HID // C
    LD = 3
    name, name1 = f"m2_{layer}", f"m1_{layer}"
    W1 = W_WIDTH[name1]
    gate = dict(GATED)[name]
    n_gb = [n for n, _ in GATED].index(name)
    with nc.cleanup_on_exit(), ExitStack() as ctx:
        tag = f"mlp{layer}_"

        def sb(name, shape, dtype=F32):
            return ctx.enter_context(nc.sbuf_tensor(tag + name, shape, dtype))

        def ps(name, shape):
            return ctx.enter_context(nc.psum_tensor(tag + name, shape, F32))

        def sem(name):
            return nc.alloc_semaphore(tag + name)

        w1, w2 = sb("w1", [C, 2, W1], F32R), sb("w2", [C, 2, NC * C], F32R)
        stats, mv = sb("stats", [T, G, 6]), sb("mv", [T, G, 2])
        vareps, rstd = sb("vareps", [T, G]), sb("rstd", [T, G])
        xn, hT = sb("xn", [T, G, C]), sb("hT", [C, GT])
        hT2 = sb("hT2", [C, 2, 2, GT], F32R)
        half = sb("half", [C, 2, GT]) if swiglu else None
        NB = 2 if swiglu else NC
        hid = sb("hid", [C, NB, GT])
        hid2 = sb("hid2", [C, NC, 2, GT], F32R)
        pg = sb("pg", [C, GT])
        l_ps, y_ps, r_ps = ps("l", [C, BANK]), ps("y", [C, 2, BANK]), ps("r", [T, BANK])
        u_ps = ps("u", [C, 4, BANK])
        s_stats, s_mv, s_var, s_rstd, s_xn = sem("stats"), sem("mv"), sem("var"), sem("rstd"), sem("xn")
        s_xT, s_hT, s_hhi, s_hlo, s_pg, s_pgps, s_x = (
            sem(n) for n in ("xT", "hT", "hhi", "hlo", "pg", "pgps", "x"))
        s_w, s_zeroed = sem("w"), sem("zeroed")
        s_up, s_half, s_hid, s_hi, s_lo, s_down = (sem(n) for n in ("up", "half", "hid", "hi", "lo", "down"))
        block = ctx.enter_context(nc.Block())

        def iterations(engine, body, prologue):
            prologue()
            body(0, 0, False, True, False, True, True)
            body(1, 1, True, True, False, True, True)
            body(2, 0, True, True, True, True, True)
            body(3, 1, True, True, True, True, True)
            with engine.Fori(2, NG // 2 - 1) as t:
                body(2 * t, 0, True, True, True, True, True)
                body(2 * t + 1, 1, True, True, True, True, True)
            body(NG - 2, 0, True, True, True, True, False)
            body(NG - 1, 1, True, True, True, False, False)
            body(NG, 0, True, False, True, False, False)
            body(NG + 1, 1, False, False, True, False, False)

        @block.gpsimd
        def _(pool):
            def rstd_of(g):
                pool.wait_ge(s_var, g + 1)
                nc.gpsimd.tensor_tensor(rstd[:, :], vareps[:, :], r.neg_half[:, :], ALU.pow).then_inc(s_rstd, 1)

            def prologue():
                rstd_of(0)
                rstd_of(1)
                if layer == 0:
                    nc.gpsimd.memset(r.kbd[:, :, :, :, :].bitcast(F32), 0.0).then_inc(s_zeroed, 1)
                    nc.gpsimd.memset(r.qz[:, :, :, :].bitcast(F32), 0.0).then_inc(s_zeroed, 1)

            def body(g, par, late, work, add, nxt, nxt2):
                for c in range(NC if work else 0):
                    n = NC * g + c
                    if c == 1 and nxt2:
                        rstd_of(g + 2)
                    if swiglu or c < NC - 1:
                        pool.wait_ge(s_hi, n + 1)
                        nc.gpsimd.tensor_tensor(hid2[:, c, 1, :], hid[:, c % NB, :], hid2[:, c, 0, :].bitcast(F32),
                                                ALU.subtract).then_inc(s_lo, 1)

            iterations(pool, body, prologue)

        @block.vector
        def _(dve):
            def ln_stats(g, bs):
                for b in bs:
                    last = nc.vector.bn_stats(stats[:, b, :], r.x[:, bass.ds(G * g + b, 1), :])
                if bs[-1] == G - 1:
                    last.then_inc(s_stats, 1)

            def ln_variance(g):
                after_alone(dve, s_stats, g + 1)
                for b in range(G):
                    last = nc.vector.bn_aggr(mv[:, b, :], stats[:, b, :])
                last.then_inc(s_mv, 1)
                dve.wait_ge(s_mv, g + 1)
                nc.vector.tensor_scalar(vareps[:, :], mv[:, :, 1], 1e-6, None, ALU.add).then_inc(s_var, 1)

            def ln_apply(g):
                after(dve, s_xT, g)
                dve.wait_ge(s_rstd, g + 1)
                for b in range(G):
                    last = nc.vector.tensor_scalar(xn[:, b:b + 1, :], r.x[:, bass.ds(G * g + b, 1), :],
                                                   mv[:, b, 0:1], rstd[:, b:b + 1], ALU.subtract, ALU.mult)
                last.then_inc(s_xn, 1)

            def split_h(g, par):
                after(dve, s_up, NC * (g - 1))
                dve.wait_ge(s_hT, g + 1)
                nc.vector.tensor_copy(hT2[:, par, 0, :], hT[:, :]).then_inc(s_hhi, 1)
                dve.wait_ge(s_hhi, g + 1)
                nc.vector.tensor_tensor(hT2[:, par, 1, :], hT[:, :], hT2[:, par, 0, :].bitcast(F32),
                                        ALU.subtract).then_inc(s_hlo, 1)

            def prologue():
                ln_stats(0, range(G))
                ln_variance(0)
                split_weights(nc, nc.vector.tensor_copy, dve, w1, r.W(name1, 0, W1), s_w, 0)
                ln_apply(0)
                ln_stats(1, range(G))
                ln_variance(1)
                split_weights(nc, nc.vector.tensor_copy, dve, w2, r.W(name, 0, NC * C), s_w, 2)
                ln_apply(1)
                split_h(0, 0)

            def body(g, par, late, work, add, nxt, nxt2):
                for c in range(NC if work or add else 0):
                    n = NC * g + c
                    if add and c == 1:
                        after_alone(dve, s_pgps, g - 1)
                        xg = r.x[:, bass.ds(G * g - 2 * G, G), :]
                        nc.vector.tensor_tensor(xg, r_ps[:, :].rearrange("p (b c) -> p b c", b=G), xg,
                                                ALU.add).then_inc(s_x, 1)
                    if not work:
                        continue
                    if c == 2 and nxt:
                        split_h(g + 1, 1 - par)
                    if swiglu:
                        after(dve, s_lo, n + 1 - NB)
                        dve.wait_ge(s_half, n + 1)
                        nc.vector.scalar_tensor_tensor(hid[:, c % NB, :], u_ps[:, (2 * c + 1) % 4, :],
                                                       r.bcol("m1_0", NC + c), half[:, c % 2, :],
                                                       ALU.add, ALU.mult).then_inc(s_hid, 1)
                    if nxt2 and c == 0:
                        ln_stats(g + 2, range(G))
                    if nxt2 and c == 1:
                        ln_variance(g + 2)
                    if not swiglu:
                        after(dve, s_down, n - 3)
                        dve.wait_ge(s_hid, n + 1)
                        nc.vector.tensor_copy(hid2[:, c, 0, :], hid[:, c % NB, :]).then_inc(s_hi, 1)
                    if c == 2 and nxt2:
                        ln_apply(g + 2)
                    if c == 3 and not swiglu:
                        dve.wait_ge(s_hi, n + 1)
                        after(dve, s_lo, n)
                        nc.vector.tensor_tensor(hid2[:, c, 1, :], hid[:, c % NB, :], hid2[:, c, 0, :].bitcast(F32),
                                                ALU.subtract).then_inc(s_lo, 1)
            iterations(dve, body, prologue)

        @block.scalar
        def _(act):
            def modulate(g, bs):
                after(act, s_hlo, g)
                after_alone(act, s_xT, g + 1)
                for b in bs:
                    last = nc.scalar.activation(
                        hT[:, b * T:(b + 1) * T], l_ps[:, b * T:(b + 1) * T], ACT.Identity,
                        scale=r.mod[:, SC_M[layer], bass.ds(G * g + b, 1)],
                        bias=r.mod[:, SH_M[layer], bass.ds(G * g + b, 1)])
                if bs[-1] == G - 1:
                    last.then_inc(s_hT, 1)

            def apply_gate(g, par, bs):
                after(act, s_pgps, g)
                after_alone(act, s_down, NC * g + NC)
                for b in bs:
                    last = nc.scalar.activation(
                        pg[:, b * T:(b + 1) * T], y_ps[:, par, b * T:(b + 1) * T], ACT.Identity,
                        scale=r.mod[:, gate, bass.ds(G * g + b, 1)],
                        bias=r.gb[:, n_gb, bass.ds(G * g + b, 1)])
                if bs[-1] == G - 1:
                    last.then_inc(s_pg, 1)

            def body(g, par, late, work, add, nxt, nxt2):
                for c in range(NC):
                    n = NC * g + c
                    if work and swiglu:
                        after(act, s_hid, n - 1)
                        act.wait_ge(s_up, n + 1)
                        nc.scalar.activation(half[:, c % 2, :], u_ps[:, (2 * c) % 4, :], ACT.Silu,
                                             bias=r.bcol("m1_0", c)).then_inc(s_half, 1)
                    if swiglu and (work if c else late):
                        after(act, s_down, n - 4)
                        act.wait_ge(s_hid, n)
                        nc.scalar.copy(hid2[:, (c - 1) % NC, 0, :], hid[:, (c - 1) % NB, :]).then_inc(s_hi, 1)
                    if work and not swiglu:
                        after(act, s_lo, n - 3)
                        act.wait_ge(s_up, n + 1)
                        nc.scalar.activation(hid[:, c % NB, :], u_ps[:, c, :], ACT.Gelu_apprx_tanh,
                                             bias=r.bcol(name1, c)).then_inc(s_hid, 1)
                    if c < 2 and nxt and work:
                        modulate(g + 1, [2 * c, 2 * c + 1])
                    if c >= 2 and late:
                        apply_gate(g - 1, 1 - par, [2 * c - 4, 2 * c - 3])

            iterations(act, body, lambda: modulate(0, range(G)))

        @block.tensor
        def _(pe):
            def transpose_xn(g):
                after(pe, s_hT, g)
                pe.wait_ge(s_xn, g + 1)
                for b in range(G):
                    last = nc.tensor.transpose(l_ps[:, b * T:(b + 1) * T], xn[:, b, :], r.ident[:, :])
                last.then_inc(s_xT, 1)

            def parts(w, c0):
                return [w[:, k, c0:c0 + C] for k in range(2)]

            def up(g, c, par):
                n = NC * g + c
                after(pe, s_hid, n - 1 if swiglu else n - 3)
                if c == 0:
                    pe.wait_ge(s_hlo, g + 1)
                    pe.wait_ge(s_w, 2)
                x = [hT2[:, par, k, :] for k in range(2)]
                if swiglu:
                    product3(nc, u_ps[:, (2 * c) % 4, :], parts(w1, c * C), x)
                    product3(nc, u_ps[:, (2 * c + 1) % 4, :], parts(w1, HID + c * C), x).then_inc(s_up, 1)
                else:
                    product3(nc, u_ps[:, c, :], parts(w1, c * C), x).then_inc(s_up, 1)

            def down(g, c, par):
                n = NC * g + c
                if c == 0:
                    after(pe, s_pg, g - 1)
                    pe.wait_ge(s_w, 4)
                pe.wait_ge(s_lo, n + 1)
                product3(nc, y_ps[:, par, :], parts(w2, c * C), [hid2[:, c, k, :] for k in range(2)],
                         start=(c == 0), stop=(c == NC - 1)).then_inc(s_down, 1)

            def body(g, par, late, work, add, nxt, nxt2):
                for c in range(NC):
                    if work:
                        up(g, c, par)
                    if c >= LD and work:
                        down(g, c - LD, par)
                    elif c < LD and late:
                        down(g - 1, c - LD + NC, 1 - par)
                    if c == 1 and add:
                        after(pe, s_x, g - 2)
                        pe.wait_ge(s_pg, g - 1)
                        for b in range(G):
                            last = nc.tensor.transpose(r_ps[:, b * C:(b + 1) * C], pg[:, b * T:(b + 1) * T],
                                                       r.ident[:, :])
                        last.then_inc(s_pgps, 1)
                    if c == 0 and nxt and work:
                        transpose_xn(g + 1)

            iterations(pe, body, lambda: transpose_xn(0))


def evidence_phase(nc, r, st):
    K4 = G * S
    scale = float(C) ** -0.5
    with nc.cleanup_on_exit(), ExitStack() as ctx:
        tag = "evid_"

        def sb(name, shape):
            return ctx.enter_context(nc.sbuf_tensor(tag + name, shape, F32))

        def ps(name, shape):
            return ctx.enter_context(nc.psum_tensor(tag + name, shape, F32))

        def sem(name):
            return nc.alloc_semaphore(tag + name)

        stats, mv = sb("stats", [T, G, 6]), sb("mv", [T, G, 2])
        vareps, rstd = sb("vareps", [T, G]), sb("rstd", [T, G])
        xn = sb("xn", [T, G, C])
        ctxs = sb("ctxs", [C, K4])
        qT, kT, v = sb("qT", [C, GT]), sb("kT", [C, K4]), sb("v", [S, G, C])
        mx, dif, prob, pn = sb("mx", [T, G]), sb("dif", [T, K4]), sb("prob", [T, K4]), sb("pn", [T, K4])
        den, rden = sb("den", [T, G]), sb("rden", [T, G])
        pT = sb("pT", [S, GT])
        rl = sb("rl", [E, GT])
        rmx, rdif, rexp = sb("rmx", [T, G]), sb("rdif", [T, G * E]), sb("rexp", [T, G * E])
        rden2, rrd = sb("rden2", [T, G]), sb("rrd", [T, G])
        l_ps, s_ps, t_ps, e_ps = ps("l", [C, BANK]), ps("s", [T, BANK]), ps("t", [S, BANK]), ps("e", [C, BANK])
        rt_ps, rr_ps = ps("rt", [E, BANK]), ps("rr", [T, BANK])
        a_ps = ps("a", [C, BANK])
        s_w3, s_aps, s_anchor = sem("w3"), sem("aps"), sem("anchor")
        s_stats, s_mv, s_var, s_rstd, s_xn = sem("stats"), sem("mv"), sem("var"), sem("rstd"), sem("xn")
        s_xT, s_nx, s_kps, s_kT, s_qps, s_qT, s_vps, s_v = (sem(n) for n in ("xT", "nx", "kps", "kT", "qps", "qT", "vps", "v"))
        s_ctx, s_scores, s_max, s_dif, s_exp, s_den, s_rden, s_pn = (
            sem(n) for n in ("ctx", "scores", "max", "dif", "exp", "den", "rden", "pn"))
        s_tps, s_pT, s_eps, s_ev = sem("tps"), sem("pT"), sem("eps"), sem("ev")
        s_rtps, s_rl, s_rrps, s_rmax, s_rdif, s_rexp, s_rsum, s_rrd, s_probs = (
            sem(n) for n in ("rtps", "rl", "rrps", "rmax", "rdif", "rexp", "rsum", "rrd", "probs"))
        block = ctx.enter_context(nc.Block())

        def iterations(engine, body, prologue):
            prologue()
            body(0, False, True, True, True)
            body(1, True, True, True, True)
            with engine.Fori(2, NG - 2) as g:
                body(g, True, True, True, True)
            body(NG - 2, True, True, True, False)
            body(NG - 1, True, True, False, False)
            body(NG, True, False, False, False)

        def by_batch(ap, n):
            return ap.rearrange("p (b k) -> p b k", k=n)

        def spread(ap, n):
            return ap.rearrange("p (b a) -> p b a", a=1).broadcast_to([T, G, n])

        @block.sync
        def _(sp):
            def stage_context(g):
                after_alone(sp, s_vps, g)
                sp.dma_start(by_batch(ctxs[:, :], S), r.ctxT[:, bass.ds(G * g, G), :]).then_inc(s_ctx, 16)

            stage_context(0)
            sp.dma_start(r.w3[:, :], st.weights3).then_inc(s_w3, 16)
            with sp.Fori(1, NG) as g:
                stage_context(g)
            sp.wait_ge(s_w3, 16)

        @block.gpsimd
        def _(pool):
            def rstd_of(g):
                pool.wait_ge(s_var, g + 1)
                nc.gpsimd.tensor_tensor(rstd[:, :], vareps[:, :], r.neg_half[:, :], ALU.pow).then_inc(s_rstd, 1)

            rstd_of(0)
            with pool.Fori(1, NG) as g:
                rstd_of(g)

        @block.vector
        def _(dve):
            def statistics(g):
                for b in range(G):
                    last = nc.vector.bn_stats(stats[:, b, :], r.x[:, bass.ds(G * g + b, 1), :])
                last.then_inc(s_stats, 1)
                after_alone(dve, s_stats, g + 1)
                for b in range(G):
                    last = nc.vector.bn_aggr(mv[:, b, :], stats[:, b, :])
                last.then_inc(s_mv, 1)
                dve.wait_ge(s_mv, g + 1)
                nc.vector.tensor_scalar(vareps[:, :], mv[:, :, 1], 1e-5, None, ALU.add).then_inc(s_var, 1)

            def apply(g):
                after(dve, s_xT, g)
                dve.wait_ge(s_rstd, g + 1)
                for b in range(G):
                    last = nc.vector.tensor_scalar(xn[:, b:b + 1, :], r.x[:, bass.ds(G * g + b, 1), :],
                                                   mv[:, b, 0:1], rstd[:, b:b + 1], ALU.subtract, ALU.mult)
                last.then_inc(s_xn, 1)

            def values_out(g):
                dve.wait_ge(s_vps, g + 1)
                nc.vector.tensor_copy(v[:, :, :], l_ps[0:S, :].rearrange("p (b c) -> p b c", b=G)
                                      ).then_inc(s_v, 1)

            def prologue():
                statistics(0)
                apply(0)
                statistics(1)
                apply(1)
                values_out(0)

            def body(i, router, work, nxt, nxt2):
                if work:
                    dve.wait_ge(s_scores, i + 1)
                    nc.vector.tensor_reduce(mx[:, :], by_batch(s_ps[:, 0:K4], S), AX.X, ALU.max).then_inc(s_max, 1)
                    dve.wait_ge(s_max, i + 1)
                    nc.vector.tensor_tensor(by_batch(dif[:, :], S), by_batch(s_ps[:, 0:K4], S),
                                            spread(mx[:, :], S), ALU.subtract).then_inc(s_dif, 1)
                if router:
                    after(dve, s_rrps, i - 1)
                    after_alone(dve, s_rtps, i)
                    nc.vector.tensor_tensor(
                        by_batch(rl[:, :], T), by_batch(rt_ps[:, :], T),
                        r.anchor_rt[:, bass.ds(G * i - G, G)].rearrange("p (b a) -> p b a", a=1)
                        .broadcast_to([E, G, T]), ALU.add).then_inc(s_rl, 1)
                if work:
                    dve.wait_ge(s_exp, i + 1)
                    nc.vector.tensor_reduce(den[:, :], by_batch(prob[:, :], S), AX.X, ALU.add).then_inc(s_den, 1)
                    dve.wait_ge(s_den, i + 1)
                    nc.vector.reciprocal(rden[:, :], den[:, :]).then_inc(s_rden, 1)
                    dve.wait_ge(s_rden, i + 1)
                    after(dve, s_tps, i)
                    nc.vector.tensor_tensor(by_batch(pn[:, :], S), by_batch(prob[:, :], S),
                                            spread(rden[:, :], S), ALU.mult).then_inc(s_pn, 1)
                if nxt2:
                    statistics(i + 2)
                if router:
                    dve.wait_ge(s_rrps, i)
                    nc.vector.tensor_reduce(rmx[:, :], by_batch(rr_ps[:, 0:G * E], E), AX.X, ALU.max).then_inc(s_rmax, 1)
                    dve.wait_ge(s_rmax, i)
                    nc.vector.tensor_tensor(by_batch(rdif[:, :], E), by_batch(rr_ps[:, 0:G * E], E),
                                            spread(rmx[:, :], E), ALU.subtract).then_inc(s_rdif, 1)
                if nxt2:
                    apply(i + 2)
                if router:
                    dve.wait_ge(s_rexp, i)
                    nc.vector.tensor_reduce(rden2[:, :], by_batch(rexp[:, :], E), AX.X, ALU.add).then_inc(s_rsum, 1)
                    dve.wait_ge(s_rsum, i)
                    nc.vector.reciprocal(rrd[:, :], rden2[:, :]).then_inc(s_rrd, 1)
                    dve.wait_ge(s_rrd, i)
                    nc.vector.tensor_tensor(st.probs[:, bass.ds(G * i - G, G), :], by_batch(rexp[:, :], E),
                                            spread(rrd[:, :], E), ALU.mult).then_inc(s_probs, 1)
                if nxt:
                    values_out(i + 1)

            iterations(dve, body, prologue)
            dve.wait_ge(s_aps, 1)
            for k in range(7):
                bias = r.bcol("e1", k) if k < 6 else r.bcol("g1")
                last = nc.vector.tensor_scalar(st.anchor[:, k, :], a_ps[:, k * B:(k + 1) * B], bias, None, ALU.add)
            last.then_inc(s_anchor, 1)

        @block.scalar
        def _(act):
            def normalised(g):
                after_alone(act, s_xT, g + 1)
                nc.scalar.activation(st.nx[:, bass.ds(G * g, G), :],
                                     l_ps[:, :].rearrange("p (b k) -> p b k", b=G), ACT.Identity,
                                     scale=r.bcol("gamma"), bias=r.bcol("beta")).then_inc(s_nx, 1)

            def keys_out(g):
                act.wait_ge(s_kps, g + 1)
                nc.scalar.copy(kT[:, :], l_ps[:, 0:K4]).then_inc(s_kT, 1)

            def queries_out(g):
                act.wait_ge(s_qps, g + 1)
                nc.scalar.copy(qT[:, :], l_ps[:, :]).then_inc(s_qT, 1)

            def prologue():
                normalised(0)
                keys_out(0)
                queries_out(0)

            def body(i, router, work, nxt, nxt2):
                if work:
                    after(act, s_pn, i)
                    act.wait_ge(s_dif, i + 1)
                    nc.scalar.activation(prob[:, :], dif[:, :], ACT.Exp, scale=scale).then_inc(s_exp, 1)
                if nxt:
                    normalised(i + 1)
                    keys_out(i + 1)
                if work:
                    act.wait_ge(s_tps, i + 1)
                    nc.scalar.copy(pT[:, :], t_ps[:, :]).then_inc(s_pT, 1)
                if nxt:
                    queries_out(i + 1)
                if router:
                    after(act, s_probs, i - 1)
                    act.wait_ge(s_rdif, i)
                    nc.scalar.activation(rexp[:, :], rdif[:, :], ACT.Exp).then_inc(s_rexp, 1)
                if work:
                    after_alone(act, s_eps, i + 1)
                    nc.scalar.copy(st.ev[:, bass.ds(G * i, G), :],
                                   e_ps[:, :].rearrange("p (b k) -> p b k", b=G)).then_inc(s_ev, 1)

            iterations(act, body, prologue)

        @block.tensor
        def _(pe):
            def transpose_xn(g):
                after(pe, s_v, g)
                pe.wait_ge(s_xn, g + 1)
                for b in range(G):
                    last = nc.tensor.transpose(l_ps[:, b * T:(b + 1) * T], xn[:, b, :], r.ident[:, :])
                last.then_inc(s_xT, 1)

            def project_keys(g):
                pe.wait_ge(s_ctx, 16 * g + 16)
                pe.wait_ge(s_nx, g + 1)
                nc.tensor.matmul(l_ps[:, 0:K4], r.W("k3"), ctxs[:, :], start=True, stop=True).then_inc(s_kps, 1)

            def project_queries(g):
                pe.wait_ge(s_kT, g + 1)
                nc.tensor.matmul(l_ps[:, :], r.W("q3"), st.nx[:, bass.ds(G * g, G), :],
                                 start=True, stop=True).then_inc(s_qps, 1)

            def project_values(g):
                pe.wait_ge(s_qT, g + 1)
                for b in range(G):
                    last = nc.tensor.matmul(l_ps[0:S, b * C:(b + 1) * C], ctxs[:, b * S:(b + 1) * S], r.W("v3"),
                                            start=True, stop=True)
                last.then_inc(s_vps, 1)

            def prologue():
                transpose_xn(0)
                project_keys(0)
                project_queries(0)
                project_values(0)

            def body(i, router, work, nxt, nxt2):
                if work:
                    pe.wait_ge(s_qT, i + 1)
                    after(pe, s_dif, i)
                    for b in range(G):
                        last = nc.tensor.matmul(s_ps[:, b * S:(b + 1) * S], qT[:, b * T:(b + 1) * T],
                                                kT[:, b * S:(b + 1) * S], start=True, stop=True)
                    last.then_inc(s_scores, 1)
                if nxt:
                    transpose_xn(i + 1)
                if router:
                    after(pe, s_rl, i - 1)
                    pe.wait_ge(s_ev, i)
                    nc.tensor.matmul(rt_ps[:, :], r.W("rw", 0, E), st.nx[:, bass.ds(G * i - G, G), :],
                                     start=True, stop=False)
                    nc.tensor.matmul(rt_ps[:, :], r.W("rw", E, E), st.ev[:, bass.ds(G * i - G, G), :],
                                     start=False, stop=True).then_inc(s_rtps, 1)
                if nxt:
                    project_keys(i + 1)
                if work:
                    after(pe, s_pT, i)
                    pe.wait_ge(s_pn, i + 1)
                    for b in range(G):
                        last = nc.tensor.transpose(t_ps[:, b * T:(b + 1) * T], pn[:, b * S:(b + 1) * S],
                                                   r.ident[:, :])
                    last.then_inc(s_tps, 1)
                if nxt:
                    project_queries(i + 1)
                if router:
                    pe.wait_ge(s_rl, i)
                    after_alone(pe, s_rdif, i - 1)
                    for b in range(G):
                        last = nc.tensor.transpose(rr_ps[:, b * E:(b + 1) * E], rl[:, b * T:(b + 1) * T],
                                                   r.ident[0:E, 0:E])
                    last.then_inc(s_rrps, 1)
                if work:
                    after(pe, s_ev, i)
                    pe.wait_ge(s_pT, i + 1)
                    pe.wait_ge(s_v, i + 1)
                    for b in range(G):
                        last = nc.tensor.matmul(e_ps[:, b * T:(b + 1) * T], v[:, b, :], pT[:, b * T:(b + 1) * T],
                                                start=True, stop=True)
                    last.then_inc(s_eps, 1)
                if nxt:
                    project_values(i + 1)

            iterations(pe, body, prologue)
            pe.wait_ge(s_w3, 16)
            for k in range(6):
                e, c = divmod(k, 2)
                nc.tensor.matmul(a_ps[:, k * B:(k + 1) * B],
                                 r.W("e1", (e * 3 + 2) * RH + c * C), r.condT[:, :], start=True, stop=True)
            nc.tensor.matmul(a_ps[:, 6 * B:7 * B], r.W("g1", 2 * C), r.condT[:, :], start=True, stop=True
                             ).then_inc(s_aps, 1)


def expert_phase(nc, r, st, io):
    with nc.cleanup_on_exit(), ExitStack() as ctx:
        tag = "expert_"

        def sb(name, shape):
            return ctx.enter_context(nc.sbuf_tensor(tag + name, shape, F32))

        def ps(name, shape):
            return ctx.enter_context(nc.psum_tensor(tag + name, shape, F32))

        def sem(name):
            return nc.alloc_semaphore(tag + name)

        b2 = sb("b2", [T, E * C])
        g2h = sb("g2h", [C, 1])
        g1 = sb("g1", [C, GT])
        hid = sb("hid", [C, 2 * E, GT])
        th, gt = sb("th", [C, GT]), sb("gt", [C, 2, GT])
        eo, acc = sb("eo", [T, 2, E * C]), sb("acc", [T, 2, 2, C])
        routed, roT = sb("routed", [T, G, C]), sb("roT", [C, GT])
        delta = sb("delta", [C, GT])
        y = sb("y", [T, 2, G, C])
        u_ps, e_ps = ps("u", [C, 3, BANK]), ps("e", [T, 2, BANK])
        g_ps, l_ps, r_ps = ps("g", [C, BANK]), ps("l", [C, BANK]), ps("r", [T, BANK])
        s_b2, s_g2h = sem("b2"), sem("g2h")
        s_up, s_hid = sem("up"), sem("hid")
        s_eps, s_eo, s_acc, s_routed = sem("eps"), sem("eo"), sem("acc"), sem("routed")
        s_gps, s_th, s_gt = sem("gps"), sem("th"), sem("gt")
        s_rps, s_roT, s_ops, s_delta, s_dps, s_y = (sem(n) for n in ("rps", "roT", "ops", "delta", "dps", "y"))
        s_store = [sem("store0"), sem("store1")]
        NK = 1 + 2 * E
        block = ctx.enter_context(nc.Block())
        out_v = io["out"].rearrange("b t c -> t b c")

        def iterations(engine, body):
            body(0, 0, False, True)
            for i in range(1, 4):
                body(i, i % 2, True, True)
            with engine.Fori(2, NG // 2) as t:
                body(2 * t, 0, True, True)
                body(2 * t + 1, 1, True, True)
            body(NG, 0, True, False)

        @block.sync
        def _(sp):
            sp.dma_start(b2[:, :], io["e_b2"].rearrange("(a n) -> a n", a=1).broadcast_to([T, E * C])
                         ).then_inc(s_b2, 16)

            def store(g, p):
                after_alone(sp, s_y, g + 1)
                sp.dma_start(out_v[SHIFT:T, bass.ds(G * g, G), :], y[0:T - SHIFT, p]).then_inc(s_store[p], 16)
                sp.dma_start(out_v[0:SHIFT, bass.ds(G * g, G), :], y[T - SHIFT:T, p]).then_inc(s_store[p], 16)

            with sp.Fori(0, NG // 2) as t:
                store(2 * t, 0)
                store(2 * t + 1, 1)
            sp.wait_ge(s_b2, 16)
            sp.wait_ge(s_store[0], 16 * NG)
            sp.wait_ge(s_store[1], 16 * NG)

        @block.gpsimd
        def _(pool):
            nc.gpsimd.tensor_scalar(g2h[:, :], r.bcol("g2"), 0.5, None, ALU.mult).then_inc(s_g2h, 1)

            def gate(g, p):
                after(pool, s_delta, g - 1)
                after_alone(pool, s_th, g + 1)
                nc.gpsimd.tensor_scalar(gt[:, p, :], th[:, :], 0.5, 0.5, ALU.mult, ALU.add).then_inc(s_gt, 1)

            gate(0, 0)
            gate(1, 1)
            with pool.Fori(1, NG // 2) as t:
                gate(2 * t, 0)
                gate(2 * t + 1, 1)

        @block.vector
        def _(dve):
            dve.wait_ge(s_b2, 16)

            def body(i, par, finish, work):
                if finish:
                    dve.wait_ge(s_gt, i)
                    dve.wait_ge(s_ops, i)
                    nc.vector.scalar_tensor_tensor(delta[:, :], l_ps[:, :], r.bcol("ow"), gt[:, 1 - par, :],
                                                   ALU.add, ALU.mult).then_inc(s_delta, 1)
                    after(dve, s_store[1 - par], 16 * (i - 1 - (1 - par)))
                    dve.wait_ge(s_dps, i)
                    nc.vector.tensor_tensor(y[:, 1 - par], r_ps[:, :].rearrange("p (b c) -> p b c", b=G),
                                            r.x[:, bass.ds(G * i - G, G), :], ALU.add).then_inc(s_y, 1)
                if not work:
                    return
                for b in range(G):
                    m = G * i + b
                    dve.wait_ge(s_eps, m + 1)
                    nc.vector.tensor_tensor(eo[:, b % 2, :], e_ps[:, b % 2, 0:E * C], b2[:, :], ALU.add
                                            ).then_inc(s_eo, 1)
                    p = [st.probs[:, bass.ds(m, 1), e] for e in range(E)]
                    dve.wait_ge(s_eo, m + 1)
                    nc.vector.tensor_scalar(acc[:, b % 2, 0, :], eo[:, b % 2, 0:C], p[0], None, ALU.mult
                                            ).then_inc(s_acc, 1)
                    dve.wait_ge(s_acc, 2 * m + 1)
                    nc.vector.scalar_tensor_tensor(acc[:, b % 2, 1, :], eo[:, b % 2, C:2 * C], p[1],
                                                   acc[:, b % 2, 0, :], ALU.mult, ALU.add).then_inc(s_acc, 1)
                    if b == 0:
                        after(dve, s_rps, i)
                    dve.wait_ge(s_acc, 2 * m + 2)
                    nc.vector.scalar_tensor_tensor(routed[:, b, :], eo[:, b % 2, 2 * C:3 * C], p[2],
                                                   acc[:, b % 2, 1, :], ALU.mult, ALU.add).then_inc(s_routed, 1)

            iterations(dve, body)

        @block.scalar
        def _(act):
            act.wait_ge(s_g2h, 1)

            def body(i, par, finish, work):
                def hidden(k):
                    after_alone(act, s_up, NK * i + k + 1)
                    out = g1 if k == 0 else hid[:, k - 1]
                    for b in range(G):
                        last = nc.scalar.activation(
                            out[:, b * T:(b + 1) * T], u_ps[:, (k + par * NK) % 3, b * T:(b + 1) * T], ACT.Silu,
                            bias=st.anchor[:, 6 if k == 0 else k - 1, bass.ds(G * i + b, 1)])
                    last.then_inc(s_hid, 1)

                if work:
                    hidden(0)
                    hidden(1)
                if finish:
                    act.wait_ge(s_rps, i)
                    nc.scalar.copy(roT[:, :], l_ps[:, :]).then_inc(s_roT, 1)
                if work:
                    for k in range(2, NK):
                        hidden(k)
                    after(act, s_gt, i)
                    act.wait_ge(s_gps, i + 1)
                    nc.scalar.activation(th[:, :], g_ps[:, :], ACT.Tanh, scale=0.5, bias=g2h[:, 0:1]
                                         ).then_inc(s_th, 1)

            iterations(act, body)

        @block.tensor
        def _(pe):
            def body(i, par, finish, work):
                def up(k):
                    n = NK * i + k
                    after(pe, s_hid, n - 1 if par == 0 and k < 2 else n - 2)
                    w = ("g1", 0, C) if k == 0 else ("e1", ((k - 1) // 2) * 3 * RH + (k - 1) % 2 * C, RH)
                    bank = u_ps[:, (k + par * NK) % 3, :]
                    nc.tensor.matmul(bank, r.W(w[0], w[1]), st.nx[:, bass.ds(G * i, G), :],
                                     start=True, stop=False)
                    nc.tensor.matmul(bank, r.W(w[0], w[1] + w[2]), st.ev[:, bass.ds(G * i, G), :],
                                     start=False, stop=True).then_inc(s_up, 1)

                if work:
                    up(0)
                    up(1)
                if finish:
                    pe.wait_ge(s_routed, G * i)
                    after(pe, s_delta, i - 1)
                    for b in range(G):
                        last = nc.tensor.transpose(l_ps[:, b * T:(b + 1) * T], routed[:, b, :], r.ident[:, :])
                    last.then_inc(s_rps, 1)
                if work:
                    up(2)
                if finish:
                    pe.wait_ge(s_roT, i)
                    nc.tensor.matmul(l_ps[:, :], r.W("ow"), roT[:, :], start=True, stop=True).then_inc(s_ops, 1)
                if work:
                    up(3)
                    up(4)
                if work:
                    up(5)
                    up(6)
                if finish:
                    after(pe, s_y, i - 1)
                    pe.wait_ge(s_delta, i)
                    for b in range(G):
                        last = nc.tensor.transpose(r_ps[:, b * C:(b + 1) * C], delta[:, b * T:(b + 1) * T],
                                                   r.ident[:, :])
                    last.then_inc(s_dps, 1)
                if work:
                    after(pe, s_th, i)
                    pe.wait_ge(s_hid, NK * i + 1)
                    nc.tensor.matmul(g_ps[:, :], r.W("g2"), g1[:, :], start=True, stop=True).then_inc(s_gps, 1)
                    for b in range(G):
                        m = G * i + b
                        after(pe, s_eo, m - 1)
                        if b == 0:
                            pe.wait_ge(s_hid, NK * i + NK)
                        for e in range(E):
                            for c in range(2):
                                last = nc.tensor.matmul(e_ps[:, b % 2, e * C:(e + 1) * C],
                                                        hid[:, 2 * e + c, b * T:(b + 1) * T],
                                                        r.W("e2", (2 * e + c) * C), start=(c == 0), stop=(c == 1))
                        last.then_inc(s_eps, 1)

            iterations(pe, body)


def build(nc, io):
    with ExitStack() as ctx:
        r = resident(nc, ctx)
        with ExitStack() as first:
            r.ctxnT = first.enter_context(nc.sbuf_tensor("ctxnT", [C, B, S], F32))
            with nc.sbuf_tensor("kbd", [C, H, GT], F32) as r.kbd:
                setup_phase(nc, r, io)
                attention_phase(nc, r, 0, "window")
                attention_phase(nc, r, 0, "topk")
            r.kbd = first.enter_context(nc.sbuf_tensor("split_keys", [C, 2, 4, 2, GT], F32R))
            r.qz = first.enter_context(nc.sbuf_tensor("split_queries", [C, 4, 2, GT], F32R))
            mlp_phase(nc, r, 0)
            for layer in (1, 2):
                attention_phase(nc, r, layer, "self")
                attention_phase(nc, r, layer, "cross")
                mlp_phase(nc, r, layer)
        st = Resident()
        st.nx = ctx.enter_context(nc.sbuf_tensor("nx", [C, B, T], F32))
        st.ev = ctx.enter_context(nc.sbuf_tensor("ev", [C, B, T], F32))
        st.anchor = ctx.enter_context(nc.sbuf_tensor("anchor", [C, 7, B], F32))
        r.w3 = ctx.enter_context(nc.sbuf_tensor("weights3", [C, sum(W3_WIDTH.values())], F32))
        st.weights3 = io["weights3"]
        st.probs = ctx.enter_context(nc.sbuf_tensor("probs", [T, B, E], F32))
        evidence_phase(nc, r, st)
        expert_phase(nc, r, st, io)


def packed(inputs):
    import numpy as np

    def a(name):
        return np.asarray(inputs[name])

    def rows(w):
        n = w.shape[0] // C
        return w.reshape(n, C, w.shape[1]).transpose(1, 0, 2).reshape(C, n * w.shape[1])

    def columns(*vectors):
        return np.concatenate([v.reshape(-1, C) for v in vectors]).T

    L0, L1, L2, L3 = "L0_xcond_", "L1_xcond_", "L2_xcond_", "L3_xcond_"
    e_w1, e_w2 = a(L3 + "e_w1"), a(L3 + "e_w2")
    matrices = {
        "qkv0": a(L0 + "w_qkv"), "so0": a(L0 + "w_so"), "q0": a(L0 + "w_q"), "kv0": a(L0 + "w_kv"),
        "co0": a(L0 + "w_co"), "m1_0": a(L0 + "w_m1"), "m2_0": rows(a(L0 + "w_m2")),
        "qkv1": a(L1 + "W_qkv"), "so1": a(L1 + "W_proj"), "q1": a(L1 + "W_qc"), "kv1": a(L1 + "W_kvc"),
        "co1": a(L1 + "W_cproj"), "m1_1": a(L1 + "W_mlp1"), "m2_1": rows(a(L1 + "W_mlp2")),
        "qkv2": a(L2 + "qkv_w"), "so2": a(L2 + "sa_proj_w"), "q2": a(L2 + "q_w"), "kv2": a(L2 + "kv_w"),
        "co2": a(L2 + "ca_proj_w"), "m1_2": a(L2 + "fc1_w"), "m2_2": rows(a(L2 + "fc2_w")),
        "q3": a(L3 + "Wq"), "k3": a(L3 + "Wk"), "v3": a(L3 + "Wv"), "rw": rows(a(L3 + "router_W")),
        "e1": np.concatenate([rows(w) for w in e_w1], axis=1),
        "e2": np.concatenate([rows(w) for w in e_w2], axis=1),
        "g1": rows(a(L3 + "gate_w1")), "g2": a(L3 + "gate_w2"), "ow": a(L3 + "out_w"),
    }
    vectors = {
        "mod": columns(a(L0 + "b_ada"), a(L1 + "b_mod"), a(L2 + "adaln_b")),
        "qkv0": columns(a(L0 + "b_qkv")), "so0": columns(a(L0 + "b_so")), "q0": columns(a(L0 + "b_q")),
        "kv0": columns(a(L0 + "b_kv")), "co0": columns(a(L0 + "b_co")), "m1_0": columns(a(L0 + "b_m1")),
        "m2_0": columns(a(L0 + "b_m2")),
        "qkv1": columns(a(L1 + "b_qkv")), "so1": columns(a(L1 + "b_proj")), "q1": columns(a(L1 + "b_qc")),
        "kv1": columns(a(L1 + "b_kvc")), "co1": columns(a(L1 + "b_cproj")), "m1_1": columns(a(L1 + "b_mlp1")),
        "m2_1": columns(a(L1 + "b_mlp2")),
        "qkv2": columns(a(L2 + "qkv_b")), "so2": columns(a(L2 + "sa_proj_b")), "q2": columns(a(L2 + "q_b")),
        "kv2": columns(a(L2 + "kv_b")), "co2": columns(a(L2 + "ca_proj_b")), "m1_2": columns(a(L2 + "fc1_b")),
        "m2_2": columns(a(L2 + "fc2_b")),
        "gamma": columns(a(L3 + "ln_gamma")), "beta": columns(a(L3 + "ln_beta")),
        "e1": columns(a(L3 + "e_b1").reshape(-1)), "g1": columns(a(L3 + "gate_b1")),
        "g2": columns(a(L3 + "gate_b2")), "ow": columns(a(L3 + "out_b")),
    }
    assert all(matrices[n].shape == (C, w) for n, w in [*W_WIDTH.items(), *W3_WIDTH.items()])
    assert all(vectors[n].shape == (C, w) for n, w in B_WIDTH.items())
    return {
        "x": a("x"), "cond": a("cond_1024"), "ctx": a("ctx_1024"),
        "weights": np.concatenate([matrices[n] for n in W_WIDTH], axis=1),
        "weights3": np.concatenate([matrices[n] for n in W3_WIDTH], axis=1),
        "wmod": np.concatenate([a(L0 + "w_ada"), a(L1 + "W_mod"), a(L2 + "adaln_w")], axis=1),
        "bias": np.concatenate([vectors[n] for n in B_WIDTH], axis=1),
        "router_b": a(L3 + "router_b"), "e_b2": a(L3 + "e_b2").reshape(-1),
    }


def kernel(**inputs):
    import numpy as np
    import concourse.bacc as bacc
    from concourse.bass_utils import run_bass_kernel_spmd

    nc = bacc.Bacc("TRN2", target_bir_lowering=False, num_devices=1)
    arrays = {f"in_{k}": np.ascontiguousarray(v) for k, v in packed(inputs).items()}
    io = {k[3:]: nc.dram_tensor(k, v.shape, mybir.dt.from_np(v.dtype), kind="ExternalInput").ap()
          for k, v in arrays.items()}
    io["out"] = nc.dram_tensor("out_x", (B, T, C), F32, kind="ExternalOutput").ap()
    build(nc, io)
    return run_bass_kernel_spmd(nc, [arrays], core_ids=[0]).results[0]["out_x"]
```
